# Optimizing a Trainium2 kernel written in Bass

```python
import numpy as np
import jax
import jax.numpy as jnp

def _softmax(x, axis=-1):
    return jax.nn.softmax(x, axis=axis)

def _gelu(x):
    return jax.nn.gelu(x, approximate=True)

def _silu(x):
    return jax.nn.silu(x)

def _sigmoid(x):
    return jax.nn.sigmoid(x)

def _layernorm(x, axis=-1, eps=1e-05):
    m = jnp.mean(x, axis=axis, keepdims=True)
    v = jnp.var(x, axis=axis, keepdims=True)
    return (x - m) / jnp.sqrt(v + eps)

def _scatter_add(tgt, idx, src, axis=0):
    return tgt.at[idx].add(src)

def _segment_sum(src, seg, n):
    return jax.ops.segment_sum(src, seg, n)
kernel_name = 'mk_adaln_d1_jaxref_r8_7ddd5d'

def setup_inputs(seed: int=0):
    np.random.seed(seed)
    _w = jnp.asarray

    def _L0_attn_setup():
        import jax, jax.numpy as jnp
        import numpy as np
        B, S, H_DIM = (2, 256, 256)
        N_HEADS, D_HEAD = (16, 128)
        key = jax.random.key(seed)
        k1, k2, k3 = jax.random.split(key, 3)
        x = jax.random.normal(k1, (B, S, H_DIM), dtype=jnp.float32)
        w_qkv = jax.random.normal(k2, (H_DIM, 3 * N_HEADS * D_HEAD), dtype=jnp.float32) * 0.02
        w_o = jax.random.normal(k3, (N_HEADS * D_HEAD, H_DIM), dtype=jnp.float32) * 0.02
        return {'x': x, 'w_qkv': w_qkv, 'w_o': w_o}
    _L0_attn_in = _L0_attn_setup()

    def _L0_ffn_setup():
        import jax, jax.numpy as jnp
        import numpy as np
        B, S, H, F, E, R, K = (2, 128, 256, 896, 8, 32, 2)

        def _gather_slot(a_all, e):
            return jnp.take_along_axis(a_all, e[:, None, None], axis=1)[:, 0]
        key = jax.random.key(seed)
        ks = jax.random.split(key, 12)
        sc = 0.02
        n = lambda k, shape, s: jax.random.normal(k, shape, dtype=jnp.float32) * s
        return {'hidden_states': n(ks[0], (B, S, H), 1.0), 'Wg': n(ks[1], (E, H), sc), 'W1': n(ks[2], (F, H), sc), 'W2': n(ks[3], (H, F), sc), 'W3': n(ks[4], (F, H), sc), 'A1': n(ks[5], (E, R, H), sc), 'B1': n(ks[6], (E, F, R), sc), 'A2': n(ks[7], (E, R, F), sc), 'B2': n(ks[8], (E, H, R), sc), 'A3': n(ks[9], (E, R, H), sc), 'B3': n(ks[10], (E, F, R), sc)}
    _L0_ffn_in = _L0_ffn_setup()
    _L0_c = _w((lambda *s: np.random.randn(*s).astype(np.float32) * 0.05)(16, 256))
    _L0_wmod = _w((lambda *s: np.random.randn(*s).astype(np.float32) * 0.05)(256, 6 * 256) * 256 ** (-0.5))
    _d = {'L0_attn_x': _L0_attn_in['x'], 'L0_attn_w_qkv': _L0_attn_in['w_qkv'], 'L0_attn_w_o': _L0_attn_in['w_o'], 'L0_ffn_Wg': _L0_ffn_in['Wg'], 'L0_ffn_W1': _L0_ffn_in['W1'], 'L0_ffn_W2': _L0_ffn_in['W2'], 'L0_ffn_W3': _L0_ffn_in['W3'], 'L0_ffn_A1': _L0_ffn_in['A1'], 'L0_ffn_B1': _L0_ffn_in['B1'], 'L0_ffn_A2': _L0_ffn_in['A2'], 'L0_ffn_B2': _L0_ffn_in['B2'], 'L0_ffn_A3': _L0_ffn_in['A3'], 'L0_ffn_B3': _L0_ffn_in['B3'], 'L0_c': _L0_c, 'L0_wmod': _L0_wmod}
    _x0 = _d['L0_attn_x']
    _d['L0_attn_x'] = jax.random.normal(jax.random.fold_in(jax.random.key(seed), 1), (16, 256, 256), dtype=_x0.dtype)
    del _x0
    return _d

def reference(L0_attn_x, L0_attn_w_qkv, L0_attn_w_o, L0_ffn_Wg, L0_ffn_W1, L0_ffn_W2, L0_ffn_W3, L0_ffn_A1, L0_ffn_B1, L0_ffn_A2, L0_ffn_B2, L0_ffn_A3, L0_ffn_B3, L0_c, L0_wmod):

    def _L0_attn_ref(x, w_qkv, w_o):
        import jax, jax.numpy as jnp
        import numpy as np
        B, S, H_DIM = (2, 256, 256)
        N_HEADS, D_HEAD = (16, 128)
        b, s, _ = x.shape
        qkv = jnp.einsum('bsh,hf->bsf', x, w_qkv)
        qkv = qkv.reshape(b, s, 3, N_HEADS, D_HEAD)
        q, k, v = (qkv[:, :, 0], qkv[:, :, 1], qkv[:, :, 2])
        q = q.transpose(0, 2, 1, 3)
        k = k.transpose(0, 2, 1, 3)
        v = v.transpose(0, 2, 1, 3)
        scores = jnp.einsum('bhqd,bhkd->bhqk', q, k) / jnp.sqrt(jnp.float32(D_HEAD))
        probs = jax.nn.softmax(scores, axis=-1)
        values = jnp.einsum('bhqk,bhkd->bhkd', probs, v)
        values = values.transpose(0, 2, 1, 3).reshape(b, s, N_HEADS * D_HEAD)
        out = jnp.einsum('bsf,fh->bsh', values, w_o)
        return out

    def _L0_ffn_ref(hidden_states, Wg, W1, W2, W3, A1, B1, A2, B2, A3, B3):
        import jax, jax.numpy as jnp
        import numpy as np
        B, S, H, F, E, R, K = (2, 128, 256, 896, 8, 32, 2)

        def _gather_slot(a_all, e):
            return jnp.take_along_axis(a_all, e[:, None, None], axis=1)[:, 0]
        b, s, h = hidden_states.shape
        x = hidden_states.reshape(-1, h)
        nE = Wg.shape[0]
        logits = x @ Wg.T
        probs = jax.nn.softmax(logits.astype(jnp.float32), axis=-1)
        rw, sel = jax.lax.top_k(probs, K)
        rw = (rw / rw.sum(axis=-1, keepdims=True)).astype(x.dtype)
        base1 = x @ W1.T
        base3 = x @ W3.T
        a1_all = jnp.einsum('th,erh->ter', x, A1)
        a3_all = jnp.einsum('th,erh->ter', x, A3)
        out = jnp.zeros_like(x)
        for k in range(K):
            e = sel[:, k]
            mask = jax.nn.one_hot(e, nE, dtype=x.dtype)
            a1 = _gather_slot(a1_all, e)
            a3 = _gather_slot(a3_all, e)
            lora1 = jnp.einsum('ter,efr->tf', mask[:, :, None] * a1[:, None, :], B1)
            lora3 = jnp.einsum('ter,efr->tf', mask[:, :, None] * a3[:, None, :], B3)
            x1 = base1 + lora1
            x3 = base3 + lora3
            x2 = jax.nn.silu(x1) * x3
            down = x2 @ W2.T
            a2_all = jnp.einsum('tf,erf->ter', x2, A2)
            a2 = _gather_slot(a2_all, e)
            lora2 = jnp.einsum('ter,ehr->th', mask[:, :, None] * a2[:, None, :], B2)
            out = out + (down + lora2) * rw[:, k:k + 1]
        return out.reshape(b, s, h)
    x = L0_attn_x
    mod = (_silu(L0_c) @ L0_wmod).reshape(L0_c.shape[0], 6, 1, -1)
    sa, ca, ga, sb, cb, gb = (mod[:, 0], mod[:, 1], mod[:, 2], mod[:, 3], mod[:, 4], mod[:, 5])
    ga = (2 * (ga >= 0) - 1) * jnp.maximum(jnp.abs(ga), 0.25)
    gb = (2 * (gb >= 0) - 1) * jnp.maximum(jnp.abs(gb), 0.25)
    h = _layernorm(x, axis=-1) * (1 + ca) + sa
    x = x + ga * _L0_attn_ref(h, L0_attn_w_qkv, L0_attn_w_o)
    h = _layernorm(x, axis=-1) * (1 + cb) + sb
    x = x + gb * _L0_ffn_ref(h, L0_ffn_Wg, L0_ffn_W1, L0_ffn_W2, L0_ffn_W3, L0_ffn_A1, L0_ffn_B1, L0_ffn_A2, L0_ffn_B2, L0_ffn_A3, L0_ffn_B3)
    return x

_drawn_inputs = setup_inputs


def setup_inputs(seed=0):
    import zlib

    import numpy as np

    out = dict(_drawn_inputs(seed))
    spreads = {}
    factors = {'L0_ffn_Wg': 8.0,
     'L0_ffn_W1': 7.2,
     'L0_ffn_W2': 7.136,
     'L0_ffn_W3': 7.114,
     'L0_ffn_A1': 8.0,
     'L0_ffn_B1': 8.0,
     'L0_ffn_A2': 8.0,
     'L0_ffn_B2': 8.0,
     'L0_ffn_A3': 8.0,
     'L0_ffn_B3': 8.0}
    for name, (base, spread) in spreads.items():
        noise = np.random.default_rng([zlib.crc32(name.encode()), seed]).standard_normal(out[name].shape)
        drawn = base * np.exp(spread * noise) if base else spread * noise
        out[name] = jnp.asarray(drawn.astype(out[name].dtype))
    for name, factor in factors.items():
        out[name] = (out[name] * factor).astype(out[name].dtype)
    return out
```

```python
import concourse.bass as bass
from concourse import mybir
from contextlib import ExitStack
import math

F32 = mybir.dt.float32
F32R = mybir.dt.float32r
BF16 = mybir.dt.bfloat16
ALU = mybir.AluOpType
ACT = mybir.ActivationFunctionType
AX = mybir.AxisListType

P = 128
B, S, D = 16, 256, 256
HEADS, DH = 16, 128
KT = D // P
PAIRS = B // 2
PT = 2 * S
TOK = B * S
FF, EXPERTS, RANK = 896, 8, 32
FT = FF // P
ER = EXPERTS * RANK
ET = ER // P
EPS = 1e-5
SCALE = 1.0 / math.sqrt(DH)
SA, CA, GA, SB_, CB, GB = range(6)


def at_least(eng, sem, value):
    if isinstance(value, int) and value <= 0:
        return
    eng.wait_ge(sem, value)


def three_pass(nc, out, w_hi, w_lo, x_hi, x_lo, first, last, **kw):
    nc.tensor.matmul(out, w_hi, x_hi, start=first, stop=False, **kw)
    nc.tensor.matmul(out, w_hi, x_lo, start=False, stop=False, **kw)
    return nc.tensor.matmul(out, w_lo, x_hi, start=False, stop=last, **kw)


class Memory:

    def __init__(self, nc, ctx):
        self.nc, self.ctx = nc, ctx

    def sb(self, name, shape, dt=F32):
        return self.ctx.enter_context(self.nc.sbuf_tensor(name, shape, dt))

    def ps(self, name, shape=(P, 512)):
        return self.ctx.enter_context(self.nc.psum_tensor(name, list(shape), F32))

    def sem(self, name):
        return self.ctx.enter_context(self.nc.semaphore(name))


def combine_stats(nc, dve, stats, meanvar, vareps, moments, ve_ready, done):
    even_mean, odd_mean = stats[:, :, 1], stats[:, :, 4]
    nc.vector.tensor_tensor(meanvar[:, :, 0], even_mean, odd_mean, ALU.add).then_inc(moments, 1)
    nc.vector.tensor_tensor(meanvar[:, :, 1], even_mean, odd_mean, ALU.subtract).then_inc(moments, 1)
    nc.vector.tensor_tensor(vareps, stats[:, :, 2], stats[:, :, 5], ALU.add).then_inc(moments, 1)
    dve.wait_ge(moments, 3 * done + 3)
    nc.vector.tensor_scalar(meanvar[:, :, 0], meanvar[:, :, 0], 0.5, None, ALU.mult).then_inc(ve_ready, 1)
    nc.vector.tensor_scalar(vareps, vareps, 1.0 / D, EPS, ALU.mult, ALU.add).then_inc(ve_ready, 1)
    nc.vector.scalar_tensor_tensor(meanvar[:, :, 1], meanvar[:, :, 1], 0.25, meanvar[:, :, 1], ALU.mult, ALU.mult).then_inc(ve_ready, 1)
    dve.wait_ge(ve_ready, 4 * done + 3)
    nc.vector.tensor_tensor(vareps, vareps, meanvar[:, :, 1], ALU.add).then_inc(ve_ready, 1)


def setup_phase(nc, mem, dram, g):
    with ExitStack() as ctx:
        m = Memory(nc, ctx)
        c_sb = m.sb("c_sb", [B, D])
        sc = m.sb("silu_c", [B, D])
        scT = m.sb("silu_cT", [P, KT, B])
        wmod = g.accT[:, 0, 0:KT * 6 * D].rearrange("p (k n) -> p k n", k=KT)
        mod_row = g.accT[0:B, 1, 0:6 * D]
        gate_sign = m.sb("gate_sign", [P, 2, KT, B])
        gate_abs = m.sb("gate_abs", [P, 2, KT, B])
        x_in = m.sb("x_in", [P, 2, 4, D])
        stats = m.sb("ln_stats", [P, 2, 4, 6])
        meanvar = m.sb("ln_meanvar", [P, 2, 4, 2])
        vareps = m.sb("ln_vareps", [P, 2, 4])
        rstd = m.sb("ln_rstd", [P, 2, 4])
        xn = m.sb("xn", [P, 2, 4, D])
        h32 = m.sb("h32", [P, 2, KT, PT])
        ps_small = m.ps("ps_small")
        ps_t = [[m.ps(f"ps_t{r}{k}") for k in range(KT)] for r in range(2)]
        ps_mod = [ps_t[0][0], ps_t[0][1], ps_t[1][0]]

        c_loaded, wmod_loaded = m.sem("c_loaded"), m.sem("wmod_loaded")
        x_loaded = [m.sem("x_loaded0"), m.sem("x_loaded1")]
        silu_done, cT_ready, cT_copied = m.sem("silu_done"), m.sem("cT_ready"), m.sem("cT_copied")
        mod_ready, mod_copied, modT_ready = m.sem("mod_ready"), m.sem("mod_copied"), m.sem("modT_ready")
        modT_copied, gate_step, mod_final = m.sem("modT_copied"), m.sem("gate_step"), m.sem("mod_final")
        stats_ready, moments, ve_ready = m.sem("stats_ready"), m.sem("moments"), m.sem("ve_ready")
        rstd_ready, xn_ready, xnT_ready = m.sem("rstd_ready"), m.sem("xn_ready"), m.sem("xnT_ready")
        h_ready, h_hi_ready, h_lo_ready = m.sem("h_ready"), m.sem("h_hi_ready"), m.sem("h_lo_ready")
        const_step = m.sem("const_step")

        block = ctx.enter_context(nc.Block())

        @block.sync
        def _(sp):
            sp.dma_start(c_sb[:], dram["c"]).then_inc(c_loaded, 16)
            xg = dram["x"].rearrange("b (t p) c -> b p t c", p=P)
            for r in range(2):
                for j in range(2):
                    sp.dma_start(x_in[:, r, 2 * j:2 * j + 2, :], xg[2 * r + j]).then_inc(x_loaded[r], 16)
            sp.dma_start(wmod, dram["wmod"].rearrange("(k p) n -> p k n", p=P)).then_inc(wmod_loaded, 16)
            load_head(nc, sp, dram, g, 0, 0)
            load_head(nc, sp, dram, g, 1, 1)
            with sp.Fori(0, PAIRS // 2 - 1) as i:
                for r in range(2):
                    sp.wait_ge(xn_ready, 8 * i + 4 * r + 4)
                    for j in range(2):
                        sp.dma_start(x_in[:, r, 2 * j:2 * j + 2, :], xg[4 * i + (4 + 2 * r + j)]).then_inc(x_loaded[r], 16)
            load_ffn_weights(nc, sp, dram, g)

        @block.gpsimd
        def _(pool):
            nc.gpsimd.memset(g.ident[:], 0.0).then_inc(const_step, 1)
            pool.wait_ge(const_step, 1)
            nc.gpsimd.affine_select(out=g.ident[:], in_=g.ident[:], compare_op=ALU.not_equal, fill=1.0,
                                    base=0, pattern=[[-1, P]], channel_multiplier=1).then_inc(g.ident_ready, 1)
            nc.gpsimd.memset(g.ones[:], 1.0).then_inc(g.ones_ready, 1)
            nc.gpsimd.memset(g.minus_half[:], -0.5).then_inc(g.half_const_ready, 1)
            for e in range(EXPERTS):
                nc.gpsimd.memset(g.first_rank[:, :, e:e + 1], float(EXPERTS - e)).then_inc(g.rank_ready, 1)
            split_head_weights_lo(nc, pool, g, 0, 0)
            pool.wait_ge(g.half_const_ready, 1)
            with pool.Fori(0, PAIRS // 2) as i:
                for r in range(2):
                    n = 2 * i + r
                    pool.wait_ge(ve_ready, 4 * n + 4)
                    nc.gpsimd.tensor_tensor(rstd[:, r, :], vareps[:, r, :], g.minus_half[:, 0:4], ALU.pow).then_inc(rstd_ready, 1)

        @block.tensor
        def _(pe):
            pe.wait_ge(g.ident_ready, 1)
            pe.wait_ge(silu_done, 1)
            for k in range(KT):
                last = nc.tensor.transpose(ps_small[:, k * B:(k + 1) * B], sc[:, k * P:(k + 1) * P], g.ident[0:B, 0:B])
            last.then_inc(cT_ready, 1)
            pe.wait_ge(cT_copied, 1)
            pe.wait_ge(wmod_loaded, 16)
            for n in range(3):
                for k in range(KT):
                    last = nc.tensor.matmul(ps_mod[n][0:B, :], scT[:, k, :], wmod[:, k, n * 512:(n + 1) * 512],
                                            start=(k == 0), stop=(k == KT - 1))
            last.then_inc(mod_ready, 1)
            pe.wait_ge(mod_copied, 3)
            for n in range(6 * KT):
                last = nc.tensor.transpose(ps_small[:, n * B:(n + 1) * B], mod_row[:, n * P:(n + 1) * P], g.ident[0:B, 0:B])
            last.then_inc(modT_ready, 1)
            transpose_head_values(nc, pe, g, 0, 0)
            combine_head_values(nc, pe, g, 0, 0)
            with pe.Fori(0, PAIRS // 2) as i:
                for r in range(2):
                    n = 2 * i + r
                    pe.wait_ge(xn_ready, 4 * n + 4)
                    pe.wait_ge(h_ready, 8 * i)
                    for k in range(KT):
                        for t in range(4):
                            last = nc.tensor.transpose(ps_t[r][k][:, t * P:(t + 1) * P], xn[:, r, t, k * P:(k + 1) * P], g.ident[:])
                        last.then_inc(xnT_ready, 1)

        @block.scalar
        def _(act):
            act.wait_ge(c_loaded, 16)
            nc.scalar.activation(sc[:], c_sb[:], ACT.Silu).then_inc(silu_done, 1)
            act.wait_ge(cT_ready, 1)
            nc.scalar.copy(scT[:].rearrange("p k b -> p (k b)"), ps_small[:, 0:KT * B]).then_inc(cT_copied, 1)
            act.wait_ge(mod_ready, 1)
            for n in range(3):
                nc.scalar.copy(mod_row[:, n * 512:(n + 1) * 512], ps_mod[n][0:B, :]).then_inc(mod_copied, 1)
            act.wait_ge(modT_ready, 1)
            nc.scalar.copy(g.modT[:].rearrange("p s k b -> p (s k b)"), ps_small[:, 0:6 * KT * B]).then_inc(modT_copied, 1)
            copy_head_values(nc, act, g, 0, 0)
            split_head_weights_hi(nc, act, g, 0, 0)
            split_head_values_hi(nc, act, g, 0, 0)
            act.wait_ge(mod_final, 1)
            with act.Fori(0, PAIRS // 2) as i:
                for r in range(2):
                    n = 2 * i + r
                    act.wait_ge(h_lo_ready, 2 * i)
                    for k in range(KT):
                        act.wait_ge(xnT_ready, 2 * n + k + 1)
                        for j in range(2):
                            b = 4 * i + (2 * r + j)
                            nc.scalar.activation(h32[:, r, k, j * S:(j + 1) * S], ps_t[r][k][:, j * S:(j + 1) * S],
                                                 ACT.Identity, scale=g.modT[:, CA, k, bass.ds(b, 1)],
                                                 bias=g.modT[:, SA, k, bass.ds(b, 1)]).then_inc(h_ready, 1)
                    act.wait_ge(h_ready, 4 * n + 4)
                    nc.scalar.copy(g.h_hi[:, :, bass.ds(n * PT, PT)], h32[:, r, :, :]).then_inc(h_hi_ready, 1)

        @block.vector
        def _(dve):
            dve.wait_ge(modT_copied, 1)
            for row in (CA, CB):
                nc.vector.tensor_scalar(g.modT[:, row], g.modT[:, row], 1.0, None, ALU.add).then_inc(gate_step, 1)
            for n, row in enumerate((GA, GB)):
                nc.vector.tensor_scalar(gate_sign[:, n], g.modT[:, row], 0.0, 2.0, ALU.is_ge, ALU.mult).then_inc(gate_step, 1)
                nc.vector.scalar_tensor_tensor(gate_abs[:, n], g.modT[:, row], -1.0, g.modT[:, row], ALU.mult, ALU.max).then_inc(gate_step, 1)
            dve.wait_ge(gate_step, 6)
            nc.vector.tensor_scalar(gate_abs[:], gate_abs[:], 0.25, None, ALU.max).then_inc(gate_step, 1)
            dve.wait_ge(gate_step, 7)
            for n, row in enumerate((GA, GB)):
                nc.vector.scalar_tensor_tensor(g.modT[:, row], gate_sign[:, n], -1.0, gate_abs[:, n], ALU.add, ALU.mult).then_inc(gate_step, 1)
            dve.wait_ge(gate_step, 9)
            nc.vector.memset(vareps[:], 1.0).then_inc(mod_final, 1)
            split_head_values_lo(nc, dve, g, 0, 0)
            nc.vector.memset(g.accT[:], 0.0).then_inc(g.acc_zeroed, 1)
            dve.wait_ge(g.ones_ready, 1)
            nc.vector.tensor_copy(g.ones_r[:], g.ones[:]).then_inc(g.ones_r_ready, 1)

            def normalise(i, r):
                n = 2 * i + r
                dve.wait_ge(x_loaded[r], 32 * i + 32)
                for t in range(4):
                    nc.vector.bn_stats(stats[:, r, t, :], x_in[:, r, t, :]).then_inc(stats_ready, 1)
                dve.wait_ge(stats_ready, 4 * n + 4)
                combine_stats(nc, dve, stats[:, r], meanvar[:, r], vareps[:, r, :], moments, ve_ready, n)
                dve.wait_ge(rstd_ready, n + 1)
                dve.wait_ge(xnT_ready, 4 * i)
                for t in range(4):
                    nc.vector.tensor_scalar(xn[:, r, t, :], x_in[:, r, t, :], meanvar[:, r, t, 0:1], rstd[:, r, t:t + 1],
                                            ALU.subtract, ALU.mult).then_inc(xn_ready, 1)

            def split_lo(i, r):
                n = 2 * i + r
                dve.wait_ge(h_hi_ready, n + 1)
                out = g.h_lo[:, :, bass.ds(n * PT, PT)]
                nc.vector.tensor_tensor(out, h32[:, r], g.h_hi[:, :, bass.ds(n * PT, PT)].bitcast(F32), ALU.subtract).then_inc(h_lo_ready, 1)

            with dve.Fori(0, PAIRS // 2) as i:
                for r in range(2):
                    normalise(i, r)
                    split_lo(i, r)
            dve.wait_ge(h_lo_ready, PAIRS)



RAW_LOADS = 16 * (KT + 1)


def load_head(nc, sp, dram, g, h, r):
    columns = dram["w_qkv"].rearrange("(k p) (t h d) -> h k p t d", p=P, t=3, h=HEADS)
    for k in range(KT):
        sp.dma_start(g.raw_qkv[:, r, k], columns[h, k]).then_inc(g.raw_loaded[r], 16)
    sp.dma_start(g.raw_o[:, r], dram["w_o"].rearrange("(h d) n -> h d n", d=DH)[h]).then_inc(g.raw_loaded[r], 16)


def raw_there(eng, g, pair_of_head, r):
    eng.wait_ge(g.raw_loaded[r], RAW_LOADS * (pair_of_head + 1))


def transpose_head_values(nc, pe, g, hp, r):
    h = 2 * hp + r
    raw_there(pe, g, hp, r)
    at_least(pe, g.m_lo_ready, h)
    for k in range(KT):
        last = nc.tensor.transpose(g.ps_head[:, k * P:(k + 1) * P], g.raw_qkv[:, r, k, 2, :], g.ident[:])
    last.then_inc(g.wvT_ready, 1)


def combine_head_values(nc, pe, g, hp, r):
    h = 2 * hp + r
    pe.wait_ge(g.wvT_copied, h + 1)
    for k in range(KT):
        last = nc.tensor.matmul(g.ps_head[:, k * D:(k + 1) * D], g.wvT[:, k * P:(k + 1) * P], g.raw_o[:, r, :], start=True, stop=True)
    last.then_inc(g.m_ready, 1)


def copy_head_values(nc, act, g, hp, r):
    act.wait_ge(g.wvT_ready, 2 * hp + r + 1)
    nc.scalar.copy(g.wvT[:], g.ps_head[:, 0:D]).then_inc(g.wvT_copied, 1)


def split_head_weights_hi(nc, act, g, hp, r):
    raw_there(act, g, hp, r)
    nc.scalar.copy(g.wqk_hi[r][:], g.raw_qkv[:, r, :, 0:2, :]).then_inc(g.wqk_hi_ready, 1)


def split_head_weights_lo(nc, pool, g, hp, r):
    pool.wait_ge(g.wqk_hi_ready, 2 * hp + r + 1)
    nc.gpsimd.tensor_tensor(g.wqk_lo[r][:], g.raw_qkv[:, r, :, 0:2, :], g.wqk_hi[r][:].bitcast(F32), ALU.subtract).then_inc(g.wqk_lo_ready, 1)


def split_head_values_hi(nc, act, g, hp, r):
    act.wait_ge(g.m_ready, 2 * hp + r + 1)
    nc.scalar.copy(g.m_hi[r][:].rearrange("p k n -> p (k n)"), g.ps_head[:]).then_inc(g.m_hi_ready, 1)


def split_head_values_lo(nc, dve, g, hp, r):
    dve.wait_ge(g.m_hi_ready, 2 * hp + r + 1)
    nc.vector.tensor_tensor(g.m_lo[r][:].rearrange("p k n -> p (k n)"), g.ps_head[:],
                            g.m_hi[r][:].rearrange("p k n -> p (k n)").bitcast(F32), ALU.subtract).then_inc(g.m_lo_ready, 1)


def attention_phase(nc, mem, dram, g):
    with ExitStack() as ctx:
        m = Memory(nc, ctx)
        q_hi, q_lo = m.sb("q_hi", [P, PT], F32R), m.sb("q_lo", [P, PT], F32R)
        k_hi, k_lo = m.sb("k_hi", [P, PT], F32R), m.sb("k_lo", [P, PT], F32R)
        negmax, rowsum, rinv = m.sb("negmax", [P, 4]), m.sb("rowsum", [P, 4]), m.sb("rinv", [P, 4])
        probs = m.sb("probs", [P, 2, 2, S])
        half = m.sb("half_sum", [P, 2, S])
        wsum = m.sb("wsum", [P, 2, S])
        wsum_hi, wsum_lo = m.sb("wsum_hi", [P, PT], F32R), m.sb("wsum_lo", [P, PT], F32R)
        colsum = m.sb("colsum", [P, PT])
        prod = m.sb("prod", [P, KT, PT])
        ps_q, ps_k = m.ps("ps_q"), m.ps("ps_k")
        ps_s = [m.ps("ps_s0"), m.ps("ps_s1")]
        ps_y = [m.ps("ps_y0"), m.ps("ps_y1")]
        ps_c = m.ps("ps_c")

        proj_ready = m.sem("proj_ready")
        qk_hi_ready = m.sem("qk_hi_ready")
        qk_lo_ready = m.sem("qk_lo_ready")
        scores_ready = m.sem("scores_ready")
        negmax_ready = m.sem("negmax_ready")
        probs_ready = m.sem("probs_ready")
        rinv_ready = m.sem("rinv_ready")
        half_ready = m.sem("half_ready")
        wsum_ready = m.sem("wsum_ready")
        wsum_hi_ready = m.sem("wsum_hi_ready")
        wsum_lo_ready = m.sem("wsum_lo_ready")
        y_ready = m.sem("y_ready")
        c_ready = m.sem("c_ready")
        c_copied = m.sem("c_copied")
        prod_ready = m.sem("prod_ready")
        acc_added = m.sem("acc_added")

        def run_heads(eng, head):
            with eng.Fori(0, HEADS // 2 - 1) as hp:
                head(hp, 0, False)
                head(hp, 1, False)
            head(HEADS // 2 - 1, 0, False)
            head(HEADS // 2 - 1, 1, True)

        block = ctx.enter_context(nc.Block())

        @block.sync
        def _(sp):
            with sp.Fori(0, HEADS // 2 - 1) as i:
                for r in range(2):
                    done = 2 * i + r + 1
                    sp.wait_ge(g.m_ready, done)
                    sp.wait_ge(g.wqk_hi_ready, done)
                    sp.wait_ge(g.wqk_lo_ready, done)
                    load_head(nc, sp, dram, g, 2 * i + (2 + r), r)

        @block.tensor
        def _(pe):
            def project(n, pair, r, k_wqk):
                at_least(pe, g.wqk_hi_ready, k_wqk)
                at_least(pe, g.wqk_lo_ready, k_wqk)
                for t, ps in enumerate((ps_q, ps_k)):
                    for k in range(KT):
                        cols = bass.ds(pair * PT, PT)
                        last = three_pass(nc, ps[:], g.wqk_hi[r][:, k, t, :], g.wqk_lo[r][:, k, t, :],
                                          g.h_hi[:, k, cols], g.h_lo[:, k, cols], k == 0, k == KT - 1)
                    last.then_inc(proj_ready, 1)

            def step(n, pair, r, follow):
                pe.wait_ge(qk_hi_ready, 2 * n + 2)
                pe.wait_ge(qk_lo_ready, 2 * n + 2)
                pe.wait_ge(probs_ready, 4 * n)
                for j in range(2):
                    keys = slice(j * S, (j + 1) * S)
                    for qt in range(2):
                        qs = slice(j * S + qt * P, j * S + (qt + 1) * P)
                        last = three_pass(nc, ps_s[j][:, qt * S:(qt + 1) * S], q_hi[:, qs], q_lo[:, qs], k_hi[:, keys], k_lo[:, keys], True, True)
                    last.then_inc(scores_ready, 1)
                if follow:
                    project(*follow)
                pe.wait_ge(prod_ready, 2 * n)
                for o in range(KT):
                    for k in range(KT):
                        cols = bass.ds(pair * PT, PT)
                        last = three_pass(nc, ps_y[o][:], g.m_hi[r][:, k, o * P:(o + 1) * P], g.m_lo[r][:, k, o * P:(o + 1) * P],
                                          g.h_hi[:, k, cols], g.h_lo[:, k, cols], k == 0, k == KT - 1)
                    last.then_inc(y_ready, 1)
                pe.wait_ge(wsum_hi_ready, n + 1)
                pe.wait_ge(wsum_lo_ready, n + 1)
                pe.wait_ge(c_copied, n)
                nc.tensor.matmul(ps_c[:], g.ones_r[:], wsum_hi[:], start=True, stop=False)
                nc.tensor.matmul(ps_c[:], g.ones_r[:], wsum_lo[:], start=False, stop=True).then_inc(c_ready, 1)

            def head(hp, r, final):
                h = 2 * hp + r
                nhp, nr = (hp, 1) if r == 0 else (hp + 1, 0)
                pe.wait_ge(g.m_hi_ready, h + 1)
                pe.wait_ge(g.m_lo_ready, h + 1)
                if not final:
                    transpose_head_values(nc, pe, g, nhp, nr)
                with pe.Fori(0, PAIRS - 1) as p:
                    n = 8 * h + p
                    step(n, p, r, (n + 1, p + 1, r, 0))
                if not final:
                    combine_head_values(nc, pe, g, nhp, nr)
                n = 8 * h + 7
                step(n, PAIRS - 1, r, None if final else (n + 1, 0, nr, h + 2))

            pe.wait_ge(g.ones_r_ready, 1)
            project(0, 0, 0, 1)
            run_heads(pe, head)

        @block.scalar
        def _(act):
            def split_hi(n):
                for t, (ps, hi) in enumerate(((ps_q, q_hi), (ps_k, k_hi))):
                    act.wait_ge(proj_ready, 2 * n + t + 1)
                    nc.scalar.activation(hi[:], ps[:], ACT.Copy, scale=SCALE if t == 0 else 1.0).then_inc(qk_hi_ready, 1)

            def step(n, follow):
                act.wait_ge(wsum_ready, 2 * n)
                for j in range(2):
                    act.wait_ge(negmax_ready, 2 * n + j + 1)
                    for qt in range(2):
                        i = 2 * j + qt
                        nc.scalar.activation(probs[:, j, qt, :], ps_s[j][:, qt * S:(qt + 1) * S], ACT.Exp,
                                             bias=negmax[:, i:i + 1], accum_out=rowsum[:, i:i + 1]).then_inc(probs_ready, 1)
                if follow:
                    split_hi(n + 1)
                act.wait_ge(wsum_ready, 2 * n + 2)
                act.wait_ge(c_ready, n)
                nc.scalar.copy(wsum_hi[:], wsum[:].rearrange("p j s -> p (j s)")).then_inc(wsum_hi_ready, 1)
                act.wait_ge(c_ready, n + 1)
                act.wait_ge(prod_ready, 2 * n)
                nc.scalar.copy(colsum[:], ps_c[:]).then_inc(c_copied, 1)

            def head(hp, r, final):
                h = 2 * hp + r
                nhp, nr = (hp, 1) if r == 0 else (hp + 1, 0)
                if not final:
                    at_least(act, y_ready, 16 * h)
                    copy_head_values(nc, act, g, nhp, nr)
                    split_head_weights_hi(nc, act, g, nhp, nr)
                with act.Fori(0, PAIRS - 1) as p:
                    step(8 * h + p, True)
                if not final:
                    split_head_values_hi(nc, act, g, nhp, nr)
                step(8 * h + 7, not final)

            split_hi(0)
            run_heads(act, head)

        @block.vector
        def _(dve):
            def split_lo(n, t):
                ps, hi, lo = ((ps_q, q_hi, q_lo), (ps_k, k_hi, k_lo))[t]
                dve.wait_ge(qk_hi_ready, 2 * n + t + 1)
                nc.vector.scalar_tensor_tensor(lo[:], ps[:], SCALE if t == 0 else 1.0, hi[:].bitcast(F32), ALU.mult, ALU.subtract).then_inc(qk_lo_ready, 1)

            def maxima(n):
                for j in range(2):
                    dve.wait_ge(scores_ready, 2 * n + j + 1)
                    nc.vector.tensor_reduce(negmax[:, 2 * j:2 * j + 2], ps_s[j][:].rearrange("p (q s) -> p q s", q=2),
                                            AX.X, ALU.max, negate=True).then_inc(negmax_ready, 1)

            def step(n, follow):
                for j in range(2):
                    dve.wait_ge(probs_ready, 4 * n + 2 * j + 2)
                    nc.vector.reciprocal(rinv[:, 2 * j:2 * j + 2], rowsum[:, 2 * j:2 * j + 2]).then_inc(rinv_ready, 1)
                    dve.wait_ge(rinv_ready, 2 * n + j + 1)
                    nc.vector.tensor_scalar(half[:, j, :], probs[:, j, 0, :], rinv[:, 2 * j:2 * j + 1], None, ALU.mult).then_inc(half_ready, 1)
                    dve.wait_ge(half_ready, 2 * n + j + 1)
                    dve.wait_ge(wsum_lo_ready, n)
                    nc.vector.scalar_tensor_tensor(wsum[:, j, :], probs[:, j, 1, :], rinv[:, 2 * j + 1:2 * j + 2], half[:, j, :],
                                                   ALU.mult, ALU.add).then_inc(wsum_ready, 1)
                if follow:
                    split_lo(n + 1, 0)
                dve.wait_ge(wsum_hi_ready, n + 1)
                nc.vector.tensor_tensor(wsum_lo[:], wsum[:].rearrange("p j s -> p (j s)"), wsum_hi[:].bitcast(F32), ALU.subtract).then_inc(wsum_lo_ready, 1)
                if follow:
                    split_lo(n + 1, 1)
                    maxima(n + 1)
                dve.wait_ge(c_copied, n + 1)
                dve.wait_ge(acc_added, 2 * n)
                for o in range(KT):
                    nc.vector.tensor_tensor(prod[:, o, :], ps_y[o][:], colsum[:], ALU.mult).then_inc(prod_ready, 1)

            def head(hp, r, final):
                h = 2 * hp + r
                nhp, nr = (hp, 1) if r == 0 else (hp + 1, 0)
                with dve.Fori(0, PAIRS - 1) as p:
                    step(8 * h + p, True)
                if not final:
                    split_head_values_lo(nc, dve, g, nhp, nr)
                step(8 * h + 7, not final)

            split_lo(0, 0)
            split_lo(0, 1)
            maxima(0)
            run_heads(dve, head)

        @block.gpsimd
        def _(pool):
            def step(n, pair):
                for o in range(KT):
                    pool.wait_ge(prod_ready, 2 * n + o + 1)
                    cols = g.accT[:, o, bass.ds(pair * PT, PT)]
                    nc.gpsimd.tensor_tensor(cols, cols, prod[:, o, :], ALU.add).then_inc(acc_added, 1)

            def head(hp, r, final):
                h = 2 * hp + r
                nhp, nr = (hp, 1) if r == 0 else (hp + 1, 0)
                at_least(pool, acc_added, 16 * h)
                if not final:
                    split_head_weights_lo(nc, pool, g, nhp, nr)
                with pool.Fori(0, PAIRS - 1) as p:
                    step(8 * h + p, p)
                step(8 * h + 7, PAIRS - 1)

            pool.wait_ge(g.acc_zeroed, 1)
            run_heads(pool, head)
            pool.wait_ge(acc_added, 2 * HEADS * PAIRS)


class Shared:
    pass


def shared_memory(nc, m):
    g = Shared()
    g.ident = m.sb("ident", [P, P])
    g.ones = m.sb("ones", [P, P])
    g.ones_r = m.sb("ones_r", [P, P], F32R)
    g.minus_half = m.sb("minus_half", [P, 4])
    g.first_rank = m.sb("first_rank", [P, 2, EXPERTS])
    g.modT = m.sb("modT", [P, 6, KT, B])
    g.ident_ready, g.ones_ready, g.ones_r_ready = m.sem("ident_ready"), m.sem("ones_ready"), m.sem("ones_r_ready")
    g.half_const_ready, g.rank_ready = m.sem("half_const_ready"), m.sem("rank_ready")
    g.ffn_raw_loaded = m.sem("ffn_raw_loaded")
    g.raw_wg = m.sb("raw_wg", [EXPERTS, D])
    g.arena_offset = nc.sbuf_base
    g.arena = m.sb("arena", [P, ARENA])
    return g


def head_memory(nc, m, g):
    g.accT = m.sb("accT", [P, KT, TOK])
    g.h_hi, g.h_lo = m.sb("h_hi", [P, KT, TOK], F32R), m.sb("h_lo", [P, KT, TOK], F32R)
    g.raw_qkv = m.sb("raw_qkv", [P, 2, KT, 3, DH])
    g.raw_o = m.sb("raw_o", [P, 2, D])
    g.wvT = m.sb("wvT", [P, D])
    g.wqk_hi = [m.sb(f"wqk_hi{r}", [P, KT, 2, DH], F32R) for r in range(2)]
    g.wqk_lo = [m.sb(f"wqk_lo{r}", [P, KT, 2, DH], F32R) for r in range(2)]
    g.m_hi = [m.sb(f"m_hi{r}", [P, KT, D], F32R) for r in range(2)]
    g.m_lo = [m.sb(f"m_lo{r}", [P, KT, D], F32R) for r in range(2)]
    g.ps_head = m.ps("ps_head")
    g.raw_loaded = [m.sem("raw_loaded0"), m.sem("raw_loaded1")]
    g.wvT_ready, g.wvT_copied = m.sem("wvT_ready"), m.sem("wvT_copied")
    g.wqk_hi_ready, g.wqk_lo_ready = m.sem("wqk_hi_ready"), m.sem("wqk_lo_ready")
    g.m_ready, g.m_hi_ready, g.m_lo_ready = m.sem("m_ready"), m.sem("m_hi_ready"), m.sem("m_lo_ready")
    g.acc_zeroed = m.sem("acc_zeroed")


def ffn_memory(nc, m, g):
    shapes = dict(A1=(KT, ER), A3=(KT, ER), W1=(KT, FF), W3=(KT, FF), B1=(ET, FF), B3=(ET, FF), W2=(FT, D), A2=(FT, ER), B2=(ET, D))
    g.wgT = m.sb("wgT", [P, KT, EXPERTS])
    g.w_hi = {name: m.sb(f"{name}T_hi", [P, *shape], F32R) for name, shape in shapes.items()}
    g.w_lo = {name: m.sb(f"{name}T_lo", [P, *shape], F32R) for name, shape in shapes.items()}


def store_attention(nc, dram, g):
    with nc.semaphore("acc_stored") as acc_stored, nc.Block() as block:
        @block.sync
        def _(sp):
            sp.dma_start(dram["acc"], g.accT[:]).then_inc(acc_stored, 16)
            sp.wait_ge(acc_stored, 16)



ARENA = 12288


class Arena:

    def __init__(self, nc, base, size):
        self.nc, self.at, self.end = nc, base, base + size

    def sb(self, name, shape, dt=F32):
        size = math.prod(shape[1:]) * (2 if dt == BF16 else 4)
        assert self.at + size <= self.end, name
        t = self.nc.alloc_sbuf_tensor_at(name, shape, dt, offset=self.at)
        self.at += size
        return t


def raw_weights(g):
    shapes = dict(A1=(ET, D), A3=(ET, D), W1=(FT, D), W3=(FT, D), B1=(FT, ER), B3=(FT, ER),
                  W2=(KT, FF), A2=(ET, FF), B2=(KT, ER))
    at, views = 0, {}
    for name, (tiles, n) in shapes.items():
        views[name] = g.arena[:, at:at + tiles * n].rearrange("p (t n) -> p t n", t=tiles)
        at += tiles * n
    assert at <= ARENA
    return views


def load_ffn_weights(nc, sp, dram, g):
    raw = raw_weights(g)
    for name in ("W1", "W3", "W2"):
        sp.dma_start(raw[name], dram[name].rearrange("(t p) n -> p t n", p=P)).then_inc(g.ffn_raw_loaded, 16)
    for name in ("A1", "A3", "A2"):
        sp.dma_start(raw[name], dram[name].rearrange("e r n -> (e r) n").rearrange("(t p) n -> p t n", p=P)).then_inc(g.ffn_raw_loaded, 16)
    for name, tiles in (("B1", FT), ("B3", FT), ("B2", KT)):
        src = dram[name].rearrange("e (t p) r -> t p e r", p=P)
        for t in range(tiles):
            sp.dma_start(raw[name][:, t].rearrange("p (e r) -> p e r", e=EXPERTS), src[t]).then_inc(g.ffn_raw_loaded, 16)
    sp.dma_start(g.raw_wg[:], dram["Wg"]).then_inc(g.ffn_raw_loaded, 16)


FFN_LOADS = 16 * (6 + 2 * FT + KT + 1)


def ffn_weight_phase(nc, mem, dram, g):
    with ExitStack() as ctx:
        m = Memory(nc, ctx)
        banks = [m.ps(f"ps_w{i}") for i in range(4)]
        ps_wg = m.ps("ps_wg")
        w_transposed, w_hi_ready, w_lo_ready = m.sem("w_transposed"), m.sem("w_hi_ready"), m.sem("w_lo_ready")
        wg_ready, wg_copied = m.sem("wg_ready"), m.sem("wg_copied")
        raw = raw_weights(g)
        groups = []
        for name in ("A1", "A3", "W1", "W3", "B1", "B3", "W2", "A2", "B2"):
            tiles = raw[name].shape[1]
            blocks = [(outer, inner) for outer in range(raw[name].shape[2] // P) for inner in range(tiles)]
            for at in range(0, len(blocks), 4):
                part = blocks[at:at + 4]
                groups.append((name, at * P, part))

        block = ctx.enter_context(nc.Block())

        def flat(t):
            return t[:].rearrange("p a b -> p (a b)")

        @block.tensor
        def _(pe):
            pe.wait_ge(g.ffn_raw_loaded, FFN_LOADS)
            for k in range(KT):
                last = nc.tensor.transpose(ps_wg[:, k * EXPERTS:(k + 1) * EXPERTS], g.raw_wg[:, k * P:(k + 1) * P], g.ident[0:EXPERTS, 0:EXPERTS])
            last.then_inc(wg_ready, 1)
            for n, (name, at, part) in enumerate(groups):
                at_least(pe, w_lo_ready, n - 3)
                for i, (outer, inner) in enumerate(part):
                    last = nc.tensor.transpose(banks[n % 4][:, i * P:(i + 1) * P], raw[name][:, inner, outer * P:(outer + 1) * P], g.ident[:])
                last.then_inc(w_transposed, 1)

        @block.scalar
        def _(act):
            act.wait_ge(wg_ready, 1)
            nc.scalar.copy(g.wgT[:].rearrange("p k e -> p (k e)"), ps_wg[:, 0:KT * EXPERTS]).then_inc(wg_copied, 1)
            for n, (name, at, part) in enumerate(groups):
                act.wait_ge(w_transposed, n + 1)
                size = len(part) * P
                nc.scalar.copy(flat(g.w_hi[name])[:, at:at + size], banks[n % 4][:, 0:size]).then_inc(w_hi_ready, 1)
            act.wait_ge(wg_copied, 1)

        @block.vector
        def _(dve):
            for n, (name, at, part) in enumerate(groups):
                dve.wait_ge(w_hi_ready, n + 1)
                size = len(part) * P
                nc.vector.tensor_tensor(flat(g.w_lo[name])[:, at:at + size], banks[n % 4][:, 0:size],
                                        flat(g.w_hi[name])[:, at:at + size].bitcast(F32), ALU.subtract).then_inc(w_lo_ready, 1)
            dve.wait_ge(w_lo_ready, len(groups))


ROUTE = 17


def ffn_phase(nc, mem, dram, g):
    with ExitStack() as ctx:
        m = Memory(nc, ctx)
        arena = Arena(nc, g.arena_offset, 4 * ARENA)
        sb = arena.sb
        x_in = [sb(f"x_in2_{r}", [P, 2, D]) for r in range(2)]
        acc_in = [sb(f"acc_in{r}", [P, KT, S]) for r in range(2)]
        x2 = [sb(f"x2_{r}", [P, 2, D]) for r in range(2)]
        gated = sb("gated", [P, KT, S])
        xn = gated[:]
        h32 = sb("h32_2", [P, KT, S])
        chosen = sb("chosen_by_rank", [P, 2, 2, ER])
        maskT = [[sb(f"maskT{r}{k}", [P, ET, S], BF16) for k in range(2)] for r in range(2)]
        mask_step = sb("mask_step", [P, ET, S], BF16)
        weightT = [sb(f"weightT{r}", [P, 2, S]) for r in range(2)]
        a_masked = [sb(f"a_masked{i}", [P, ET, S]) for i in range(2)]
        silu = [sb(f"silu{k}", [P, S]) for k in range(2)]
        glu = [sb(f"glu{k}", [P, S]) for k in range(2)]
        first_w = [sb(f"first_weighted{i}", [P, S]) for i in range(2)]
        second_w = sb("second_weighted", [P, S])
        both_w = sb("both_weighted", [P, S])
        a2_part = [sb(f"a2_part{k}", [P, ET, S]) for k in range(2)]
        out_gated = sb("out_gated", [P, KT, S])
        y_out = m.sb("y_out", [P, 2, D])
        stats, meanvar = m.sb("ln2_stats", [P, 2, 6]), m.sb("ln2_meanvar", [P, 2, 2])
        vareps, rstd = m.sb("ln2_vareps", [P, 2]), m.sb("ln2_rstd", [P, 2])
        logits, rest = m.sb("logits", [P, 2, EXPERTS]), m.sb("logits_rest", [P, 2, EXPERTS])
        equal = [m.sb(f"equal{k}", [P, 2, EXPERTS]) for k in range(2)]
        ranked = [m.sb(f"ranked{k}", [P, 2, EXPERTS]) for k in range(2)]
        onehot = [m.sb(f"onehot{k}", [P, 2, EXPERTS]) for k in range(2)]
        top = [m.sb(f"top{k}", [P, 2]) for k in range(2)]
        best = [m.sb(f"best_rank{k}", [P, 2]) for k in range(2)]
        gap, tanh_gap, weight = m.sb("gap", [P, 2]), m.sb("tanh_gap", [P, 2]), m.sb("weight", [P, 2, 2])
        h_hi = [m.sb(f"h2_hi{r}", [P, KT, S], F32R) for r in range(2)]
        h_lo = [m.sb(f"h2_lo{r}", [P, KT, S], F32R) for r in range(2)]
        a_hi = [[[m.sb(f"a_hi{r}{w}{k}", [P, ET, S], F32R) for k in range(2)] for w in range(2)] for r in range(2)]
        a_lo = [[[m.sb(f"a_lo{r}{w}{k}", [P, ET, S], F32R) for k in range(2)] for w in range(2)] for r in range(2)]
        v_hi = [[m.sb(f"v_hi{k}{i}", [P, S], F32R) for i in range(2)] for k in range(3)]
        v_lo = [[m.sb(f"v_lo{k}{i}", [P, S], F32R) for i in range(2)] for k in range(3)]
        a2_hi, a2_lo = m.sb("a2_hi", [P, ET, S], F32R), m.sb("a2_lo", [P, ET, S], F32R)

        ps_x1 = [m.ps(f"ps_x1_{i}") for i in range(2)]
        ps_x3 = [m.ps(f"ps_x3_{i}") for i in range(2)]
        ps_out = m.ps("ps_out")
        ps_a2 = [m.ps(f"ps_a2_{k}") for k in range(2)]
        ps_p = m.ps("ps_prep")

        inputs_loaded = [m.sem("inputs_loaded0"), m.sem("inputs_loaded1")]
        gated_ready = m.sem("gated_ready")
        gatedT_ready = m.sem("gatedT_ready")
        x2_ready = m.sem("x2_ready")
        stats_ready, moments, ve_ready = m.sem("stats2_ready"), m.sem("moments2"), m.sem("ve2_ready")
        rstd_ready = m.sem("rstd2_ready")
        xn_ready = m.sem("xn2_ready")
        xnT_ready = m.sem("xn2T_ready")
        h32_ready = m.sem("h2_ready")
        h_hi_ready, h_lo_ready = m.sem("h2_hi_ready"), m.sem("h2_lo_ready")
        logits_ready = m.sem("logits_ready")
        route = m.sem("route")
        tanh_ready = m.sem("tanh_ready")
        mask_ready, maskT_ready = m.sem("mask_transposed"), m.sem("maskT_ready")
        mask_step_ready = m.sem("mask_step_ready")
        weight_ready, weightT_ready = m.sem("weight_transposed"), m.sem("weightT_ready")
        a_ready = m.sem("a_ready")
        masked_ready = m.sem("masked_ready")
        a_hi_ready, a_lo_ready = m.sem("a_hi_ready"), m.sem("a_lo_ready")
        up_ready = [m.sem("up_first_ready"), m.sem("up_second_ready")]
        silu_ready = [m.sem("silu_first_ready"), m.sem("silu_second_ready")]
        glu_ready = [m.sem("glu_first_ready"), m.sem("glu_second_ready")]
        weighted = [m.sem("weighted_first"), m.sem("weighted_second"), m.sem("weighted_both")]
        v_hi_ready = [m.sem(f"v_hi_ready{k}") for k in range(3)]
        v_lo_ready = [m.sem(f"v_lo_ready{k}") for k in range(3)]
        down_ready = m.sem("down_ready")
        a2_step = m.sem("a2_step")
        a2_hi_ready, a2_lo_ready = m.sem("a2_hi_ready"), m.sem("a2_lo_ready")
        out_ready = m.sem("out_ready")
        out_gated_ready = m.sem("out_gated_ready")
        outT_ready = m.sem("outT_ready")
        y_ready = m.sem("y_ready2")
        stored = m.sem("stored")

        xg = dram["x"].rearrange("b (t p) c -> b p t c", p=P)
        og = dram["out"].rearrange("b (t p) c -> b p t c", p=P)
        accg = dram["acc"].rearrange("p k (b s) -> b p k s", s=S)

        block = ctx.enter_context(nc.Block())

        @block.sync
        def _(sp):
            def load(b, r):
                sp.dma_start(x_in[r][:], xg[b]).then_inc(inputs_loaded[r], 16)
                sp.dma_start(acc_in[r][:], accg[b]).then_inc(inputs_loaded[r], 16)

            def iteration(b, r, more):
                if more:
                    sp.wait_ge(x2_ready, b + 1)
                    load(b + 2, r)
                sp.wait_ge(y_ready, b + 1)
                sp.dma_start(og[b], y_out[:]).then_inc(stored, 16)

            load(0, 0)
            load(1, 1)
            with sp.Fori(0, B // 2 - 1) as i:
                for r in range(2):
                    iteration(2 * i + r, r, True)
            for r in range(2):
                iteration(B - 2 + r, r, False)
            sp.wait_ge(stored, 16 * B)

        def all_batches(eng, iteration):
            iteration(0, 0, False, True)
            with eng.Fori(0, B // 2 - 1) as i:
                iteration(2 * i + 1, 1, True, True)
                iteration(2 * i + 2, 0, True, True)
            iteration(B - 1, 1, True, False)

        @block.tensor
        def _(pe):
            def transpose_gated(q, r):
                pe.wait_ge(gated_ready, 2 * q + 2)
                at_least(pe, masked_ready, 4 * q)
                at_least(pe, y_ready, q - 1)
                for t in range(2):
                    for k in range(KT):
                        last = nc.tensor.transpose(ps_p[:, t * D + k * P:t * D + (k + 1) * P], gated[:, k, t * P:(t + 1) * P], g.ident[:])
                last.then_inc(gatedT_ready, 1)

            def transpose_normalised(q, r):
                pe.wait_ge(xn_ready, 2 * q + 2)
                for k in range(KT):
                    for t in range(2):
                        last = nc.tensor.transpose(ps_p[:, k * S + t * P:k * S + (t + 1) * P], xn[:, t, k * P:(k + 1) * P], g.ident[:])
                last.then_inc(xnT_ready, 1)

            def router(q, r):
                pe.wait_ge(h32_ready, 2 * q + 2)
                for t in range(2):
                    for k in range(KT):
                        last = nc.tensor.matmul(ps_p[:, t * EXPERTS:(t + 1) * EXPERTS], h32[:, k, t * P:(t + 1) * P], g.wgT[:, k, :],
                                                start=(k == 0), stop=(k == KT - 1))
                last.then_inc(logits_ready, 1)

            def transpose_masks(q, choice):
                pe.wait_ge(route, ROUTE * q + ROUTE)
                if choice == 1:
                    pe.wait_ge(maskT_ready, 2 * q + 1)
                for e in range(ET):
                    for t in range(2):
                        last = nc.tensor.transpose(ps_p[:, e * S + t * P:e * S + (t + 1) * P], chosen[:, t, choice, e * P:(e + 1) * P], g.ident[:])
                last.then_inc(mask_ready, 1)

            def transpose_weights(q):
                pe.wait_ge(maskT_ready, 2 * q + 2)
                for k in range(2):
                    for t in range(2):
                        last = nc.tensor.transpose(ps_p[:, k * S + t * P:k * S + (t + 1) * P], weight[:, t, k:k + 1].broadcast_to([P, P]), g.ident[:])
                last.then_inc(weight_ready, 1)

            def lora_a(q, r, w):
                if w == 0:
                    pe.wait_ge(weightT_ready, q + 1)
                    pe.wait_ge(h_hi_ready, q + 1)
                    pe.wait_ge(h_lo_ready, q + 1)
                else:
                    pe.wait_ge(masked_ready, 4 * q + 2)
                hi, lo = g.w_hi[("A1", "A3")[w]], g.w_lo[("A1", "A3")[w]]
                for e in range(ET):
                    for k in range(KT):
                        cols = slice(e * P, (e + 1) * P)
                        last = three_pass(nc, ps_p[:, e * S:(e + 1) * S], hi[:, k, cols], lo[:, k, cols], h_hi[r][:, k, :], h_lo[r][:, k, :], k == 0, k == KT - 1)
                last.then_inc(a_ready, 1)

            def up_first(b, r, f):
                at_least(pe, glu_ready[1], FT * b + f - 1)
                if f == 0:
                    pe.wait_ge(h_hi_ready, b + 1)
                    pe.wait_ge(h_lo_ready, b + 1)
                    pe.wait_ge(a_hi_ready, 4 * b + 4)
                    pe.wait_ge(a_lo_ready, 4 * b + 4)
                cols = slice(f * P, (f + 1) * P)
                for w, ps in enumerate((ps_x1[f % 2], ps_x3[f % 2])):
                    base, lora = ("W1", "W3")[w], ("B1", "B3")[w]
                    for k in range(KT):
                        three_pass(nc, ps[:, 0:S], g.w_hi[base][:, k, cols], g.w_lo[base][:, k, cols], h_hi[r][:, k, :], h_lo[r][:, k, :],
                                   k == 0, False, skip_group_check=True)
                    for e in range(ET):
                        last = three_pass(nc, ps[:, 0:S], g.w_hi[lora][:, e, cols], g.w_lo[lora][:, e, cols], a_hi[r][w][0][:, e, :], a_lo[r][w][0][:, e, :],
                                          False, e == ET - 1, skip_group_check=True)
                    last.then_inc(up_ready[0], 1)

            def up_second(b, r, f):
                pe.wait_ge(glu_ready[0], FT * b + f + 1)
                cols = slice(f * P, (f + 1) * P)
                for w, ps in enumerate((ps_x1[f % 2], ps_x3[f % 2])):
                    lora = ("B1", "B3")[w]
                    for e in range(ET):
                        last = three_pass(nc, ps[:, 0:S], g.w_hi[lora][:, e, cols], g.w_lo[lora][:, e, cols], a_hi[r][w][1][:, e, :], a_lo[r][w][1][:, e, :],
                                          False, e == ET - 1, skip_group_check=True)
                    last.then_inc(up_ready[1], 1)

            def down(b, f):
                if f == 0:
                    at_least(pe, out_gated_ready, 2 * b)
                    at_least(pe, a2_step, 3 * b)
                i = f % 2
                for k in range(2):
                    pe.wait_ge(v_hi_ready[k], FT * b + f + 1)
                    pe.wait_ge(v_lo_ready[k], FT * b + f + 1)
                    for e in range(ET):
                        cols = slice(e * P, (e + 1) * P)
                        three_pass(nc, ps_a2[k][:, e * S:(e + 1) * S], g.w_hi["A2"][:, f, cols], g.w_lo["A2"][:, f, cols], v_hi[k][i][:], v_lo[k][i][:],
                                   f == 0 and e == 0, f == FT - 1, skip_group_check=True)
                pe.wait_ge(v_hi_ready[2], FT * b + f + 1)
                pe.wait_ge(v_lo_ready[2], FT * b + f + 1)
                for o in range(KT):
                    cols = slice(o * P, (o + 1) * P)
                    last = three_pass(nc, ps_out[:, o * S:(o + 1) * S], g.w_hi["W2"][:, f, cols], g.w_lo["W2"][:, f, cols], v_hi[2][i][:], v_lo[2][i][:],
                                      f == 0 and o == 0, False, skip_group_check=True)
                last.then_inc(down_ready, 1)

            def lora_down(b):
                pe.wait_ge(a2_hi_ready, b + 1)
                pe.wait_ge(a2_lo_ready, b + 1)
                for o in range(KT):
                    cols = slice(o * P, (o + 1) * P)
                    for e in range(ET):
                        last = three_pass(nc, ps_out[:, o * S:(o + 1) * S], g.w_hi["B2"][:, e, cols], g.w_lo["B2"][:, e, cols], a2_hi[:, e, :], a2_lo[:, e, :],
                                          False, e == ET - 1, skip_group_check=True)
                last.then_inc(out_ready, 1)

            def transpose_out(b):
                pe.wait_ge(masked_ready, min(4 * b + 8, 4 * B) if isinstance(b, int) else 4 * b + 8)
                pe.wait_ge(out_gated_ready, 2 * b + 2)
                for t in range(2):
                    for k in range(KT):
                        last = nc.tensor.transpose(ps_p[:, t * D + k * P:t * D + (k + 1) * P], out_gated[:, k, t * P:(t + 1) * P], g.ident[:])
                last.then_inc(outT_ready, 1)

            def iteration(b, r, before, after):
                q, s = b + 1, 1 - r
                up_first(b, r, 0)
                up_first(b, r, 1)
                if before:
                    lora_down(b - 1)
                up_second(b, r, 0)
                if before:
                    transpose_out(b - 1)
                up_first(b, r, 2)
                if after:
                    transpose_gated(q, s)
                up_second(b, r, 1)
                down(b, 0)
                up_first(b, r, 3)
                if after:
                    transpose_normalised(q, s)
                up_second(b, r, 2)
                down(b, 1)
                if after:
                    router(q, s)
                up_first(b, r, 4)
                up_second(b, r, 3)
                if after:
                    transpose_masks(q, 0)
                down(b, 2)
                if after:
                    transpose_masks(q, 1)
                up_first(b, r, 5)
                up_second(b, r, 4)
                if after:
                    transpose_weights(q)
                down(b, 3)
                if after:
                    lora_a(q, s, 0)
                up_first(b, r, 6)
                up_second(b, r, 5)
                if after:
                    lora_a(q, s, 1)
                down(b, 4)
                up_second(b, r, 6)
                down(b, 5)
                down(b, 6)

            transpose_gated(0, 0)
            transpose_normalised(0, 0)
            router(0, 0)
            transpose_masks(0, 0)
            transpose_masks(0, 1)
            transpose_weights(0)
            lora_a(0, 0, 0)
            lora_a(0, 0, 1)
            all_batches(pe, iteration)
            lora_down(B - 1)
            transpose_out(B - 1)

        @block.scalar
        def _(act):
            def modulate(q, r):
                act.wait_ge(xnT_ready, q + 1)
                for k in range(KT):
                    nc.scalar.activation(h32[:, k, :], ps_p[:, k * S:(k + 1) * S], ACT.Identity,
                                         scale=g.modT[:, CB, k, bass.ds(q, 1)], bias=g.modT[:, SB_, k, bass.ds(q, 1)]).then_inc(h32_ready, 1)
                act.wait_ge(h32_ready, 2 * q + 2)
                nc.scalar.copy(h_hi[r][:], h32[:]).then_inc(h_hi_ready, 1)

            def tanh_of_gap(q):
                act.wait_ge(route, ROUTE * q + 13)
                nc.scalar.activation(tanh_gap[:], gap[:], ACT.Tanh, scale=0.5).then_inc(tanh_ready, 1)

            def copy_mask(q, r, choice):
                act.wait_ge(mask_ready, 2 * q + choice + 1)
                nc.scalar.copy(maskT[r][choice][:].rearrange("p e s -> p (e s)"), ps_p[:]).then_inc(maskT_ready, 1)

            def copy_weights(q, r):
                act.wait_ge(weight_ready, q + 1)
                nc.scalar.copy(weightT[r][:].rearrange("p k s -> p (k s)"), ps_p[:]).then_inc(weightT_ready, 1)

            def split_a_hi(q, r, w):
                for k in range(2):
                    act.wait_ge(masked_ready, 4 * q + 2 * w + k + 1)
                    nc.scalar.copy(a_hi[r][w][k][:], a_masked[k][:]).then_inc(a_hi_ready, 1)

            def silu_of(b, f, k):
                act.wait_ge(up_ready[k], 2 * FT * b + 2 * f + 1)
                at_least(act, glu_ready[k], FT * b + f)
                nc.scalar.activation(silu[k][:], ps_x1[f % 2][:, 0:S], ACT.Silu).then_inc(silu_ready[k], 1)

            def split_v_hi(b, f, k):
                src = (first_w[f % 2], second_w, both_w)[k]
                act.wait_ge(weighted[k], FT * b + f + 1)
                at_least(act, down_ready, FT * b + f - 1)
                nc.scalar.copy(v_hi[k][f % 2][:], src[:]).then_inc(v_hi_ready[k], 1)

            def split_a2_hi(b):
                act.wait_ge(a2_step, 3 * b + 3)
                nc.scalar.copy(a2_hi[:], a2_part[0][:]).then_inc(a2_hi_ready, 1)

            def gate_out(b):
                act.wait_ge(out_ready, b + 1)
                for k in range(KT):
                    nc.scalar.activation(out_gated[:, k, :], ps_out[:, k * S:(k + 1) * S], ACT.Identity,
                                         scale=g.modT[:, GB, k, bass.ds(b, 1)]).then_inc(out_gated_ready, 1)

            def iteration(b, r, before, after):
                q, s = b + 1, 1 - r
                if before:
                    split_a2_hi(b - 1)
                silu_of(b, 0, 0)
                silu_of(b, 1, 0)
                split_v_hi(b, 0, 0)
                if before:
                    gate_out(b - 1)
                silu_of(b, 0, 1)
                for f in range(2, FT):
                    split_v_hi(b, f - 2, 1)
                    split_v_hi(b, f - 2, 2)
                    if after and f == 4:
                        tanh_of_gap(q)
                    silu_of(b, f, 0)
                    if after and f == 3:
                        modulate(q, s)
                    if after and f == 5:
                        copy_mask(q, s, 1)
                    if after and f == 6:
                        split_a_hi(q, s, 0)
                    split_v_hi(b, f - 1, 0)
                    silu_of(b, f - 1, 1)
                    if after and f == 4:
                        copy_mask(q, s, 0)
                    if after and f == 5:
                        copy_weights(q, s)
                split_v_hi(b, 5, 1)
                split_v_hi(b, 5, 2)
                split_v_hi(b, 6, 0)
                silu_of(b, 6, 1)
                if after:
                    split_a_hi(q, s, 1)
                split_v_hi(b, 6, 1)
                split_v_hi(b, 6, 2)

            modulate(0, 0)
            tanh_of_gap(0)
            copy_mask(0, 0, 0)
            copy_mask(0, 0, 1)
            copy_weights(0, 0)
            split_a_hi(0, 0, 0)
            split_a_hi(0, 0, 1)
            all_batches(act, iteration)
            split_a2_hi(B - 1)
            gate_out(B - 1)

        @block.vector
        def _(dve):
            def gate_attention(q, r):
                dve.wait_ge(inputs_loaded[r], 16 * (q - r) + 32)
                at_least(dve, xnT_ready, q)
                for k in range(KT):
                    nc.vector.tensor_scalar(gated[:, k, :], acc_in[r][:, k, :], g.modT[:, GA, k, bass.ds(q, 1)], None, ALU.mult).then_inc(gated_ready, 1)

            def residual(q, r):
                dve.wait_ge(gatedT_ready, q + 1)
                nc.vector.tensor_tensor(x2[r][:].rearrange("p t c -> p (t c)"), ps_p[:], x_in[r][:].rearrange("p t c -> p (t c)"), ALU.add).then_inc(x2_ready, 1)
                dve.wait_ge(x2_ready, q + 1)
                for t in range(2):
                    nc.vector.bn_stats(stats[:, t, :], x2[r][:, t, :]).then_inc(stats_ready, 1)
                dve.wait_ge(stats_ready, 2 * q + 2)
                combine_stats(nc, dve, stats, meanvar, vareps[:], moments, ve_ready, q)

            def normalise(q, r):
                dve.wait_ge(rstd_ready, q + 1)
                for t in range(2):
                    nc.vector.tensor_scalar(xn[:, t, :], x2[r][:, t, :], meanvar[:, t, 0:1], rstd[:, t:t + 1], ALU.subtract, ALU.mult).then_inc(xn_ready, 1)

            def split_h_lo(q, r):
                dve.wait_ge(h_hi_ready, q + 1)
                nc.vector.tensor_tensor(h_lo[r][:], h32[:], h_hi[r][:].bitcast(F32), ALU.subtract).then_inc(h_lo_ready, 1)

            def routing(q):
                done = ROUTE * q

                def over_experts(t):
                    return t[:].unsqueeze(2).broadcast_to([P, 2, EXPERTS])

                dve.wait_ge(logits_ready, q + 1)
                nc.vector.tensor_copy(logits[:].rearrange("p t e -> p (t e)"), ps_p[:, 0:2 * EXPERTS]).then_inc(route, 1)
                for k, src in enumerate((logits, rest)):
                    n = done + 1 + 6 * k
                    dve.wait_ge(route, n)
                    nc.vector.tensor_reduce(top[k][:], src[:], AX.X, ALU.max).then_inc(route, 1)
                    dve.wait_ge(route, n + 1)
                    nc.vector.tensor_tensor(equal[k][:], src[:], over_experts(top[k]), ALU.is_equal).then_inc(route, 1)
                    dve.wait_ge(route, n + 2)
                    nc.vector.tensor_tensor(ranked[k][:], equal[k][:], g.first_rank[:], ALU.mult).then_inc(route, 1)
                    dve.wait_ge(route, n + 3)
                    nc.vector.tensor_reduce(best[k][:], ranked[k][:], AX.X, ALU.max).then_inc(route, 1)
                    dve.wait_ge(route, n + 4)
                    nc.vector.tensor_tensor(onehot[k][:], ranked[k][:], over_experts(best[k]), ALU.is_equal).then_inc(route, 1)
                    if k == 0:
                        dve.wait_ge(route, n + 5)
                        nc.vector.scalar_tensor_tensor(rest[:], onehot[0][:], -3.0e38, logits[:], ALU.mult, ALU.add).then_inc(route, 1)
                nc.vector.tensor_tensor(gap[:], top[0][:], top[1][:], ALU.subtract).then_inc(route, 1)

            def choices(q):
                done = ROUTE * q
                dve.wait_ge(route, done + 13)
                at_least(dve, weight_ready, q)
                for k in range(2):
                    nc.vector.tensor_copy(chosen[:, :, k, :].rearrange("p t (e r) -> p t e r", e=EXPERTS),
                                          onehot[k][:].unsqueeze(3).broadcast_to([P, 2, EXPERTS, RANK])).then_inc(route, 1)
                dve.wait_ge(tanh_ready, q + 1)
                for k, sign in enumerate((0.5, -0.5)):
                    nc.vector.tensor_scalar(weight[:, :, k], tanh_gap[:], sign, 0.5, ALU.mult, ALU.add).then_inc(route, 1)

            def step_of_masks(q, r):
                dve.wait_ge(maskT_ready, 2 * q + 2)
                nc.vector.tensor_tensor(mask_step[:], maskT[r][1][:], maskT[r][0][:], ALU.subtract).then_inc(mask_step_ready, 1)

            def mask_a(q, r, w):
                dve.wait_ge(a_ready, 2 * q + w + 1)
                dve.wait_ge(mask_step_ready, q + 1)
                at_least(dve, a_lo_ready, 4 * q + 2 * w)
                for k, mask in enumerate((maskT[r][0], mask_step)):
                    nc.vector.tensor_tensor(a_masked[k][:], ps_p[:].rearrange("p (e s) -> p e s", e=ET), mask[:], ALU.mult).then_inc(masked_ready, 1)

            def glu_of(b, f, k):
                dve.wait_ge(silu_ready[k], FT * b + f + 1)
                dve.wait_ge(up_ready[k], 2 * FT * b + 2 * f + 2)
                at_least(dve, weighted[k], FT * b + f)
                nc.vector.tensor_tensor(glu[k][:], ps_x3[f % 2][:, 0:S], silu[k][:], ALU.mult).then_inc(glu_ready[k], 1)

            def split_v_lo(b, f, k):
                src = (first_w[f % 2], second_w, both_w)[k]
                dve.wait_ge(v_hi_ready[k], FT * b + f + 1)
                nc.vector.tensor_tensor(v_lo[k][f % 2][:], src[:], v_hi[k][f % 2][:].bitcast(F32), ALU.subtract).then_inc(v_lo_ready[k], 1)

            def mask_a2(b, r):
                dve.wait_ge(down_ready, FT * b + FT)
                for k in range(2):
                    nc.vector.tensor_tensor(a2_part[k][:], ps_a2[k][:].rearrange("p (e s) -> p e s", e=ET), maskT[r][k][:], ALU.mult).then_inc(a2_step, 1)
                dve.wait_ge(a2_step, 3 * b + 2)
                nc.vector.tensor_tensor(a2_part[0][:], a2_part[0][:], a2_part[1][:], ALU.add).then_inc(a2_step, 1)
                dve.wait_ge(a2_hi_ready, b + 1)
                nc.vector.tensor_tensor(a2_lo[:], a2_part[0][:], a2_hi[:].bitcast(F32), ALU.subtract).then_inc(a2_lo_ready, 1)

            def output(b, r):
                dve.wait_ge(outT_ready, b + 1)
                at_least(dve, stored, 16 * b)
                nc.vector.tensor_tensor(y_out[:].rearrange("p t c -> p (t c)"), ps_p[:], x2[r][:].rearrange("p t c -> p (t c)"), ALU.add).then_inc(y_ready, 1)

            def iteration(b, r, before, after):
                q, s = b + 1, 1 - r
                if after:
                    gate_attention(q, s)
                if before:
                    mask_a2(b - 1, s)
                glu_of(b, 0, 0)
                glu_of(b, 1, 0)
                split_v_lo(b, 0, 0)
                glu_of(b, 0, 1)
                if before:
                    output(b - 1, s)
                for f in range(2, FT):
                    split_v_lo(b, f - 2, 1)
                    split_v_lo(b, f - 2, 2)
                    if after and f == 4:
                        routing(q)
                    glu_of(b, f, 0)
                    if after and f == 2:
                        residual(q, s)
                    if after and f == 4:
                        choices(q)
                    if after and f == 6:
                        mask_a(q, s, 0)
                    split_v_lo(b, f - 1, 0)
                    glu_of(b, f - 1, 1)
                    if after and f == 2:
                        normalise(q, s)
                    if after and f == 3:
                        split_h_lo(q, s)
                    if after and f == 5:
                        step_of_masks(q, s)
                split_v_lo(b, 5, 1)
                split_v_lo(b, 5, 2)
                if after:
                    mask_a(q, s, 1)
                split_v_lo(b, 6, 0)
                glu_of(b, 6, 1)
                split_v_lo(b, 6, 1)
                split_v_lo(b, 6, 2)

            gate_attention(0, 0)
            residual(0, 0)
            normalise(0, 0)
            split_h_lo(0, 0)
            routing(0)
            choices(0)
            step_of_masks(0, 0)
            mask_a(0, 0, 0)
            mask_a(0, 0, 1)
            all_batches(dve, iteration)
            mask_a2(B - 1, 1)
            output(B - 1, 1)

        @block.gpsimd
        def _(pool):
            def inverse_deviation(q):
                pool.wait_ge(ve_ready, 4 * q + 4)
                nc.gpsimd.tensor_tensor(rstd[:], vareps[:], g.minus_half[:, 0:2], ALU.pow).then_inc(rstd_ready, 1)

            def split_a_lo(q, r, w):
                for k in range(2):
                    pool.wait_ge(a_hi_ready, 4 * q + 2 * w + k + 1)
                    nc.gpsimd.tensor_tensor(a_lo[r][w][k][:], a_masked[k][:], a_hi[r][w][k][:].bitcast(F32), ALU.subtract).then_inc(a_lo_ready, 1)

            def weigh(b, r, f, k):
                out = (first_w[f % 2], second_w)[k]
                pool.wait_ge(glu_ready[k], FT * b + f + 1)
                at_least(pool, v_lo_ready[k], FT * b + f - (1 if k == 0 else 0))
                at_least(pool, weighted[2], FT * b + f - (1 if k == 0 else 0))
                nc.gpsimd.tensor_tensor(out[:], glu[k][:], weightT[r][:, k, :], ALU.mult).then_inc(weighted[k], 1)

            def add_choices(b, f):
                pool.wait_ge(weighted[1], FT * b + f + 1)
                at_least(pool, v_lo_ready[2], FT * b + f)
                nc.gpsimd.tensor_tensor(both_w[:], first_w[f % 2][:], second_w[:], ALU.add).then_inc(weighted[2], 1)

            def iteration(b, r, before, after):
                q, s = b + 1, 1 - r
                weigh(b, r, 0, 0)
                for f in range(1, FT):
                    weigh(b, r, f, 0)
                    if after and f == 2:
                        inverse_deviation(q)
                    weigh(b, r, f - 1, 1)
                    add_choices(b, f - 1)
                    if after and f == 6:
                        split_a_lo(q, s, 0)
                weigh(b, r, FT - 1, 1)
                add_choices(b, FT - 1)
                if after:
                    split_a_lo(q, s, 1)

            inverse_deviation(0)
            split_a_lo(0, 0, 0)
            split_a_lo(0, 0, 1)
            all_batches(pool, iteration)


def adaln_attention_mixture_kernel(nc, x, w_qkv, w_o, Wg, W1, W2, W3, A1, B1, A2, B2, A3, B3, c, wmod, out):
    dram = dict(x=x, w_qkv=w_qkv, w_o=w_o, Wg=Wg, W1=W1, W2=W2, W3=W3, A1=A1, B1=B1, A2=A2, B2=B2, A3=A3, B3=B3,
                c=c, wmod=wmod, out=out, acc=nc.dram_tensor("acc_dram", [P, KT, TOK], F32, kind="Internal").ap())
    with ExitStack() as ctx:
        m = Memory(nc, ctx)
        g = shared_memory(nc, m)
        with ExitStack() as heads:
            head_memory(nc, Memory(nc, heads), g)
            setup_phase(nc, m, dram, g)
            attention_phase(nc, m, dram, g)
            store_attention(nc, dram, g)
        with ExitStack() as ffn:
            ffn_memory(nc, Memory(nc, ffn), g)
            ffn_weight_phase(nc, m, dram, g)
            ffn_phase(nc, m, dram, g)


_INS = ['L0_attn_x', 'L0_attn_w_qkv', 'L0_attn_w_o', 'L0_ffn_Wg', 'L0_ffn_W1', 'L0_ffn_W2', 'L0_ffn_W3', 'L0_ffn_A1', 'L0_ffn_B1',
        'L0_ffn_A2', 'L0_ffn_B2', 'L0_ffn_A3', 'L0_ffn_B3', 'L0_c', 'L0_wmod']
_OUTS = [((B, S, D), 'float32')]


def kernel(**inputs):
    import numpy as _np
    import concourse.bacc as _bacc
    from concourse import mybir as _mybir
    from concourse.bass_utils import run_bass_kernel_spmd as _run

    nc = _bacc.Bacc("TRN2", target_bir_lowering=False, num_devices=1)
    arrays, args = {}, []
    for name in _INS:
        a = _np.ascontiguousarray(inputs[name])
        arrays[f"in_{name}_dram"] = a
        args.append(nc.dram_tensor(f"in_{name}_dram", a.shape, _mybir.dt.from_np(a.dtype), kind="ExternalInput").ap())
    for i, (shape, dtype) in enumerate(_OUTS):
        dt = _mybir.dt.from_np(_np.dtype(dtype))
        args.append(nc.dram_tensor(f"out_{i}_dram", shape, dt, kind="ExternalOutput").ap())
    adaln_attention_mixture_kernel(nc, *args)
    r = _run(nc, [arrays], core_ids=[0])
    return r.results[0]["out_0_dram"]
```

```python
import concourse.bass as bass
from concourse import mybir
from contextlib import ExitStack
import math

F32 = mybir.dt.float32
F32R = mybir.dt.float32r
BF16 = mybir.dt.bfloat16
ALU = mybir.AluOpType
ACT = mybir.ActivationFunctionType
AX = mybir.AxisListType

P = 128
B, S, D = 16, 256, 256
HEADS, DH = 16, 128
KT = D // P
PAIRS = B // 2
STEPS = HEADS * PAIRS
PT = 2 * S
TOK = B * S
FF, EXPERTS, RANK = 896, 8, 32
FT = FF // P
ER = EXPERTS * RANK
ET = ER // P
EPS = 1e-5
SCALE = 1.0 / math.sqrt(DH)
SA, CA, GA, SB_, CB, GB = range(6)


def at_least(eng, sem, value):
    if isinstance(value, int) and value <= 0:
        return
    eng.wait_ge(sem, value)


def three_pass(nc, out, w_hi, w_lo, x_hi, x_lo, first, last, **kw):
    nc.tensor.matmul(out, w_hi, x_hi, start=first, stop=False, **kw)
    nc.tensor.matmul(out, w_hi, x_lo, start=False, stop=False, **kw)
    return nc.tensor.matmul(out, w_lo, x_hi, start=False, stop=last, **kw)


class Memory:

    def __init__(self, nc, ctx):
        self.nc, self.ctx = nc, ctx

    def sb(self, name, shape, dt=F32):
        return self.ctx.enter_context(self.nc.sbuf_tensor(name, shape, dt))

    def ps(self, name, shape=(P, 512)):
        return self.ctx.enter_context(self.nc.psum_tensor(name, list(shape), F32))

    def sem(self, name):
        return self.ctx.enter_context(self.nc.semaphore(name))


def combine_stats(nc, dve, stats, meanvar, vareps, moments, ve_ready, done):
    even_mean, odd_mean = stats[:, :, 1], stats[:, :, 4]
    nc.vector.tensor_tensor(meanvar[:, :, 0], even_mean, odd_mean, ALU.add).then_inc(moments, 1)
    nc.vector.tensor_tensor(meanvar[:, :, 1], even_mean, odd_mean, ALU.subtract).then_inc(moments, 1)
    nc.vector.tensor_tensor(vareps, stats[:, :, 2], stats[:, :, 5], ALU.add).then_inc(moments, 1)
    dve.wait_ge(moments, 3 * done + 3)
    nc.vector.tensor_scalar(meanvar[:, :, 0], meanvar[:, :, 0], 0.5, None, ALU.mult).then_inc(ve_ready, 1)
    nc.vector.tensor_scalar(vareps, vareps, 1.0 / D, EPS, ALU.mult, ALU.add).then_inc(ve_ready, 1)
    nc.vector.scalar_tensor_tensor(meanvar[:, :, 1], meanvar[:, :, 1], 0.25, meanvar[:, :, 1], ALU.mult, ALU.mult).then_inc(ve_ready, 1)
    dve.wait_ge(ve_ready, 4 * done + 3)
    nc.vector.tensor_tensor(vareps, vareps, meanvar[:, :, 1], ALU.add).then_inc(ve_ready, 1)


def setup_phase(nc, mem, dram, g):
    with ExitStack() as ctx:
        m = Memory(nc, ctx)
        c_sb = m.sb("c_sb", [B, D])
        sc = m.sb("silu_c", [B, D])
        scT = m.sb("silu_cT", [P, KT, B])
        mod_row = m.sb("mod_row", [B, 6 * D])
        gate_sign = m.sb("gate_sign", [P, 2, KT, B])
        gate_abs = m.sb("gate_abs", [P, 2, KT, B])
        stats = m.sb("ln_stats", [P, 4 * PAIRS, 6])
        meanvar = m.sb("ln_meanvar", [P, 4 * PAIRS, 2])
        vareps = m.sb("ln_vareps", [P, 4 * PAIRS])
        rstd = m.sb("ln_rstd", [P, 4 * PAIRS])
        x_all = g.accT[:].rearrange("p k n -> p (k n)").rearrange("p (t c) -> p t c", c=D)
        arena = Arena(nc, g.arena_offset, 4 * ARENA)
        h32 = arena.sb("h32", [P, KT, TOK])
        wmod = arena.sb("wmod", [P, KT, 6 * D])
        ps_small = m.ps("ps_small")
        ps_t = [[m.ps(f"ps_t{r}{k}") for k in range(KT)] for r in range(2)]
        ps_mod = [ps_t[0][0], ps_t[0][1], ps_t[1][0]]

        c_loaded, wmod_loaded = m.sem("c_loaded"), m.sem("wmod_loaded")
        x_loaded = [m.sem("x_loaded0"), m.sem("x_loaded1")]
        silu_done, cT_ready, cT_copied = m.sem("silu_done"), m.sem("cT_ready"), m.sem("cT_copied")
        mod_ready, mod_copied, modT_ready = m.sem("mod_ready"), m.sem("mod_copied"), m.sem("modT_ready")
        modT_copied, gate_step = m.sem("modT_copied"), m.sem("gate_step")
        stats_ready, moments, ve_ready = m.sem("stats_ready"), m.sem("moments"), m.sem("ve_ready")
        rstd_ready, xn_ready, xnT_ready = m.sem("rstd_ready"), m.sem("xn_ready"), m.sem("xnT_ready")
        h_ready, h_hi_ready, h_lo_ready = m.sem("h_ready"), m.sem("h_hi_ready"), m.sem("h_lo_ready")
        zero_ready = m.sem("zero_ready")

        block = ctx.enter_context(nc.Block())

        @block.sync
        def _(sp):
            xg = dram["x"].rearrange("b (t p) c -> b p t c", p=P)

            def load_pair(i, r):
                n = 2 * i + r
                for j in range(2):
                    sp.dma_start(x_all[:, bass.ds(4 * n + 2 * j, 2), :], xg[2 * n + j]).then_inc(x_loaded[r], 16)

            sp.dma_start(c_sb[:], dram["c"]).then_inc(c_loaded, 16)
            load_pair(0, 0)
            load_pair(0, 1)
            sp.dma_start(wmod[:], dram["wmod"].rearrange("(k p) n -> p k n", p=P)).then_inc(wmod_loaded, 16)
            load_head(nc, sp, dram, g, 0, 0)
            with sp.Fori(1, PAIRS // 2) as i:
                for r in range(2):
                    sp.wait_ge(stats_ready, 8 * i + (4 * r - 4))
                    load_pair(i, r)
            load_head(nc, sp, dram, g, 1, 1)

        @block.gpsimd
        def _(pool):
            nc.gpsimd.memset(g.ident[:], 0.0).then_inc(zero_ready, 1)
            pool.wait_ge(zero_ready, 1)
            nc.gpsimd.affine_select(out=g.ident[:], in_=g.ident[:], compare_op=ALU.not_equal, fill=1.0,
                                    base=0, pattern=[[-1, P]], channel_multiplier=1).then_inc(g.ident_ready, 1)
            nc.gpsimd.memset(g.minus_half[:], -0.5).then_inc(g.half_const_ready, 1)
            nc.gpsimd.memset(g.ones[:], 1.0).then_inc(g.ones_ready, 1)
            for e in range(EXPERTS):
                nc.gpsimd.memset(g.first_rank[:, :, e:e + 1], float(EXPERTS - e)).then_inc(g.rank_ready, 1)
            pool.wait_ge(g.half_const_ready, 1)
            with pool.Fori(0, PAIRS) as n:
                pool.wait_ge(ve_ready, 4 * n + 4)
                rows = bass.ds(4 * n, 4)
                nc.gpsimd.tensor_tensor(rstd[:, rows], vareps[:, rows], g.minus_half[:], ALU.pow).then_inc(rstd_ready, 1)
            split_head_weights_lo(nc, pool, g, 0, 0)
            for n in range(PAIRS):
                pool.wait_ge(xnT_ready, 2 * n + 2)
                nc.gpsimd.memset(x_all[:, 4 * n:4 * n + 4, :], 0.0).then_inc(g.acc_zeroed, 1)
            pool.wait_ge(g.acc_zeroed, PAIRS)

        @block.tensor
        def _(pe):
            def transpose_pair(n):
                r = n % 2
                pe.wait_ge(xn_ready, 4 * n + 4)
                at_least(pe, h_ready, 4 * n - 4)
                for k in range(KT):
                    for t in range(4):
                        last = nc.tensor.transpose(ps_t[r][k][:, t * P:(t + 1) * P], x_all[:, 4 * n + t, k * P:(k + 1) * P], g.ident[:])
                    last.then_inc(xnT_ready, 1)

            pe.wait_ge(g.ident_ready, 1)
            pe.wait_ge(silu_done, 1)
            for k in range(KT):
                last = nc.tensor.transpose(ps_small[:, k * B:(k + 1) * B], sc[:, k * P:(k + 1) * P], g.ident[0:B, 0:B])
            last.then_inc(cT_ready, 1)
            pe.wait_ge(cT_copied, 1)
            pe.wait_ge(wmod_loaded, 16)
            for n in range(3):
                for k in range(KT):
                    last = nc.tensor.matmul(ps_mod[n][0:B, :], scT[:, k, :], wmod[:, k, n * 512:(n + 1) * 512],
                                            start=(k == 0), stop=(k == KT - 1))
                last.then_inc(mod_ready, 1)
            transpose_head_values(nc, pe, g, 0, 0)
            pe.wait_ge(mod_copied, 3)
            for n in range(6 * KT):
                last = nc.tensor.transpose(ps_small[:, n * B:(n + 1) * B], mod_row[:, n * P:(n + 1) * P], g.ident[0:B, 0:B])
            last.then_inc(modT_ready, 1)
            transpose_pair(0)
            transpose_pair(1)
            combine_head_values(nc, pe, g, 0, 0)
            for n in range(2, PAIRS):
                transpose_pair(n)

        @block.scalar
        def _(act):
            def modulate(i, r):
                n = 2 * i + r
                for k in range(KT):
                    act.wait_ge(xnT_ready, 2 * n + k + 1)
                    for j in range(2):
                        b = 2 * n + j
                        nc.scalar.activation(h32[:, k, bass.ds(b * S, S)], ps_t[r][k][:, j * S:(j + 1) * S],
                                             ACT.Identity, scale=g.modT[:, CA, k, bass.ds(b, 1)],
                                             bias=g.modT[:, SA, k, bass.ds(b, 1)]).then_inc(h_ready, 1)
                act.wait_ge(h_ready, 4 * n + 4)
                cols = bass.ds(n * PT, PT)
                nc.scalar.copy(g.h_hi[:, :, cols], h32[:, :, cols]).then_inc(h_hi_ready, 1)

            act.wait_ge(c_loaded, 16)
            nc.scalar.activation(sc[:], c_sb[:], ACT.Silu).then_inc(silu_done, 1)
            act.wait_ge(cT_ready, 1)
            nc.scalar.copy(scT[:].rearrange("p k b -> p (k b)"), ps_small[:, 0:KT * B]).then_inc(cT_copied, 1)
            for n in range(3):
                act.wait_ge(mod_ready, n + 1)
                nc.scalar.copy(mod_row[:, n * 512:(n + 1) * 512], ps_mod[n][0:B, :]).then_inc(mod_copied, 1)
            copy_head_values(nc, act, g, 0, 0)
            split_head_weights_hi(nc, act, g, 0, 0)
            act.wait_ge(modT_ready, 1)
            modT_ps = ps_small[:, 0:6 * KT * B].rearrange("p (s n) -> p s n", s=6)
            for row in range(6):
                nc.scalar.activation(g.modT[:, row].rearrange("p k b -> p (k b)"), modT_ps[:, row], ACT.Copy,
                                     bias=1.0 if row in (CA, CB) else 0.0).then_inc(modT_copied, 1)
            act.wait_ge(modT_copied, 6)
            with act.Fori(0, PAIRS // 2) as i:
                modulate(i, 0)
                modulate(i, 1)
            split_head_values_hi(nc, act, g, 0, 0)

        @block.vector
        def _(dve):
            def statistics(i, r):
                n = 2 * i + r
                dve.wait_ge(x_loaded[r], 32 * i + 32)
                for t in range(4):
                    nc.vector.bn_stats(stats[:, 4 * n + t, :], x_all[:, 4 * n + t, :]).then_inc(stats_ready, 1)
                dve.wait_ge(stats_ready, 4 * n + 4)
                rows = bass.ds(4 * n, 4)
                combine_stats(nc, dve, stats[:, rows], meanvar[:, rows], vareps[:, rows], moments, ve_ready, n)

            def normalise(i, r):
                n = 2 * i + r
                dve.wait_ge(rstd_ready, n + 1)
                for t in range(4):
                    row = 4 * n + t
                    nc.vector.tensor_scalar(x_all[:, row, :], x_all[:, row, :], meanvar[:, row, 0:1], rstd[:, bass.ds(row, 1)],
                                            ALU.subtract, ALU.mult).then_inc(xn_ready, 1)

            statistics(0, 0)
            with dve.Fori(0, PAIRS // 2 - 1) as i:
                statistics(i, 1)
                normalise(i, 0)
                statistics(i + 1, 0)
                normalise(i, 1)
            statistics(PAIRS // 2 - 1, 1)
            normalise(PAIRS // 2 - 1, 0)
            normalise(PAIRS // 2 - 1, 1)
            dve.wait_ge(modT_copied, 6)
            for n, row in enumerate((GA, GB)):
                nc.vector.tensor_scalar(gate_sign[:, n], g.modT[:, row], 0.0, 2.0, ALU.is_ge, ALU.mult).then_inc(gate_step, 1)
                nc.vector.scalar_tensor_tensor(gate_abs[:, n], g.modT[:, row], -1.0, g.modT[:, row], ALU.mult, ALU.max).then_inc(gate_step, 1)
            dve.wait_ge(gate_step, 4)
            nc.vector.tensor_scalar(gate_abs[:], gate_abs[:], 0.25, None, ALU.max).then_inc(gate_step, 1)
            dve.wait_ge(gate_step, 5)
            for n, row in enumerate((GA, GB)):
                nc.vector.scalar_tensor_tensor(g.modT[:, row], gate_sign[:, n], -1.0, gate_abs[:, n], ALU.add, ALU.mult).then_inc(gate_step, 1)
            dve.wait_ge(g.ones_ready, 1)
            nc.vector.tensor_copy(g.ones_r[:], g.ones[:]).then_inc(g.ones_r_ready, 1)
            with dve.Fori(0, PAIRS) as n:
                dve.wait_ge(h_hi_ready, n + 1)
                cols = bass.ds(n * PT, PT)
                nc.vector.tensor_tensor(g.h_lo[:, :, cols], h32[:, :, cols], g.h_hi[:, :, cols].bitcast(F32), ALU.subtract).then_inc(h_lo_ready, 1)
            split_head_values_lo(nc, dve, g, 0, 0)
            dve.wait_ge(h_lo_ready, PAIRS)



RAW_LOADS = 16 * (KT + 1)


def load_head(nc, sp, dram, g, h, r):
    columns = dram["w_qkv"].rearrange("(k p) (t h d) -> h k p t d", p=P, t=3, h=HEADS)
    for k in range(KT):
        sp.dma_start(g.raw_qkv[:, r, k], columns[h, k]).then_inc(g.raw_loaded[r], 16)
    sp.dma_start(g.raw_o[:, r], dram["w_o"].rearrange("(h d) n -> h d n", d=DH)[h]).then_inc(g.raw_loaded[r], 16)


def raw_there(eng, g, pair_of_head, r):
    eng.wait_ge(g.raw_loaded[r], RAW_LOADS * (pair_of_head + 1))


def transpose_head_values(nc, pe, g, hp, r):
    h = 2 * hp + r
    raw_there(pe, g, hp, r)
    at_least(pe, g.m_lo_ready, h)
    for k in range(KT):
        last = nc.tensor.transpose(g.ps_head[:, k * P:(k + 1) * P], g.raw_qkv[:, r, k, 2, :], g.ident[:])
    last.then_inc(g.wvT_ready, 1)


def combine_head_values(nc, pe, g, hp, r):
    h = 2 * hp + r
    pe.wait_ge(g.wvT_copied, h + 1)
    for k in range(KT):
        last = nc.tensor.matmul(g.ps_head[:, k * D:(k + 1) * D], g.wvT[:, k * P:(k + 1) * P], g.raw_o[:, r, :], start=True, stop=True)
    last.then_inc(g.m_ready, 1)


def copy_head_values(nc, act, g, hp, r):
    act.wait_ge(g.wvT_ready, 2 * hp + r + 1)
    nc.scalar.copy(g.wvT[:], g.ps_head[:, 0:D]).then_inc(g.wvT_copied, 1)


def split_head_weights_hi(nc, act, g, hp, r):
    raw_there(act, g, hp, r)
    nc.scalar.copy(g.wqk_hi[r][:], g.raw_qkv[:, r, :, 0:2, :]).then_inc(g.wqk_hi_ready, 1)


def split_head_weights_lo(nc, pool, g, hp, r):
    pool.wait_ge(g.wqk_hi_ready, 2 * hp + r + 1)
    nc.gpsimd.tensor_tensor(g.wqk_lo[r][:], g.raw_qkv[:, r, :, 0:2, :], g.wqk_hi[r][:].bitcast(F32), ALU.subtract).then_inc(g.wqk_lo_ready, 1)


def split_head_values_hi(nc, act, g, hp, r):
    act.wait_ge(g.m_ready, 2 * hp + r + 1)
    nc.scalar.copy(g.m_hi[r][:].rearrange("p k n -> p (k n)"), g.ps_head[:]).then_inc(g.m_hi_ready, 1)


def split_head_values_lo(nc, dve, g, hp, r):
    dve.wait_ge(g.m_hi_ready, 2 * hp + r + 1)
    nc.vector.tensor_tensor(g.m_lo[r][:].rearrange("p k n -> p (k n)"), g.ps_head[:],
                            g.m_hi[r][:].rearrange("p k n -> p (k n)").bitcast(F32), ALU.subtract).then_inc(g.m_lo_ready, 1)


def attention_phase(nc, mem, dram, g):
    with ExitStack() as ctx:
        m = Memory(nc, ctx)
        q32 = m.sb("q32", [P, PT])
        q_hi, q_lo = m.sb("q_hi", [P, PT], F32R), m.sb("q_lo", [P, PT], F32R)
        k_hi, k_lo = m.sb("k_hi", [P, PT], F32R), m.sb("k_lo", [P, PT], F32R)
        negmax, rowsum, rinv = m.sb("negmax", [P, 4]), m.sb("rowsum", [P, 4]), m.sb("rinv", [P, 4])
        probs = m.sb("probs", [P, 2, 2, S])
        half = m.sb("half_sum", [P, 2, S])
        wsum = m.sb("wsum", [P, 2, S])
        wsum_hi, wsum_lo = m.sb("wsum_hi", [P, PT], F32R), m.sb("wsum_lo", [P, PT], F32R)
        colsum = m.sb("colsum", [P, PT])
        prod = m.sb("prod", [P, KT, PT])
        ps_q, ps_k = m.ps("ps_q"), m.ps("ps_k")
        ps_s = [m.ps("ps_s0"), m.ps("ps_s1")]
        ps_y = [m.ps("ps_y0"), m.ps("ps_y1")]
        ps_c = m.ps("ps_c")

        proj_ready = m.sem("proj_ready")
        qk_hi_ready = m.sem("qk_hi_ready")
        q32_ready = m.sem("q32_ready")
        q_lo_ready = m.sem("q_lo_ready")
        k_lo_ready = m.sem("k_lo_ready")
        scores_ready = m.sem("scores_ready")
        negmax_ready = m.sem("negmax_ready")
        probs_ready = m.sem("probs_ready")
        rinv_ready = m.sem("rinv_ready")
        half_ready = m.sem("half_ready")
        wsum_ready = m.sem("wsum_ready")
        wsum_hi_ready = m.sem("wsum_hi_ready")
        wsum_lo_ready = m.sem("wsum_lo_ready")
        y_ready = m.sem("y_ready")
        c_ready = m.sem("c_ready")
        c_copied = m.sem("c_copied")
        prod_ready = m.sem("prod_ready")
        acc_added = m.sem("acc_added")
        acc_stored = m.sem("acc_stored")

        def run_heads(eng, head):
            head(0, 0, True, False)
            head(0, 1, False, False)
            with eng.Fori(1, HEADS // 2 - 1) as hp:
                head(hp, 0, False, False)
                head(hp, 1, False, False)
            head(HEADS // 2 - 1, 0, False, False)
            head(HEADS // 2 - 1, 1, False, True)

        def run_inner_pairs(eng, step, h):
            with eng.Fori(0, PAIRS // 2 - 1) as i:
                for j in (1, 2):
                    step(PAIRS * h + 2 * i + j, 2 * i + j)

        block = ctx.enter_context(nc.Block())

        @block.sync
        def _(sp):
            load_ffn_weights(nc, sp, dram, g)
            with sp.Fori(0, HEADS // 2 - 1) as i:
                for r in range(2):
                    done = 2 * i + r + 1
                    sp.wait_ge(g.m_ready, done)
                    sp.wait_ge(g.wqk_hi_ready, done)
                    sp.wait_ge(g.wqk_lo_ready, done)
                    load_head(nc, sp, dram, g, 2 * i + (2 + r), r)
            for p in range(PAIRS):
                sp.wait_ge(acc_added, 2 * (8 * (HEADS - 1) + p) + 2)
                sp.dma_start(dram["acc"][:, :, p * PT:(p + 1) * PT], g.accT[:, :, p * PT:(p + 1) * PT]).then_inc(acc_stored, 16)
            sp.wait_ge(acc_stored, 16 * PAIRS)

        @block.tensor
        def _(pe):
            def project(n, pair, r, k_wqk):
                at_least(pe, g.wqk_hi_ready, k_wqk)
                at_least(pe, g.wqk_lo_ready, k_wqk)
                for t, ps in enumerate((ps_q, ps_k)):
                    for k in range(KT):
                        cols = bass.ds(pair * PT, PT)
                        last = three_pass(nc, ps[:], g.wqk_hi[r][:, k, t, :], g.wqk_lo[r][:, k, t, :],
                                          g.h_hi[:, k, cols], g.h_lo[:, k, cols], k == 0, k == KT - 1)
                    last.then_inc(proj_ready, 1)

            def column_sums(n):
                pe.wait_ge(wsum_hi_ready, n + 1)
                pe.wait_ge(wsum_lo_ready, n + 1)
                at_least(pe, c_copied, n)
                nc.tensor.matmul(ps_c[:], g.ones_r[:], wsum_hi[:], start=True, stop=False)
                nc.tensor.matmul(ps_c[:], g.ones_r[:], wsum_lo[:], start=False, stop=True).then_inc(c_ready, 1)

            def step(n, pair, before, r, follow, m_needed=None):
                pe.wait_ge(qk_hi_ready, 2 * n + 2)
                pe.wait_ge(q_lo_ready, n + 1)
                pe.wait_ge(k_lo_ready, n + 1)
                at_least(pe, probs_ready, 4 * n)
                for j in range(2):
                    keys = slice(j * S, (j + 1) * S)
                    for qt in range(2):
                        qs = slice(j * S + qt * P, j * S + (qt + 1) * P)
                        last = three_pass(nc, ps_s[j][:, qt * S:(qt + 1) * S], q_hi[:, qs], q_lo[:, qs], k_hi[:, keys], k_lo[:, keys], True, True)
                    last.then_inc(scores_ready, 1)
                if before:
                    column_sums(n - 1)
                if follow:
                    project(*follow)
                if m_needed is not None:
                    pe.wait_ge(g.m_hi_ready, m_needed)
                    pe.wait_ge(g.m_lo_ready, m_needed)
                at_least(pe, prod_ready, 2 * n)
                for o in range(KT):
                    for k in range(KT):
                        cols = bass.ds(pair * PT, PT)
                        last = three_pass(nc, ps_y[o][:], g.m_hi[r][:, k, o * P:(o + 1) * P], g.m_lo[r][:, k, o * P:(o + 1) * P],
                                          g.h_hi[:, k, cols], g.h_lo[:, k, cols], k == 0, k == KT - 1)
                    last.then_inc(y_ready, 1)

            def head(hp, r, first, final):
                h = 2 * hp + r
                nhp, nr = (hp, 1) if r == 0 else (hp + 1, 0)
                step(8 * h, 0, not first, r, (8 * h + 1, 1, r, 0), h + 1)
                if not final:
                    transpose_head_values(nc, pe, g, nhp, nr)
                run_inner_pairs(pe, lambda n, p: step(n, p, True, r, (n + 1, p + 1, r, 0)), h)
                if not final:
                    combine_head_values(nc, pe, g, nhp, nr)
                n = 8 * h + 7
                step(n, PAIRS - 1, True, r, None if final else (n + 1, 0, nr, h + 2))

            pe.wait_ge(g.ones_r_ready, 1)
            project(0, 0, 0, 1)
            run_heads(pe, head)
            column_sums(STEPS - 1)

        @block.scalar
        def _(act):
            def split_hi(n):
                act.wait_ge(proj_ready, 2 * n + 1)
                nc.scalar.activation(q32[:], ps_q[:], ACT.Copy, scale=SCALE).then_inc(q32_ready, 1)
                nc.scalar.activation(q_hi[:], ps_q[:], ACT.Copy, scale=SCALE).then_inc(qk_hi_ready, 1)
                act.wait_ge(proj_ready, 2 * n + 2)
                nc.scalar.copy(k_hi[:], ps_k[:]).then_inc(qk_hi_ready, 1)

            def copy_column_sums(n):
                act.wait_ge(c_ready, n + 1)
                at_least(act, prod_ready, 2 * n)
                nc.scalar.copy(colsum[:], ps_c[:]).then_inc(c_copied, 1)

            def step(n, pair, before, follow):
                at_least(act, wsum_ready, 2 * n)
                for j in range(2):
                    act.wait_ge(negmax_ready, 2 * n + j + 1)
                    for qt in range(2):
                        i = 2 * j + qt
                        if before and i == 1:
                            copy_column_sums(n - 1)
                        nc.scalar.activation(probs[:, j, qt, :], ps_s[j][:, qt * S:(qt + 1) * S], ACT.Exp,
                                             bias=negmax[:, i:i + 1], accum_out=rowsum[:, i:i + 1]).then_inc(probs_ready, 1)
                if follow:
                    split_hi(n + 1)
                act.wait_ge(wsum_ready, 2 * n + 2)
                at_least(act, c_ready, n)
                nc.scalar.copy(wsum_hi[:], wsum[:].rearrange("p j s -> p (j s)")).then_inc(wsum_hi_ready, 1)

            def head(hp, r, first, final):
                h = 2 * hp + r
                nhp, nr = (hp, 1) if r == 0 else (hp + 1, 0)
                step(8 * h, 0, not first, True)
                if not final:
                    at_least(act, y_ready, 16 * h)
                    copy_head_values(nc, act, g, nhp, nr)
                    split_head_weights_hi(nc, act, g, nhp, nr)
                run_inner_pairs(act, lambda n, p: step(n, p, True, True), h)
                if not final:
                    split_head_values_hi(nc, act, g, nhp, nr)
                step(8 * h + 7, PAIRS - 1, True, not final)

            split_hi(0)
            run_heads(act, head)
            copy_column_sums(STEPS - 1)

        @block.vector
        def _(dve):
            def split_k_lo(n):
                dve.wait_ge(qk_hi_ready, 2 * n + 2)
                nc.vector.tensor_tensor(k_lo[:], ps_k[:], k_hi[:].bitcast(F32), ALU.subtract).then_inc(k_lo_ready, 1)

            def maxima(n):
                for j in range(2):
                    dve.wait_ge(scores_ready, 2 * n + j + 1)
                    nc.vector.tensor_reduce(negmax[:, 2 * j:2 * j + 2], ps_s[j][:].rearrange("p (q s) -> p q s", q=2),
                                            AX.X, ALU.max, negate=True).then_inc(negmax_ready, 1)

            def weigh_rows(n):
                dve.wait_ge(probs_ready, 4 * n + 4)
                nc.vector.reciprocal(rinv[:], rowsum[:]).then_inc(rinv_ready, 1)
                dve.wait_ge(rinv_ready, n + 1)
                for j in range(2):
                    nc.vector.tensor_scalar(half[:, j, :], probs[:, j, 0, :], rinv[:, 2 * j:2 * j + 1], None, ALU.mult).then_inc(half_ready, 1)
                at_least(dve, wsum_lo_ready, n)
                for j in range(2):
                    dve.wait_ge(half_ready, 2 * n + j + 1)
                    nc.vector.scalar_tensor_tensor(wsum[:, j, :], probs[:, j, 1, :], rinv[:, 2 * j + 1:2 * j + 2], half[:, j, :],
                                                   ALU.mult, ALU.add).then_inc(wsum_ready, 1)

            def products(n):
                dve.wait_ge(c_copied, n + 1)
                at_least(dve, acc_added, 2 * n)
                for o in range(KT):
                    nc.vector.tensor_tensor(prod[:, o, :], ps_y[o][:], colsum[:], ALU.mult).then_inc(prod_ready, 1)

            def step(n, pair, before, follow):
                maxima(n)
                if before:
                    products(n - 1)
                weigh_rows(n)
                if follow:
                    split_k_lo(n + 1)

            def head(hp, r, first, final):
                h = 2 * hp + r
                nhp, nr = (hp, 1) if r == 0 else (hp + 1, 0)
                step(8 * h, 0, not first, True)
                run_inner_pairs(dve, lambda n, p: step(n, p, True, True), h)
                step(8 * h + 7, PAIRS - 1, True, not final)
                if not final:
                    split_head_values_lo(nc, dve, g, nhp, nr)

            split_k_lo(0)
            run_heads(dve, head)
            products(STEPS - 1)

        @block.gpsimd
        def _(pool):
            def split_q_lo(n):
                pool.wait_ge(q32_ready, n + 1)
                pool.wait_ge(qk_hi_ready, 2 * n + 1)
                nc.gpsimd.tensor_tensor(q_lo[:], q32[:], q_hi[:].bitcast(F32), ALU.subtract).then_inc(q_lo_ready, 1)

            def add_products(n, pair, o):
                pool.wait_ge(prod_ready, 2 * n + o + 1)
                cols = g.accT[:, o, bass.ds(pair * PT, PT)]
                nc.gpsimd.tensor_tensor(cols, cols, prod[:, o, :], ALU.add).then_inc(acc_added, 1)

            def step(n, before, pair_before, follow):
                if before:
                    add_products(n - 1, pair_before, 0)
                if follow:
                    split_q_lo(n + 1)
                pool.wait_ge(wsum_hi_ready, n + 1)
                nc.gpsimd.tensor_tensor(wsum_lo[:], wsum[:].rearrange("p j s -> p (j s)"), wsum_hi[:].bitcast(F32), ALU.subtract).then_inc(wsum_lo_ready, 1)
                if before:
                    add_products(n - 1, pair_before, 1)

            def head(hp, r, first, final):
                h = 2 * hp + r
                nhp, nr = (hp, 1) if r == 0 else (hp + 1, 0)
                at_least(pool, acc_added, 16 * h - 2)
                step(8 * h, not first, PAIRS - 1, True)
                if not final:
                    split_head_weights_lo(nc, pool, g, nhp, nr)
                run_inner_pairs(pool, lambda n, p: step(n, True, p - 1, True), h)
                step(8 * h + 7, True, PAIRS - 2, not final)

            pool.wait_ge(g.acc_zeroed, PAIRS)
            split_q_lo(0)
            run_heads(pool, head)
            for o in range(KT):
                add_products(STEPS - 1, PAIRS - 1, o)
            pool.wait_ge(acc_added, 2 * STEPS)


class Shared:
    pass


def shared_memory(nc, m):
    g = Shared()
    g.ident = m.sb("ident", [P, P])
    g.ones = m.sb("ones", [P, P])
    g.ones_r = m.sb("ones_r", [P, P], F32R)
    g.minus_half = m.sb("minus_half", [P, 4])
    g.first_rank = m.sb("first_rank", [P, 2, EXPERTS])
    g.modT = m.sb("modT", [P, 6, KT, B])
    g.ident_ready, g.ones_ready, g.ones_r_ready = m.sem("ident_ready"), m.sem("ones_ready"), m.sem("ones_r_ready")
    g.half_const_ready, g.rank_ready = m.sem("half_const_ready"), m.sem("rank_ready")
    g.ffn_raw_loaded = m.sem("ffn_raw_loaded")
    g.raw_wg = m.sb("raw_wg", [EXPERTS, D])
    g.arena_offset = nc.sbuf_base
    g.arena = m.sb("arena", [P, ARENA])
    return g


def head_memory(nc, m, g):
    g.accT = m.sb("accT", [P, KT, TOK])
    g.h_hi, g.h_lo = m.sb("h_hi", [P, KT, TOK], F32R), m.sb("h_lo", [P, KT, TOK], F32R)
    g.raw_qkv = m.sb("raw_qkv", [P, 2, KT, 3, DH])
    g.raw_o = m.sb("raw_o", [P, 2, D])
    g.wvT = m.sb("wvT", [P, D])
    g.wqk_hi = [m.sb(f"wqk_hi{r}", [P, KT, 2, DH], F32R) for r in range(2)]
    g.wqk_lo = [m.sb(f"wqk_lo{r}", [P, KT, 2, DH], F32R) for r in range(2)]
    g.m_hi = [m.sb(f"m_hi{r}", [P, KT, D], F32R) for r in range(2)]
    g.m_lo = [m.sb(f"m_lo{r}", [P, KT, D], F32R) for r in range(2)]
    g.ps_head = m.ps("ps_head")
    g.raw_loaded = [m.sem("raw_loaded0"), m.sem("raw_loaded1")]
    g.wvT_ready, g.wvT_copied = m.sem("wvT_ready"), m.sem("wvT_copied")
    g.wqk_hi_ready, g.wqk_lo_ready = m.sem("wqk_hi_ready"), m.sem("wqk_lo_ready")
    g.m_ready, g.m_hi_ready, g.m_lo_ready = m.sem("m_ready"), m.sem("m_hi_ready"), m.sem("m_lo_ready")
    g.acc_zeroed = m.sem("acc_zeroed")


def ffn_memory(nc, m, g):
    shapes = dict(A1=(KT, ER), A3=(KT, ER), W1=(KT, FF), W3=(KT, FF), B1=(ET, FF), B3=(ET, FF), W2=(FT, D), A2=(FT, ER), B2=(ET, D))
    g.wgT = m.sb("wgT", [P, KT, EXPERTS])
    g.w_hi = {name: m.sb(f"{name}T_hi", [P, *shape], F32R) for name, shape in shapes.items()}
    g.w_lo = {name: m.sb(f"{name}T_lo", [P, *shape], F32R) for name, shape in shapes.items()}




ARENA = 12288


class Arena:

    def __init__(self, nc, base, size):
        self.nc, self.at, self.end = nc, base, base + size

    def sb(self, name, shape, dt=F32):
        size = math.prod(shape[1:]) * (2 if dt == BF16 else 4)
        assert self.at + size <= self.end, name
        t = self.nc.alloc_sbuf_tensor_at(name, shape, dt, offset=self.at)
        self.at += size
        return t


def raw_weights(g):
    shapes = dict(A1=(ET, D), A3=(ET, D), W1=(FT, D), W3=(FT, D), B1=(FT, ER), B3=(FT, ER),
                  W2=(KT, FF), A2=(ET, FF), B2=(KT, ER))
    at, views = 0, {}
    for name, (tiles, n) in shapes.items():
        views[name] = g.arena[:, at:at + tiles * n].rearrange("p (t n) -> p t n", t=tiles)
        at += tiles * n
    assert at <= ARENA
    return views


def load_ffn_weights(nc, sp, dram, g):
    raw = raw_weights(g)
    for name in ("W1", "W3", "W2"):
        sp.dma_start(raw[name], dram[name].rearrange("(t p) n -> p t n", p=P)).then_inc(g.ffn_raw_loaded, 16)
    for name in ("A1", "A3", "A2"):
        sp.dma_start(raw[name], dram[name].rearrange("e r n -> (e r) n").rearrange("(t p) n -> p t n", p=P)).then_inc(g.ffn_raw_loaded, 16)
    for name, tiles in (("B1", FT), ("B3", FT), ("B2", KT)):
        src = dram[name].rearrange("e (t p) r -> t p e r", p=P)
        for t in range(tiles):
            sp.dma_start(raw[name][:, t].rearrange("p (e r) -> p e r", e=EXPERTS), src[t]).then_inc(g.ffn_raw_loaded, 16)
    sp.dma_start(g.raw_wg[:], dram["Wg"]).then_inc(g.ffn_raw_loaded, 16)


FFN_LOADS = 16 * (6 + 2 * FT + KT + 1)


def ffn_weight_phase(nc, mem, dram, g):
    with ExitStack() as ctx:
        m = Memory(nc, ctx)
        banks = [m.ps(f"ps_w{i}") for i in range(4)]
        ps_wg = m.ps("ps_wg")
        w_transposed, w_hi_ready, w_lo_ready = m.sem("w_transposed"), m.sem("w_hi_ready"), m.sem("w_lo_ready")
        wg_ready, wg_copied = m.sem("wg_ready"), m.sem("wg_copied")
        raw = raw_weights(g)
        groups = []
        for name in ("A1", "A3", "W1", "W3", "B1", "B3", "W2", "A2", "B2"):
            tiles = raw[name].shape[1]
            blocks = [(outer, inner) for outer in range(raw[name].shape[2] // P) for inner in range(tiles)]
            for at in range(0, len(blocks), 4):
                part = blocks[at:at + 4]
                groups.append((name, at * P, part))

        block = ctx.enter_context(nc.Block())

        def flat(t):
            return t[:].rearrange("p a b -> p (a b)")

        @block.tensor
        def _(pe):
            pe.wait_ge(g.ffn_raw_loaded, FFN_LOADS)
            for k in range(KT):
                last = nc.tensor.transpose(ps_wg[:, k * EXPERTS:(k + 1) * EXPERTS], g.raw_wg[:, k * P:(k + 1) * P], g.ident[0:EXPERTS, 0:EXPERTS])
            last.then_inc(wg_ready, 1)
            for n, (name, at, part) in enumerate(groups):
                at_least(pe, w_lo_ready, n - 3)
                for i, (outer, inner) in enumerate(part):
                    last = nc.tensor.transpose(banks[n % 4][:, i * P:(i + 1) * P], raw[name][:, inner, outer * P:(outer + 1) * P], g.ident[:])
                last.then_inc(w_transposed, 1)

        @block.scalar
        def _(act):
            act.wait_ge(wg_ready, 1)
            nc.scalar.copy(g.wgT[:].rearrange("p k e -> p (k e)"), ps_wg[:, 0:KT * EXPERTS]).then_inc(wg_copied, 1)
            for n, (name, at, part) in enumerate(groups):
                act.wait_ge(w_transposed, n + 1)
                size = len(part) * P
                nc.scalar.copy(flat(g.w_hi[name])[:, at:at + size], banks[n % 4][:, 0:size]).then_inc(w_hi_ready, 1)
            act.wait_ge(wg_copied, 1)

        @block.vector
        def _(dve):
            for n, (name, at, part) in enumerate(groups):
                dve.wait_ge(w_hi_ready, n + 1)
                size = len(part) * P
                nc.vector.tensor_tensor(flat(g.w_lo[name])[:, at:at + size], banks[n % 4][:, 0:size],
                                        flat(g.w_hi[name])[:, at:at + size].bitcast(F32), ALU.subtract).then_inc(w_lo_ready, 1)
            dve.wait_ge(w_lo_ready, len(groups))


ROUTE = 17


def ffn_phase(nc, mem, dram, g):
    with ExitStack() as ctx:
        m = Memory(nc, ctx)
        arena = Arena(nc, g.arena_offset, 4 * ARENA)
        sb = arena.sb
        x_in = [sb(f"x_in2_{r}", [P, 2, D]) for r in range(2)]
        acc_in = [sb(f"acc_in{r}", [P, KT, S]) for r in range(2)]
        x2 = [sb(f"x2_{r}", [P, 2, D]) for r in range(2)]
        gated = sb("gated", [P, KT, S])
        xn = gated[:]
        h32 = sb("h32_2", [P, KT, S])
        chosen = sb("chosen_by_rank", [P, 2, 2, ER])
        maskT = [[sb(f"maskT{r}{k}", [P, ET, S], BF16) for k in range(2)] for r in range(2)]
        mask_step = sb("mask_step", [P, ET, S], BF16)
        weightT = [sb(f"weightT{r}", [P, 2, S]) for r in range(2)]
        a_masked = [sb(f"a_masked{i}", [P, ET, S]) for i in range(2)]
        silu = [sb(f"silu{k}", [P, S]) for k in range(2)]
        glu = [sb(f"glu{k}", [P, S]) for k in range(2)]
        first_w = [sb(f"first_weighted{i}", [P, S]) for i in range(2)]
        second_w = sb("second_weighted", [P, S])
        both_w = sb("both_weighted", [P, S])
        a2_part = [sb(f"a2_part{k}", [P, ET, S]) for k in range(2)]
        out_gated = sb("out_gated", [P, KT, S])
        y_out = m.sb("y_out", [P, 2, D])
        stats, meanvar = m.sb("ln2_stats", [P, 2, 6]), m.sb("ln2_meanvar", [P, 2, 2])
        vareps, rstd = m.sb("ln2_vareps", [P, 2]), m.sb("ln2_rstd", [P, 2])
        logits, rest = m.sb("logits", [P, 2, EXPERTS]), m.sb("logits_rest", [P, 2, EXPERTS])
        equal = [m.sb(f"equal{k}", [P, 2, EXPERTS]) for k in range(2)]
        ranked = [m.sb(f"ranked{k}", [P, 2, EXPERTS]) for k in range(2)]
        onehot = [m.sb(f"onehot{k}", [P, 2, EXPERTS]) for k in range(2)]
        top = [m.sb(f"top{k}", [P, 2]) for k in range(2)]
        best = [m.sb(f"best_rank{k}", [P, 2]) for k in range(2)]
        gap, tanh_gap, weight = m.sb("gap", [P, 2]), m.sb("tanh_gap", [P, 2]), m.sb("weight", [P, 2, 2])
        h_hi = [m.sb(f"h2_hi{r}", [P, KT, S], F32R) for r in range(2)]
        h_lo = [m.sb(f"h2_lo{r}", [P, KT, S], F32R) for r in range(2)]
        a_hi = [[[m.sb(f"a_hi{r}{w}{k}", [P, ET, S], F32R) for k in range(2)] for w in range(2)] for r in range(2)]
        a_lo = [[[m.sb(f"a_lo{r}{w}{k}", [P, ET, S], F32R) for k in range(2)] for w in range(2)] for r in range(2)]
        v_hi = [[m.sb(f"v_hi{k}{i}", [P, S], F32R) for i in range(2)] for k in range(3)]
        v_lo = [[m.sb(f"v_lo{k}{i}", [P, S], F32R) for i in range(2)] for k in range(3)]
        a2_hi, a2_lo = m.sb("a2_hi", [P, ET, S], F32R), m.sb("a2_lo", [P, ET, S], F32R)

        ps_x1 = [m.ps(f"ps_x1_{i}") for i in range(2)]
        ps_x3 = [m.ps(f"ps_x3_{i}") for i in range(2)]
        ps_out = m.ps("ps_out")
        ps_a2 = [m.ps(f"ps_a2_{k}") for k in range(2)]
        ps_p = m.ps("ps_prep")

        inputs_loaded = [m.sem("inputs_loaded0"), m.sem("inputs_loaded1")]
        gated_ready = m.sem("gated_ready")
        gatedT_ready = m.sem("gatedT_ready")
        x2_ready = m.sem("x2_ready")
        stats_ready, moments, ve_ready = m.sem("stats2_ready"), m.sem("moments2"), m.sem("ve2_ready")
        rstd_ready = m.sem("rstd2_ready")
        xn_ready = m.sem("xn2_ready")
        xnT_ready = m.sem("xn2T_ready")
        h32_ready = m.sem("h2_ready")
        h_hi_ready, h_lo_ready = m.sem("h2_hi_ready"), m.sem("h2_lo_ready")
        logits_ready = m.sem("logits_ready")
        route = m.sem("route")
        tanh_ready = m.sem("tanh_ready")
        mask_ready, maskT_ready = m.sem("mask_transposed"), m.sem("maskT_ready")
        mask_step_ready = m.sem("mask_step_ready")
        weight_ready, weightT_ready = m.sem("weight_transposed"), m.sem("weightT_ready")
        a_ready = m.sem("a_ready")
        masked_ready = m.sem("masked_ready")
        a_hi_ready, a_lo_ready = m.sem("a_hi_ready"), m.sem("a_lo_ready")
        up_ready = [m.sem("up_first_ready"), m.sem("up_second_ready")]
        silu_ready = [m.sem("silu_first_ready"), m.sem("silu_second_ready")]
        glu_ready = [m.sem("glu_first_ready"), m.sem("glu_second_ready")]
        weighted = [m.sem("weighted_first"), m.sem("weighted_second"), m.sem("weighted_both")]
        v_hi_ready = [m.sem(f"v_hi_ready{k}") for k in range(3)]
        v_lo_ready = [m.sem(f"v_lo_ready{k}") for k in range(3)]
        down_ready = m.sem("down_ready")
        a2_step = m.sem("a2_step")
        a2_hi_ready, a2_lo_ready = m.sem("a2_hi_ready"), m.sem("a2_lo_ready")
        out_ready = m.sem("out_ready")
        out_gated_ready = m.sem("out_gated_ready")
        outT_ready = m.sem("outT_ready")
        y_ready = m.sem("y_ready2")
        x2_kept = m.sem("x2_kept")
        stored = m.sem("stored")

        xg = dram["x"].rearrange("b (t p) c -> b p t c", p=P)
        og = dram["out"].rearrange("b (t p) c -> b p t c", p=P)
        accg = dram["acc"].rearrange("p k (b s) -> b p k s", s=S)

        block = ctx.enter_context(nc.Block())

        @block.sync
        def _(sp):
            def load(b, r):
                sp.dma_start(x_in[r][:], xg[b]).then_inc(inputs_loaded[r], 16)
                sp.dma_start(acc_in[r][:], accg[b]).then_inc(inputs_loaded[r], 16)

            def iteration(b, r, more):
                if more:
                    sp.wait_ge(x2_ready, b + 1)
                    load(b + 2, r)
                sp.wait_ge(y_ready, b + 1)
                sp.dma_start(og[b], y_out[:]).then_inc(stored, 16)

            load(0, 0)
            load(1, 1)
            with sp.Fori(0, B // 2 - 1) as i:
                for r in range(2):
                    iteration(2 * i + r, r, True)
            for r in range(2):
                iteration(B - 2 + r, r, False)
            sp.wait_ge(stored, 16 * B)

        def all_batches(eng, iteration):
            iteration(0, 0, False, True)
            iteration(1, 1, True, True)
            with eng.Fori(1, B // 2 - 1) as i:
                iteration(2 * i, 0, True, True)
                iteration(2 * i + 1, 1, True, True)
            iteration(B - 2, 0, True, True)
            iteration(B - 1, 1, True, False)

        @block.tensor
        def _(pe):
            def transpose_gated(q, r):
                pe.wait_ge(gated_ready, 2 * q + 2)
                at_least(pe, masked_ready, 4 * q)
                for t in range(2):
                    for k in range(KT):
                        last = nc.tensor.transpose(ps_p[:, t * D + k * P:t * D + (k + 1) * P], gated[:, k, t * P:(t + 1) * P], g.ident[:])
                last.then_inc(gatedT_ready, 1)

            def transpose_normalised(q, r):
                pe.wait_ge(xn_ready, 2 * q + 2)
                for k in range(KT):
                    for t in range(2):
                        last = nc.tensor.transpose(ps_p[:, k * S + t * P:k * S + (t + 1) * P], xn[:, t, k * P:(k + 1) * P], g.ident[:])
                last.then_inc(xnT_ready, 1)

            def router(q, r, before):
                pe.wait_ge(h32_ready, 2 * q + 2)
                if before:
                    pe.wait_ge(y_ready, q - 1)
                for t in range(2):
                    for k in range(KT):
                        last = nc.tensor.matmul(ps_p[:, t * EXPERTS:(t + 1) * EXPERTS], h32[:, k, t * P:(t + 1) * P], g.wgT[:, k, :],
                                                start=(k == 0), stop=(k == KT - 1))
                last.then_inc(logits_ready, 1)

            def transpose_masks(q, choice):
                pe.wait_ge(route, ROUTE * q + ROUTE)
                if choice == 1:
                    pe.wait_ge(maskT_ready, 2 * q + 1)
                for e in range(ET):
                    for t in range(2):
                        last = nc.tensor.transpose(ps_p[:, e * S + t * P:e * S + (t + 1) * P], chosen[:, t, choice, e * P:(e + 1) * P], g.ident[:])
                last.then_inc(mask_ready, 1)

            def transpose_weights(q):
                pe.wait_ge(maskT_ready, 2 * q + 2)
                for k in range(2):
                    for t in range(2):
                        last = nc.tensor.transpose(ps_p[:, k * S + t * P:k * S + (t + 1) * P], weight[:, t, k:k + 1].broadcast_to([P, P]), g.ident[:])
                last.then_inc(weight_ready, 1)

            def lora_a(q, r, w):
                if w == 0:
                    pe.wait_ge(weightT_ready, q + 1)
                    pe.wait_ge(h_hi_ready, q + 1)
                    pe.wait_ge(h_lo_ready, q + 1)
                else:
                    pe.wait_ge(masked_ready, 4 * q + 2)
                hi, lo = g.w_hi[("A1", "A3")[w]], g.w_lo[("A1", "A3")[w]]
                for e in range(ET):
                    for k in range(KT):
                        cols = slice(e * P, (e + 1) * P)
                        last = three_pass(nc, ps_p[:, e * S:(e + 1) * S], hi[:, k, cols], lo[:, k, cols], h_hi[r][:, k, :], h_lo[r][:, k, :], k == 0, k == KT - 1)
                last.then_inc(a_ready, 1)

            def up_first(b, r, f):
                at_least(pe, glu_ready[1], FT * b + f - 1)
                if f == 0:
                    pe.wait_ge(h_hi_ready, b + 1)
                    pe.wait_ge(h_lo_ready, b + 1)
                    pe.wait_ge(a_hi_ready, 4 * b + 4)
                    pe.wait_ge(a_lo_ready, 4 * b + 4)
                cols = slice(f * P, (f + 1) * P)
                for w, ps in enumerate((ps_x1[(f + r) % 2], ps_x3[(f + r) % 2])):
                    base, lora = ("W1", "W3")[w], ("B1", "B3")[w]
                    for k in range(KT):
                        three_pass(nc, ps[:, 0:S], g.w_hi[base][:, k, cols], g.w_lo[base][:, k, cols], h_hi[r][:, k, :], h_lo[r][:, k, :],
                                   k == 0, False, skip_group_check=True)
                    for e in range(ET):
                        last = three_pass(nc, ps[:, 0:S], g.w_hi[lora][:, e, cols], g.w_lo[lora][:, e, cols], a_hi[r][w][0][:, e, :], a_lo[r][w][0][:, e, :],
                                          False, e == ET - 1, skip_group_check=True)
                    last.then_inc(up_ready[0], 1)

            def up_second(b, r, f):
                pe.wait_ge(glu_ready[0], FT * b + f + 1)
                cols = slice(f * P, (f + 1) * P)
                for w, ps in enumerate((ps_x1[(f + r) % 2], ps_x3[(f + r) % 2])):
                    lora = ("B1", "B3")[w]
                    for e in range(ET):
                        last = three_pass(nc, ps[:, 0:S], g.w_hi[lora][:, e, cols], g.w_lo[lora][:, e, cols], a_hi[r][w][1][:, e, :], a_lo[r][w][1][:, e, :],
                                          False, e == ET - 1, skip_group_check=True)
                    last.then_inc(up_ready[1], 1)

            def down(b, r, f):
                if f == 0:
                    at_least(pe, out_gated_ready, 2 * b)
                    at_least(pe, a2_step, 3 * b)
                i = (f + r) % 2
                for k in range(2):
                    pe.wait_ge(v_hi_ready[k], FT * b + f + 1)
                    pe.wait_ge(v_lo_ready[k], FT * b + f + 1)
                    for e in range(ET):
                        cols = slice(e * P, (e + 1) * P)
                        three_pass(nc, ps_a2[k][:, e * S:(e + 1) * S], g.w_hi["A2"][:, f, cols], g.w_lo["A2"][:, f, cols], v_hi[k][i][:], v_lo[k][i][:],
                                   f == 0 and e == 0, f == FT - 1, skip_group_check=True)
                pe.wait_ge(v_hi_ready[2], FT * b + f + 1)
                pe.wait_ge(v_lo_ready[2], FT * b + f + 1)
                for o in range(KT):
                    cols = slice(o * P, (o + 1) * P)
                    last = three_pass(nc, ps_out[:, o * S:(o + 1) * S], g.w_hi["W2"][:, f, cols], g.w_lo["W2"][:, f, cols], v_hi[2][i][:], v_lo[2][i][:],
                                      f == 0 and o == 0, False, skip_group_check=True)
                last.then_inc(down_ready, 1)

            def lora_down(b):
                pe.wait_ge(a2_hi_ready, b + 1)
                pe.wait_ge(a2_lo_ready, b + 1)
                for o in range(KT):
                    cols = slice(o * P, (o + 1) * P)
                    for e in range(ET):
                        last = three_pass(nc, ps_out[:, o * S:(o + 1) * S], g.w_hi["B2"][:, e, cols], g.w_lo["B2"][:, e, cols], a2_hi[:, e, :], a2_lo[:, e, :],
                                          False, e == ET - 1, skip_group_check=True)
                last.then_inc(out_ready, 1)

            def transpose_out(b, after):
                if after:
                    pe.wait_ge(h32_ready, 2 * b + 6)
                pe.wait_ge(out_gated_ready, 2 * b + 2)
                at_least(pe, y_ready, b)
                for t in range(2):
                    for k in range(KT):
                        last = nc.tensor.transpose(ps_p[:, t * D + k * P:t * D + (k + 1) * P], out_gated[:, k, t * P:(t + 1) * P], g.ident[:])
                last.then_inc(outT_ready, 1)

            def iteration(b, r, before, after):
                q, s = b + 1, 1 - r
                up_first(b, r, 0)
                if before:
                    down(b - 1, s, FT - 1)
                if after:
                    transpose_gated(q, s)
                up_first(b, r, 1)
                up_second(b, r, 0)
                if before:
                    lora_down(b - 1)
                up_first(b, r, 2)
                if after:
                    transpose_normalised(q, s)
                up_second(b, r, 1)
                if before:
                    transpose_out(b - 1, after)
                down(b, r, 0)
                if after:
                    router(q, s, before)
                up_first(b, r, 3)
                up_second(b, r, 2)
                down(b, r, 1)
                if after:
                    transpose_masks(q, 0)
                up_first(b, r, 4)
                if after:
                    transpose_masks(q, 1)
                up_second(b, r, 3)
                if after:
                    transpose_weights(q)
                down(b, r, 2)
                if after:
                    lora_a(q, s, 0)
                up_first(b, r, 5)
                up_second(b, r, 4)
                down(b, r, 3)
                if after:
                    lora_a(q, s, 1)
                up_first(b, r, 6)
                up_second(b, r, 5)
                down(b, r, 4)
                up_second(b, r, 6)
                down(b, r, 5)

            transpose_gated(0, 0)
            transpose_normalised(0, 0)
            router(0, 0, False)
            transpose_masks(0, 0)
            transpose_masks(0, 1)
            transpose_weights(0)
            lora_a(0, 0, 0)
            lora_a(0, 0, 1)
            all_batches(pe, iteration)
            down(B - 1, 1, FT - 1)
            lora_down(B - 1)
            transpose_out(B - 1, False)

        @block.scalar
        def _(act):
            def modulate(q, r):
                act.wait_ge(xnT_ready, q + 1)
                for k in range(KT):
                    nc.scalar.activation(h32[:, k, :], ps_p[:, k * S:(k + 1) * S], ACT.Identity,
                                         scale=g.modT[:, CB, k, bass.ds(q, 1)], bias=g.modT[:, SB_, k, bass.ds(q, 1)]).then_inc(h32_ready, 1)
                act.wait_ge(h32_ready, 2 * q + 2)
                nc.scalar.copy(h_hi[r][:], h32[:]).then_inc(h_hi_ready, 1)

            def tanh_of_gap(q):
                act.wait_ge(route, ROUTE * q + 13)
                nc.scalar.activation(tanh_gap[:], gap[:], ACT.Tanh, scale=0.5).then_inc(tanh_ready, 1)

            def copy_mask(q, r, choice):
                act.wait_ge(mask_ready, 2 * q + choice + 1)
                nc.scalar.copy(maskT[r][choice][:].rearrange("p e s -> p (e s)"), ps_p[:]).then_inc(maskT_ready, 1)

            def copy_weights(q, r):
                act.wait_ge(weight_ready, q + 1)
                nc.scalar.copy(weightT[r][:].rearrange("p k s -> p (k s)"), ps_p[:]).then_inc(weightT_ready, 1)

            def split_a_hi(q, r, w):
                for k in range(2):
                    act.wait_ge(masked_ready, 4 * q + 2 * w + k + 1)
                    nc.scalar.copy(a_hi[r][w][k][:], a_masked[k][:]).then_inc(a_hi_ready, 1)

            def silu_of(b, r, f, k):
                act.wait_ge(up_ready[k], 2 * FT * b + 2 * f + 1)
                at_least(act, glu_ready[k], FT * b + f)
                nc.scalar.activation(silu[k][:], ps_x1[(f + r) % 2][:, 0:S], ACT.Silu).then_inc(silu_ready[k], 1)

            def split_v_hi(b, r, f, k):
                src = (first_w[(f + r) % 2], second_w, both_w)[k]
                act.wait_ge(weighted[k], FT * b + f + 1)
                at_least(act, down_ready, FT * b + f - 1)
                nc.scalar.copy(v_hi[k][(f + r) % 2][:], src[:]).then_inc(v_hi_ready[k], 1)

            def split_a2_hi(b):
                act.wait_ge(a2_step, 3 * b + 3)
                nc.scalar.copy(a2_hi[:], a2_part[0][:]).then_inc(a2_hi_ready, 1)

            def gate_out(b):
                act.wait_ge(out_ready, b + 1)
                for k in range(KT):
                    nc.scalar.activation(out_gated[:, k, :], ps_out[:, k * S:(k + 1) * S], ACT.Identity,
                                         scale=g.modT[:, GB, k, bass.ds(b, 1)]).then_inc(out_gated_ready, 1)

            def keep_x2(b, r):
                act.wait_ge(x2_ready, b + 1)
                at_least(act, stored, 16 * b)
                nc.scalar.copy(y_out[:], x2[r][:]).then_inc(x2_kept, 1)

            def finish_tiles(b, r):
                split_v_hi(b, r, FT - 1, 1)
                split_v_hi(b, r, FT - 1, 2)

            def iteration(b, r, before, after):
                q, s = b + 1, 1 - r
                if before:
                    finish_tiles(b - 1, s)
                    keep_x2(b - 1, s)
                silu_of(b, r, 0, 0)
                if before:
                    split_a2_hi(b - 1)
                silu_of(b, r, 1, 0)
                split_v_hi(b, r, 0, 0)
                silu_of(b, r, 0, 1)
                if before:
                    gate_out(b - 1)
                for f in range(2, FT):
                    split_v_hi(b, r, f - 2, 1)
                    split_v_hi(b, r, f - 2, 2)
                    if after and f == 4:
                        copy_mask(q, s, 0)
                    silu_of(b, r, f, 0)
                    if after and f == 2:
                        modulate(q, s)
                    if after and f == 3:
                        tanh_of_gap(q)
                    if after and f == 4:
                        copy_mask(q, s, 1)
                    split_v_hi(b, r, f - 1, 0)
                    silu_of(b, r, f - 1, 1)
                    if after and f == 4:
                        copy_weights(q, s)
                    if after and f >= 5:
                        split_a_hi(q, s, f - 5)
                split_v_hi(b, r, 5, 1)
                split_v_hi(b, r, 5, 2)
                split_v_hi(b, r, 6, 0)
                silu_of(b, r, 6, 1)

            modulate(0, 0)
            tanh_of_gap(0)
            copy_mask(0, 0, 0)
            copy_mask(0, 0, 1)
            copy_weights(0, 0)
            split_a_hi(0, 0, 0)
            split_a_hi(0, 0, 1)
            all_batches(act, iteration)
            finish_tiles(B - 1, 1)
            keep_x2(B - 1, 1)
            split_a2_hi(B - 1)
            gate_out(B - 1)

        @block.vector
        def _(dve):
            def gate_attention(q, r):
                dve.wait_ge(inputs_loaded[r], 16 * (q - r) + 32)
                at_least(dve, xnT_ready, q)
                for k in range(KT):
                    nc.vector.tensor_scalar(gated[:, k, :], acc_in[r][:, k, :], g.modT[:, GA, k, bass.ds(q, 1)], None, ALU.mult).then_inc(gated_ready, 1)

            def residual(q, r, before):
                if before:
                    dve.wait_ge(x2_kept, q - 1)
                dve.wait_ge(gatedT_ready, q + 1)
                nc.vector.tensor_tensor(x2[r][:].rearrange("p t c -> p (t c)"), ps_p[:], x_in[r][:].rearrange("p t c -> p (t c)"), ALU.add).then_inc(x2_ready, 1)

            def statistics(q, r):
                dve.wait_ge(x2_ready, q + 1)
                for t in range(2):
                    nc.vector.bn_stats(stats[:, t, :], x2[r][:, t, :]).then_inc(stats_ready, 1)
                dve.wait_ge(stats_ready, 2 * q + 2)
                combine_stats(nc, dve, stats, meanvar, vareps[:], moments, ve_ready, q)

            def normalise(q, r):
                dve.wait_ge(rstd_ready, q + 1)
                for t in range(2):
                    nc.vector.tensor_scalar(xn[:, t, :], x2[r][:, t, :], meanvar[:, t, 0:1], rstd[:, t:t + 1], ALU.subtract, ALU.mult).then_inc(xn_ready, 1)

            def split_h_lo(q, r):
                dve.wait_ge(h_hi_ready, q + 1)
                nc.vector.tensor_tensor(h_lo[r][:], h32[:], h_hi[r][:].bitcast(F32), ALU.subtract).then_inc(h_lo_ready, 1)

            def routing(q):
                done = ROUTE * q

                def over_experts(t):
                    return t[:].unsqueeze(2).broadcast_to([P, 2, EXPERTS])

                dve.wait_ge(logits_ready, q + 1)
                nc.vector.tensor_copy(logits[:].rearrange("p t e -> p (t e)"), ps_p[:, 0:2 * EXPERTS]).then_inc(route, 1)
                for k, src in enumerate((logits, rest)):
                    n = done + 1 + 6 * k
                    dve.wait_ge(route, n)
                    nc.vector.tensor_reduce(top[k][:], src[:], AX.X, ALU.max).then_inc(route, 1)
                    dve.wait_ge(route, n + 1)
                    nc.vector.tensor_tensor(equal[k][:], src[:], over_experts(top[k]), ALU.is_equal).then_inc(route, 1)
                    dve.wait_ge(route, n + 2)
                    nc.vector.tensor_tensor(ranked[k][:], equal[k][:], g.first_rank[:], ALU.mult).then_inc(route, 1)
                    dve.wait_ge(route, n + 3)
                    nc.vector.tensor_reduce(best[k][:], ranked[k][:], AX.X, ALU.max).then_inc(route, 1)
                    dve.wait_ge(route, n + 4)
                    nc.vector.tensor_tensor(onehot[k][:], ranked[k][:], over_experts(best[k]), ALU.is_equal).then_inc(route, 1)
                    if k == 0:
                        dve.wait_ge(route, n + 5)
                        nc.vector.scalar_tensor_tensor(rest[:], onehot[0][:], -3.0e38, logits[:], ALU.mult, ALU.add).then_inc(route, 1)
                nc.vector.tensor_tensor(gap[:], top[0][:], top[1][:], ALU.subtract).then_inc(route, 1)

            def choices(q):
                done = ROUTE * q
                dve.wait_ge(route, done + 13)
                at_least(dve, weight_ready, q)
                for k in range(2):
                    nc.vector.tensor_copy(chosen[:, :, k, :].rearrange("p t (e r) -> p t e r", e=EXPERTS),
                                          onehot[k][:].unsqueeze(3).broadcast_to([P, 2, EXPERTS, RANK])).then_inc(route, 1)
                dve.wait_ge(tanh_ready, q + 1)
                for k, sign in enumerate((0.5, -0.5)):
                    nc.vector.tensor_scalar(weight[:, :, k], tanh_gap[:], sign, 0.5, ALU.mult, ALU.add).then_inc(route, 1)

            def step_of_masks(q, r):
                dve.wait_ge(maskT_ready, 2 * q + 2)
                nc.vector.tensor_tensor(mask_step[:], maskT[r][1][:], maskT[r][0][:], ALU.subtract).then_inc(mask_step_ready, 1)

            def mask_a(q, r, w):
                dve.wait_ge(a_ready, 2 * q + w + 1)
                dve.wait_ge(mask_step_ready, q + 1)
                at_least(dve, a_lo_ready, 4 * q + 2 * w)
                for k, mask in enumerate((maskT[r][0], mask_step)):
                    nc.vector.tensor_tensor(a_masked[k][:], ps_p[:].rearrange("p (e s) -> p e s", e=ET), mask[:], ALU.mult).then_inc(masked_ready, 1)

            def glu_of(b, r, f, k):
                dve.wait_ge(silu_ready[k], FT * b + f + 1)
                dve.wait_ge(up_ready[k], 2 * FT * b + 2 * f + 2)
                at_least(dve, weighted[k], FT * b + f)
                nc.vector.tensor_tensor(glu[k][:], ps_x3[(f + r) % 2][:, 0:S], silu[k][:], ALU.mult).then_inc(glu_ready[k], 1)

            def split_v_lo(b, r, f, k):
                src = (first_w[(f + r) % 2], second_w, both_w)[k]
                dve.wait_ge(v_hi_ready[k], FT * b + f + 1)
                nc.vector.tensor_tensor(v_lo[k][(f + r) % 2][:], src[:], v_hi[k][(f + r) % 2][:].bitcast(F32), ALU.subtract).then_inc(v_lo_ready[k], 1)

            def mask_a2(b, r):
                dve.wait_ge(down_ready, FT * b + FT)
                for k in range(2):
                    nc.vector.tensor_tensor(a2_part[k][:], ps_a2[k][:].rearrange("p (e s) -> p e s", e=ET), maskT[r][k][:], ALU.mult).then_inc(a2_step, 1)
                dve.wait_ge(a2_step, 3 * b + 2)
                nc.vector.tensor_tensor(a2_part[0][:], a2_part[0][:], a2_part[1][:], ALU.add).then_inc(a2_step, 1)

            def split_a2_lo(b):
                dve.wait_ge(a2_hi_ready, b + 1)
                nc.vector.tensor_tensor(a2_lo[:], a2_part[0][:], a2_hi[:].bitcast(F32), ALU.subtract).then_inc(a2_lo_ready, 1)

            def output(b):
                dve.wait_ge(outT_ready, b + 1)
                dve.wait_ge(x2_kept, b + 1)
                nc.vector.tensor_tensor(y_out[:].rearrange("p t c -> p (t c)"), ps_p[:], y_out[:].rearrange("p t c -> p (t c)"), ALU.add).then_inc(y_ready, 1)

            def finish_tiles(b, r):
                split_v_lo(b, r, FT - 1, 1)
                split_v_lo(b, r, FT - 1, 2)

            def iteration(b, r, before, after):
                q, s = b + 1, 1 - r
                if before:
                    finish_tiles(b - 1, s)
                if after:
                    gate_attention(q, s)
                glu_of(b, r, 0, 0)
                if before:
                    mask_a2(b - 1, s)
                if after:
                    residual(q, s, before)
                if before:
                    split_a2_lo(b - 1)
                if after:
                    statistics(q, s)
                glu_of(b, r, 1, 0)
                split_v_lo(b, r, 0, 0)
                glu_of(b, r, 0, 1)
                if after:
                    normalise(q, s)
                for f in range(2, FT):
                    split_v_lo(b, r, f - 2, 1)
                    split_v_lo(b, r, f - 2, 2)
                    if after and f == 3:
                        routing(q)
                    if after and f >= 5:
                        mask_a(q, s, f - 5)
                    glu_of(b, r, f, 0)
                    if after and f == 3:
                        choices(q)
                    split_v_lo(b, r, f - 1, 0)
                    glu_of(b, r, f - 1, 1)
                    if before and f == 2:
                        output(b - 1)
                    if after and f == 2:
                        split_h_lo(q, s)
                    if after and f == 4:
                        step_of_masks(q, s)
                split_v_lo(b, r, 5, 1)
                split_v_lo(b, r, 5, 2)
                split_v_lo(b, r, 6, 0)
                glu_of(b, r, 6, 1)

            gate_attention(0, 0)
            residual(0, 0, False)
            statistics(0, 0)
            normalise(0, 0)
            split_h_lo(0, 0)
            routing(0)
            choices(0)
            step_of_masks(0, 0)
            mask_a(0, 0, 0)
            mask_a(0, 0, 1)
            all_batches(dve, iteration)
            finish_tiles(B - 1, 1)
            mask_a2(B - 1, 1)
            split_a2_lo(B - 1)
            output(B - 1)

        @block.gpsimd
        def _(pool):
            def inverse_deviation(q):
                pool.wait_ge(ve_ready, 4 * q + 4)
                nc.gpsimd.tensor_tensor(rstd[:], vareps[:], g.minus_half[:, 0:2], ALU.pow).then_inc(rstd_ready, 1)

            def split_a_lo(q, r, w):
                for k in range(2):
                    pool.wait_ge(a_hi_ready, 4 * q + 2 * w + k + 1)
                    nc.gpsimd.tensor_tensor(a_lo[r][w][k][:], a_masked[k][:], a_hi[r][w][k][:].bitcast(F32), ALU.subtract).then_inc(a_lo_ready, 1)

            def weigh(b, r, f, k):
                out = (first_w[(f + r) % 2], second_w)[k]
                pool.wait_ge(glu_ready[k], FT * b + f + 1)
                at_least(pool, v_lo_ready[k], FT * b + f - (1 if k == 0 else 0))
                at_least(pool, weighted[2], FT * b + f - (1 if k == 0 else 0))
                nc.gpsimd.tensor_tensor(out[:], glu[k][:], weightT[r][:, k, :], ALU.mult).then_inc(weighted[k], 1)

            def add_choices(b, r, f):
                pool.wait_ge(weighted[1], FT * b + f + 1)
                at_least(pool, v_lo_ready[2], FT * b + f)
                nc.gpsimd.tensor_tensor(both_w[:], first_w[(f + r) % 2][:], second_w[:], ALU.add).then_inc(weighted[2], 1)

            def iteration(b, r, before, after):
                q, s = b + 1, 1 - r
                weigh(b, r, 0, 0)
                if after:
                    inverse_deviation(q)
                for f in range(1, FT):
                    weigh(b, r, f, 0)
                    weigh(b, r, f - 1, 1)
                    add_choices(b, r, f - 1)
                    if after and f >= 5:
                        split_a_lo(q, s, f - 5)
                weigh(b, r, FT - 1, 1)
                add_choices(b, r, FT - 1)

            inverse_deviation(0)
            split_a_lo(0, 0, 0)
            split_a_lo(0, 0, 1)
            all_batches(pool, iteration)


def adaln_attention_mixture_kernel(nc, x, w_qkv, w_o, Wg, W1, W2, W3, A1, B1, A2, B2, A3, B3, c, wmod, out):
    dram = dict(x=x, w_qkv=w_qkv, w_o=w_o, Wg=Wg, W1=W1, W2=W2, W3=W3, A1=A1, B1=B1, A2=A2, B2=B2, A3=A3, B3=B3,
                c=c, wmod=wmod, out=out, acc=nc.dram_tensor("acc_dram", [P, KT, TOK], F32, kind="Internal").ap())
    with ExitStack() as ctx:
        m = Memory(nc, ctx)
        g = shared_memory(nc, m)
        with ExitStack() as heads:
            head_memory(nc, Memory(nc, heads), g)
            setup_phase(nc, m, dram, g)
            attention_phase(nc, m, dram, g)
        with ExitStack() as ffn:
            ffn_memory(nc, Memory(nc, ffn), g)
            ffn_weight_phase(nc, m, dram, g)
            ffn_phase(nc, m, dram, g)


_INS = ['L0_attn_x', 'L0_attn_w_qkv', 'L0_attn_w_o', 'L0_ffn_Wg', 'L0_ffn_W1', 'L0_ffn_W2', 'L0_ffn_W3', 'L0_ffn_A1', 'L0_ffn_B1',
        'L0_ffn_A2', 'L0_ffn_B2', 'L0_ffn_A3', 'L0_ffn_B3', 'L0_c', 'L0_wmod']
_OUTS = [((B, S, D), 'float32')]


def kernel(**inputs):
    import numpy as _np
    import concourse.bacc as _bacc
    from concourse import mybir as _mybir
    from concourse.bass_utils import run_bass_kernel_spmd as _run

    nc = _bacc.Bacc("TRN2", target_bir_lowering=False, num_devices=1)
    arrays, args = {}, []
    for name in _INS:
        a = _np.ascontiguousarray(inputs[name])
        arrays[f"in_{name}_dram"] = a
        args.append(nc.dram_tensor(f"in_{name}_dram", a.shape, _mybir.dt.from_np(a.dtype), kind="ExternalInput").ap())
    for i, (shape, dtype) in enumerate(_OUTS):
        dt = _mybir.dt.from_np(_np.dtype(dtype))
        args.append(nc.dram_tensor(f"out_{i}_dram", shape, dt, kind="ExternalOutput").ap())
    adaln_attention_mixture_kernel(nc, *args)
    r = _run(nc, [arrays], core_ids=[0])
    return r.results[0]["out_0_dram"]
```

```python
import concourse.bass as bass
from concourse import mybir
from contextlib import ExitStack
import math

F32 = mybir.dt.float32
F32R = mybir.dt.float32r
BF16 = mybir.dt.bfloat16
ALU = mybir.AluOpType
ACT = mybir.ActivationFunctionType
AX = mybir.AxisListType

P = 128
B, S, D = 16, 256, 256
HEADS, DH = 16, 128
KT = D // P
PAIRS = B // 2
STEPS = HEADS * PAIRS
PT = 2 * S
TOK = B * S
FF, EXPERTS, RANK = 896, 8, 32
FT = FF // P
ER = EXPERTS * RANK
ET = ER // P
EPS = 1e-5
SCALE = 1.0 / math.sqrt(DH)
SA, CA, GA, SB_, CB, GB = range(6)


def at_least(eng, sem, value):
    if isinstance(value, int) and value <= 0:
        return
    eng.wait_ge(sem, value)


def three_pass(nc, out, w_hi, w_lo, x_hi, x_lo, first, last, **kw):
    nc.tensor.matmul(out, w_hi, x_hi, start=first, stop=False, **kw)
    nc.tensor.matmul(out, w_hi, x_lo, start=False, stop=False, **kw)
    return nc.tensor.matmul(out, w_lo, x_hi, start=False, stop=last, **kw)


class Memory:

    def __init__(self, nc, ctx):
        self.nc, self.ctx = nc, ctx

    def sb(self, name, shape, dt=F32):
        return self.ctx.enter_context(self.nc.sbuf_tensor(name, shape, dt))

    def ps(self, name, shape=(P, 512)):
        return self.ctx.enter_context(self.nc.psum_tensor(name, list(shape), F32))

    def sem(self, name):
        return self.ctx.enter_context(self.nc.semaphore(name))


def combine_stats(nc, dve, stats, meanvar, vareps, moments, ve_ready, done):
    even_mean, odd_mean = stats[:, :, 1], stats[:, :, 4]
    nc.vector.tensor_tensor(meanvar[:, :, 0], even_mean, odd_mean, ALU.add).then_inc(moments, 1)
    nc.vector.tensor_tensor(meanvar[:, :, 1], even_mean, odd_mean, ALU.subtract).then_inc(moments, 1)
    nc.vector.tensor_tensor(vareps, stats[:, :, 2], stats[:, :, 5], ALU.add).then_inc(moments, 1)
    dve.wait_ge(moments, 3 * done + 3)
    nc.vector.tensor_scalar(meanvar[:, :, 0], meanvar[:, :, 0], 0.5, None, ALU.mult).then_inc(ve_ready, 1)
    nc.vector.tensor_scalar(vareps, vareps, 1.0 / D, EPS, ALU.mult, ALU.add).then_inc(ve_ready, 1)
    nc.vector.scalar_tensor_tensor(meanvar[:, :, 1], meanvar[:, :, 1], 0.25, meanvar[:, :, 1], ALU.mult, ALU.mult).then_inc(ve_ready, 1)
    dve.wait_ge(ve_ready, 4 * done + 3)
    nc.vector.tensor_tensor(vareps, vareps, meanvar[:, :, 1], ALU.add).then_inc(ve_ready, 1)


ACT_PAIRS, POOL_PAIRS = 6, 3


def setup_phase(nc, dram, g):
    with ExitStack() as ctx:
        m = Memory(nc, ctx)
        c_sb = m.sb("c_sb", [B, D])
        sc = m.sb("silu_c", [B, D])
        scT = m.sb("silu_cT", [P, KT, B])
        mod_row = m.sb("mod_row", [B, 6 * D])
        gate_sign = m.sb("gate_sign", [P, 2, KT, B])
        gate_abs = m.sb("gate_abs", [P, 2, KT, B])
        stats = m.sb("ln_stats", [P, 4 * PAIRS, 6])
        meanvar = m.sb("ln_meanvar", [P, 4 * PAIRS, 2])
        vareps = m.sb("ln_vareps", [P, 4 * PAIRS])
        rstd = m.sb("ln_rstd", [P, 4 * PAIRS])
        halves, inverse_d, epsilons = m.sb("halves", [P, 4]), m.sb("inverse_d", [P, 4]), m.sb("epsilons", [P, 4])
        x_all = g.accT[:].rearrange("p k n -> p (k n)").rearrange("p (t c) -> p t c", c=D)
        arena = Arena(nc, g.arena_offset, 4 * ARENA)
        h32 = arena.sb("h32", [P, KT, TOK])
        wmod = arena.sb("wmod", [P, KT, 6 * D])
        ps_small = m.ps("ps_small")
        ps_t = [[m.ps(f"ps_t{r}{k}") for k in range(KT)] for r in range(2)]
        ps_mod = [ps_t[0][0], ps_t[0][1], ps_t[1][0]]

        c_loaded, wmod_loaded = m.sem("c_loaded"), m.sem("wmod_loaded")
        x_loaded = [m.sem("x_loaded0"), m.sem("x_loaded1")]
        silu_done, cT_ready, cT_copied = m.sem("silu_done"), m.sem("cT_ready"), m.sem("cT_copied")
        mod_ready, mod_copied, modT_ready = m.sem("mod_ready"), m.sem("mod_copied"), m.sem("modT_ready")
        modT_copied, gate_step = m.sem("modT_copied"), m.sem("gate_step")
        stats_ready, moments, ve_ready = m.sem("stats_ready"), m.sem("moments"), m.sem("ve_ready")
        rstd_ready, xn_ready, xnT_ready = m.sem("rstd_ready"), m.sem("xn_ready"), m.sem("xnT_ready")
        h_ready, h_hi_ready, h_lo_ready = m.sem("h_ready"), m.sem("h_hi_ready"), m.sem("h_lo_ready")
        zero_ready = m.sem("zero_ready")

        def split_h_lo(engine, n):
            cols = bass.ds(n * PT, PT)
            return engine.tensor_tensor(g.h_lo[:, :, cols], h32[:, :, cols], g.h_hi[:, :, cols].bitcast(F32), ALU.subtract)

        block = ctx.enter_context(nc.Block())

        @block.sync
        def _(sp):
            xg = dram["x"].rearrange("b (t p) c -> b p t c", p=P)

            def load_pair(i, r):
                n = 2 * i + r
                for j in range(2):
                    sp.dma_start(x_all[:, bass.ds(4 * n + 2 * j, 2), :], xg[2 * n + j]).then_inc(x_loaded[r], 16)

            sp.dma_start(c_sb[:], dram["c"]).then_inc(c_loaded, 16)
            sp.dma_start(wmod[:], dram["wmod"].rearrange("(k p) n -> p k n", p=P)).then_inc(wmod_loaded, 16)
            load_pair(0, 0)
            load_pair(0, 1)
            load_head(nc, sp, dram, g, 0, 0)
            with sp.Fori(1, PAIRS // 2) as i:
                for r in range(2):
                    sp.wait_ge(stats_ready, 8 * i + (4 * r - 4))
                    load_pair(i, r)
            load_head(nc, sp, dram, g, 1, 1)

        @block.gpsimd
        def _(pool):
            nc.gpsimd.memset(g.ident[:], 0.0).then_inc(zero_ready, 1)
            pool.wait_ge(zero_ready, 1)
            nc.gpsimd.affine_select(out=g.ident[:], in_=g.ident[:], compare_op=ALU.not_equal, fill=1.0,
                                    base=0, pattern=[[-1, P]], channel_multiplier=1).then_inc(g.ident_ready, 1)
            nc.gpsimd.memset(g.minus_half[:], -0.5).then_inc(g.consts_ready, 1)
            nc.gpsimd.memset(g.ones[:], 1.0).then_inc(g.ones_ready, 1)
            for e in range(EXPERTS):
                nc.gpsimd.memset(g.first_rank[:, :, e:e + 1], float(EXPERTS - e)).then_inc(g.rank_ready, 1)
            for tile, value in ((halves, 0.5), (inverse_d, 1.0 / D), (epsilons, EPS)):
                nc.gpsimd.memset(tile[:], value).then_inc(g.consts_ready, 1)
            pool.wait_ge(g.consts_ready, 4)
            for n in range(PAIRS):
                pool.wait_ge(stats_ready, 4 * n + 4)
                rows = slice(4 * n, 4 * n + 4)
                mean, difference = meanvar[:, rows, 0], meanvar[:, rows, 1]
                ve = vareps[:, rows]
                even, odd = stats[:, rows, 0:3], stats[:, rows, 3:6]
                nc.gpsimd.tensor_tensor(mean, even[:, :, 1], odd[:, :, 1], ALU.add).then_inc(moments, 1)
                nc.gpsimd.tensor_tensor(difference, even[:, :, 1], odd[:, :, 1], ALU.subtract).then_inc(moments, 1)
                nc.gpsimd.tensor_tensor(ve, even[:, :, 2], odd[:, :, 2], ALU.add).then_inc(moments, 1)
                pool.wait_ge(moments, 3 * n + 3)
                nc.gpsimd.tensor_tensor(difference, difference, halves[:], ALU.mult).then_inc(ve_ready, 1)
                nc.gpsimd.tensor_tensor(ve, ve, inverse_d[:], ALU.mult).then_inc(ve_ready, 1)
                nc.gpsimd.tensor_tensor(mean, mean, halves[:], ALU.mult).then_inc(ve_ready, 1)
                pool.wait_ge(ve_ready, 6 * n + 3)
                nc.gpsimd.tensor_tensor(difference, difference, difference, ALU.mult).then_inc(ve_ready, 1)
                nc.gpsimd.tensor_tensor(ve, ve, epsilons[:], ALU.add).then_inc(ve_ready, 1)
                pool.wait_ge(ve_ready, 6 * n + 5)
                nc.gpsimd.tensor_tensor(ve, ve, difference, ALU.add).then_inc(ve_ready, 1)
                pool.wait_ge(ve_ready, 6 * n + 6)
                nc.gpsimd.tensor_tensor(rstd[:, rows], vareps[:, rows], g.minus_half[:], ALU.pow).then_inc(rstd_ready, 1)
            split_head_weights_lo(nc, pool, g, 0, 0)
            for n in range(POOL_PAIRS):
                pool.wait_ge(h_hi_ready, n + 1)
                split_h_lo(nc.gpsimd, n).then_inc(h_lo_ready, 1)

        @block.tensor
        def _(pe):
            def transpose_pair(n):
                r = n % 2
                pe.wait_ge(xn_ready, 4 * n + 4)
                at_least(pe, h_ready, 4 * n - 4)
                for k in range(KT):
                    for t in range(4):
                        last = nc.tensor.transpose(ps_t[r][k][:, t * P:(t + 1) * P], x_all[:, 4 * n + t, k * P:(k + 1) * P], g.ident[:])
                    last.then_inc(xnT_ready, 1)

            pe.wait_ge(g.ident_ready, 1)
            pe.wait_ge(silu_done, 1)
            for k in range(KT):
                last = nc.tensor.transpose(ps_small[:, k * B:(k + 1) * B], sc[:, k * P:(k + 1) * P], g.ident[0:B, 0:B])
            last.then_inc(cT_ready, 1)
            pe.wait_ge(cT_copied, 1)
            pe.wait_ge(wmod_loaded, 16)
            for n in range(3):
                for k in range(KT):
                    last = nc.tensor.matmul(ps_mod[n][0:B, :], scT[:, k, :], wmod[:, k, n * 512:(n + 1) * 512],
                                            start=(k == 0), stop=(k == KT - 1))
                last.then_inc(mod_ready, 1)
            transpose_head_values(nc, pe, g, 0, 0)
            pe.wait_ge(mod_copied, 3)
            for n in range(6 * KT):
                last = nc.tensor.transpose(ps_small[:, n * B:(n + 1) * B], mod_row[:, n * P:(n + 1) * P], g.ident[0:B, 0:B])
            last.then_inc(modT_ready, 1)
            transpose_pair(0)
            transpose_pair(1)
            combine_head_values(nc, pe, g, 0, 0)
            for n in range(2, PAIRS):
                transpose_pair(n)

        @block.scalar
        def _(act):
            def modulate(i, r):
                n = 2 * i + r
                for k in range(KT):
                    act.wait_ge(xnT_ready, 2 * n + k + 1)
                    for j in range(2):
                        b = 2 * n + j
                        nc.scalar.activation(h32[:, k, bass.ds(b * S, S)], ps_t[r][k][:, j * S:(j + 1) * S],
                                             ACT.Identity, scale=g.modT[:, CA, k, bass.ds(b, 1)],
                                             bias=g.modT[:, SA, k, bass.ds(b, 1)]).then_inc(h_ready, 1)

            def split_h_hi(i, r):
                n = 2 * i + r
                act.wait_ge(h_ready, 4 * n + 4)
                cols = bass.ds(n * PT, PT)
                nc.scalar.copy(g.h_hi[:, :, cols], h32[:, :, cols]).then_inc(h_hi_ready, 1)

            act.wait_ge(c_loaded, 16)
            nc.scalar.activation(sc[:], c_sb[:], ACT.Silu).then_inc(silu_done, 1)
            act.wait_ge(cT_ready, 1)
            nc.scalar.copy(scT[:].rearrange("p k b -> p (k b)"), ps_small[:, 0:KT * B]).then_inc(cT_copied, 1)
            for n in range(3):
                act.wait_ge(mod_ready, n + 1)
                nc.scalar.copy(mod_row[:, n * 512:(n + 1) * 512], ps_mod[n][0:B, :]).then_inc(mod_copied, 1)
            copy_head_values(nc, act, g, 0, 0)
            split_head_weights_hi(nc, act, g, 0, 0)
            act.wait_ge(modT_ready, 1)
            modT_ps = ps_small[:, 0:6 * KT * B].rearrange("p (s n) -> p s n", s=6)
            for row in range(6):
                nc.scalar.activation(g.modT[:, row].rearrange("p k b -> p (k b)"), modT_ps[:, row], ACT.Copy,
                                     bias=1.0 if row in (CA, CB) else 0.0).then_inc(modT_copied, 1)
            act.wait_ge(modT_copied, 6)
            with act.Fori(0, ACT_PAIRS // 2) as i:
                modulate(i, 0)
                split_h_hi(i, 0)
                modulate(i, 1)
                split_h_hi(i, 1)
            with act.Fori(ACT_PAIRS // 2, PAIRS // 2) as i:
                modulate(i, 0)
                modulate(i, 1)
            split_head_values_hi(nc, act, g, 0, 0)

        @block.vector
        def _(dve):
            def statistics(i, r):
                n = 2 * i + r
                dve.wait_ge(x_loaded[r], 32 * i + 32)
                for t in range(4):
                    nc.vector.bn_stats(stats[:, 4 * n + t, :], x_all[:, 4 * n + t, :]).then_inc(stats_ready, 1)

            def normalise(i, r):
                n = 2 * i + r
                dve.wait_ge(rstd_ready, n + 1)
                for t in range(4):
                    row = 4 * n + t
                    nc.vector.tensor_scalar(x_all[:, row, :], x_all[:, row, :], meanvar[:, row, 0:1], rstd[:, bass.ds(row, 1)],
                                            ALU.subtract, ALU.mult).then_inc(xn_ready, 1)

            statistics(0, 0)
            statistics(0, 1)
            with dve.Fori(0, PAIRS // 2 - 1) as i:
                statistics(i + 1, 0)
                normalise(i, 0)
                statistics(i + 1, 1)
                normalise(i, 1)
            normalise(PAIRS // 2 - 1, 0)
            normalise(PAIRS // 2 - 1, 1)
            dve.wait_ge(modT_copied, 6)
            for n, row in enumerate((GA, GB)):
                nc.vector.tensor_scalar(gate_sign[:, n], g.modT[:, row], 0.0, 2.0, ALU.is_ge, ALU.mult).then_inc(gate_step, 1)
                nc.vector.scalar_tensor_tensor(gate_abs[:, n], g.modT[:, row], -1.0, g.modT[:, row], ALU.mult, ALU.max).then_inc(gate_step, 1)
            dve.wait_ge(gate_step, 4)
            nc.vector.tensor_scalar(gate_abs[:], gate_abs[:], 0.25, None, ALU.max).then_inc(gate_step, 1)
            dve.wait_ge(gate_step, 5)
            for n, row in enumerate((GA, GB)):
                nc.vector.scalar_tensor_tensor(g.modT[:, row], gate_sign[:, n], -1.0, gate_abs[:, n], ALU.add, ALU.mult).then_inc(gate_step, 1)
            dve.wait_ge(g.ones_ready, 1)
            nc.vector.tensor_copy(g.ones_r[:], g.ones[:]).then_inc(g.ones_r_ready, 1)
            dve.wait_ge(g.ident_ready, 1)
            nc.vector.tensor_copy(g.ident_bf16[:], g.ident[:]).then_inc(g.ones_r_ready, 1)
            for n in range(POOL_PAIRS, ACT_PAIRS):
                dve.wait_ge(h_hi_ready, n + 1)
                split_h_lo(nc.vector, n).then_inc(h_lo_ready, 1)
            with dve.Fori(ACT_PAIRS, PAIRS) as n:
                dve.wait_ge(h_ready, 4 * n + 4)
                cols = bass.ds(n * PT, PT)
                nc.vector.tensor_copy(g.h_hi[:, :, cols], h32[:, :, cols]).then_inc(h_hi_ready, 1)
                dve.wait_ge(h_hi_ready, n + 1)
                split_h_lo(nc.vector, n).then_inc(h_lo_ready, 1)
            split_head_values_lo(nc, dve, g, 0, 0)
            dve.wait_ge(h_lo_ready, PAIRS)



RAW_LOADS = 16 * (KT + 1)


def load_head(nc, sp, dram, g, h, r):
    columns = dram["w_qkv"].rearrange("(k p) (t h d) -> h k p t d", p=P, t=3, h=HEADS)
    for k in range(KT):
        sp.dma_start(g.raw_qkv[:, r, k], columns[h, k]).then_inc(g.raw_loaded[r], 16)
    sp.dma_start(g.raw_o[:, r], dram["w_o"].rearrange("(h d) n -> h d n", d=DH)[h]).then_inc(g.raw_loaded[r], 16)


def raw_there(eng, g, pair_of_head, r):
    eng.wait_ge(g.raw_loaded[r], RAW_LOADS * (pair_of_head + 1))


def transpose_head_values(nc, pe, g, hp, r):
    h = 2 * hp + r
    raw_there(pe, g, hp, r)
    at_least(pe, g.m_lo_ready, h)
    for k in range(KT):
        last = nc.tensor.transpose(g.ps_head[:, k * P:(k + 1) * P], g.raw_qkv[:, r, k, 2, :], g.ident[:])
    last.then_inc(g.wvT_ready, 1)


def combine_head_values(nc, pe, g, hp, r):
    h = 2 * hp + r
    pe.wait_ge(g.wvT_copied, h + 1)
    for k in range(KT):
        last = nc.tensor.matmul(g.ps_head[:, k * D:(k + 1) * D], g.wvT[:, k * P:(k + 1) * P], g.raw_o[:, r, :], start=True, stop=True)
    last.then_inc(g.m_ready, 1)


def copy_head_values(nc, act, g, hp, r):
    act.wait_ge(g.wvT_ready, 2 * hp + r + 1)
    nc.scalar.copy(g.wvT[:], g.ps_head[:, 0:D]).then_inc(g.wvT_copied, 1)


def split_head_weights_hi(nc, act, g, hp, r):
    raw_there(act, g, hp, r)
    nc.scalar.copy(g.wqk_hi[r][:], g.raw_qkv[:, r, :, 0:2, :]).then_inc(g.wqk_hi_ready, 1)


def split_head_weights_lo(nc, pool, g, hp, r):
    pool.wait_ge(g.wqk_hi_ready, 2 * hp + r + 1)
    nc.gpsimd.tensor_tensor(g.wqk_lo[r][:], g.raw_qkv[:, r, :, 0:2, :], g.wqk_hi[r][:].bitcast(F32), ALU.subtract).then_inc(g.wqk_lo_ready, 1)


def split_head_values_hi(nc, act, g, hp, r):
    act.wait_ge(g.m_ready, 2 * hp + r + 1)
    nc.scalar.copy(g.m_hi[r][:].rearrange("p k n -> p (k n)"), g.ps_head[:]).then_inc(g.m_hi_ready, 1)


def split_head_values_lo(nc, dve, g, hp, r):
    dve.wait_ge(g.m_hi_ready, 2 * hp + r + 1)
    nc.vector.tensor_tensor(g.m_lo[r][:].rearrange("p k n -> p (k n)"), g.ps_head[:],
                            g.m_hi[r][:].rearrange("p k n -> p (k n)").bitcast(F32), ALU.subtract).then_inc(g.m_lo_ready, 1)


def attention_phase(nc, dram, g):
    with ExitStack() as ctx:
        m = Memory(nc, ctx)
        q32 = m.sb("q32", [P, PT])
        q_hi, q_lo = m.sb("q_hi", [P, PT], F32R), m.sb("q_lo", [P, PT], F32R)
        k_hi, k_lo = m.sb("k_hi", [P, PT], F32R), m.sb("k_lo", [P, PT], F32R)
        negmax, rowsum, rinv = m.sb("negmax", [P, 4]), m.sb("rowsum", [P, 4]), m.sb("rinv", [P, 4])
        probs = m.sb("probs", [P, 2, 2, S])
        half = m.sb("half_sum", [P, 2, S])
        wsum = m.sb("wsum", [P, 2, S])
        wsum_hi, wsum_lo = m.sb("wsum_hi", [P, PT], F32R), m.sb("wsum_lo", [P, PT], F32R)
        colsum = m.sb("colsum", [P, PT])
        prod = m.sb("prod", [P, KT, PT])
        ps_q, ps_k = m.ps("ps_q"), m.ps("ps_k")
        ps_s = [m.ps("ps_s0"), m.ps("ps_s1")]
        ps_y = [m.ps("ps_y0"), m.ps("ps_y1")]
        ps_c = m.ps("ps_c")

        proj_ready = m.sem("proj_ready")
        qk_hi_ready = m.sem("qk_hi_ready")
        q32_ready = m.sem("q32_ready")
        q_lo_ready = m.sem("q_lo_ready")
        k_lo_ready = m.sem("k_lo_ready")
        scores_ready = m.sem("scores_ready")
        negmax_ready = m.sem("negmax_ready")
        probs_ready = m.sem("probs_ready")
        rinv_ready = m.sem("rinv_ready")
        half_ready = m.sem("half_ready")
        wsum_ready = m.sem("wsum_ready")
        wsum_hi_ready = m.sem("wsum_hi_ready")
        wsum_lo_ready = m.sem("wsum_lo_ready")
        y_ready = m.sem("y_ready")
        c_ready = m.sem("c_ready")
        c_copied = m.sem("c_copied")
        prod_ready = m.sem("prod_ready")
        acc_added = m.sem("acc_added")

        def run_heads(eng, head):
            head(0, 0, first=True)
            head(0, 1, second=True)
            with eng.Fori(1, HEADS // 2 - 1) as hp:
                head(hp, 0)
                head(hp, 1)
            head(HEADS // 2 - 1, 0)
            head(HEADS // 2 - 1, 1, final=True)

        def run_inner_pairs(eng, step, h):
            with eng.Fori(0, PAIRS // 2 - 1) as i:
                for j in (1, 2):
                    step(PAIRS * h + 2 * i + j, 2 * i + j)

        block = ctx.enter_context(nc.Block())

        @block.sync
        def _(sp):
            load_ffn_weights(nc, sp, dram, g)
            with sp.Fori(0, HEADS // 2 - 1) as i:
                for r in range(2):
                    done = 2 * i + r + 1
                    sp.wait_ge(g.m_ready, done)
                    sp.wait_ge(g.wqk_hi_ready, done)
                    sp.wait_ge(g.wqk_lo_ready, done)
                    load_head(nc, sp, dram, g, 2 * i + (2 + r), r)
            for p in range(PAIRS):
                sp.wait_ge(acc_added, 2 * (8 * (HEADS - 2) + p) + 2)
                sp.dma_start(dram["acc"][:, :, p * PT:(p + 1) * PT], g.accT[:, :, p * PT:(p + 1) * PT]).then_inc(g.acc_stored, 16)

        @block.tensor
        def _(pe):
            def project(n, pair, r, k_wqk):
                at_least(pe, g.wqk_hi_ready, k_wqk)
                at_least(pe, g.wqk_lo_ready, k_wqk)
                for t, ps in enumerate((ps_q, ps_k)):
                    for k in range(KT):
                        cols = bass.ds(pair * PT, PT)
                        last = three_pass(nc, ps[:], g.wqk_hi[r][:, k, t, :], g.wqk_lo[r][:, k, t, :],
                                          g.h_hi[:, k, cols], g.h_lo[:, k, cols], k == 0, k == KT - 1)
                    last.then_inc(proj_ready, 1)

            def column_sums(n):
                pe.wait_ge(wsum_hi_ready, n + 1)
                pe.wait_ge(wsum_lo_ready, n + 1)
                at_least(pe, c_copied, n)
                nc.tensor.matmul(ps_c[:], g.ones_r[:], wsum_hi[:], start=True, stop=False)
                nc.tensor.matmul(ps_c[:], g.ones_r[:], wsum_lo[:], start=False, stop=True).then_inc(c_ready, 1)

            def step(n, pair, before, r, follow, m_needed=None):
                pe.wait_ge(qk_hi_ready, 2 * n + 2)
                pe.wait_ge(q_lo_ready, n + 1)
                pe.wait_ge(k_lo_ready, n + 1)
                at_least(pe, probs_ready, 4 * n)
                for j in range(2):
                    keys = slice(j * S, (j + 1) * S)
                    for qt in range(2):
                        qs = slice(j * S + qt * P, j * S + (qt + 1) * P)
                        last = three_pass(nc, ps_s[j][:, qt * S:(qt + 1) * S], q_hi[:, qs], q_lo[:, qs], k_hi[:, keys], k_lo[:, keys], True, True)
                    last.then_inc(scores_ready, 1)
                if before:
                    column_sums(n - 1)
                if follow:
                    project(*follow)
                if m_needed is not None:
                    pe.wait_ge(g.m_hi_ready, m_needed)
                    pe.wait_ge(g.m_lo_ready, m_needed)
                at_least(pe, prod_ready, 2 * n)
                for o in range(KT):
                    for k in range(KT):
                        cols = bass.ds(pair * PT, PT)
                        last = three_pass(nc, ps_y[o][:], g.m_hi[r][:, k, o * P:(o + 1) * P], g.m_lo[r][:, k, o * P:(o + 1) * P],
                                          g.h_hi[:, k, cols], g.h_lo[:, k, cols], k == 0, k == KT - 1)
                    last.then_inc(y_ready, 1)

            def head(hp, r, first=False, second=False, final=False):
                h = 2 * hp + r
                nhp, nr = (hp, 1) if r == 0 else (hp + 1, 0)
                step(8 * h, 0, not first, r, (8 * h + 1, 1, r, 0), h + 1)
                if not final:
                    transpose_head_values(nc, pe, g, nhp, nr)
                run_inner_pairs(pe, lambda n, p: step(n, p, True, r, (n + 1, p + 1, r, 0)), h)
                if not final:
                    combine_head_values(nc, pe, g, nhp, nr)
                n = 8 * h + 7
                step(n, PAIRS - 1, True, r, None if final else (n + 1, 0, nr, h + 2))

            pe.wait_ge(g.ones_r_ready, 1)
            project(0, 0, 0, 1)
            run_heads(pe, head)
            column_sums(STEPS - 1)

        @block.scalar
        def _(act):
            def split_hi(n):
                act.wait_ge(proj_ready, 2 * n + 1)
                nc.scalar.activation(q32[:], ps_q[:], ACT.Copy, scale=SCALE).then_inc(q32_ready, 1)
                nc.scalar.activation(q_hi[:], ps_q[:], ACT.Copy, scale=SCALE).then_inc(qk_hi_ready, 1)
                act.wait_ge(proj_ready, 2 * n + 2)
                nc.scalar.copy(k_hi[:], ps_k[:]).then_inc(qk_hi_ready, 1)

            def copy_column_sums(n):
                act.wait_ge(c_ready, n + 1)
                at_least(act, prod_ready, 2 * n)
                nc.scalar.copy(colsum[:], ps_c[:]).then_inc(c_copied, 1)

            def step(n, pair, before, follow):
                at_least(act, wsum_ready, 2 * n)
                for j in range(2):
                    act.wait_ge(negmax_ready, 2 * n + j + 1)
                    for qt in range(2):
                        i = 2 * j + qt
                        if before and i == 1:
                            copy_column_sums(n - 1)
                        nc.scalar.activation(probs[:, j, qt, :], ps_s[j][:, qt * S:(qt + 1) * S], ACT.Exp,
                                             bias=negmax[:, i:i + 1], accum_out=rowsum[:, i:i + 1]).then_inc(probs_ready, 1)
                if follow:
                    split_hi(n + 1)
                act.wait_ge(wsum_ready, 2 * n + 2)
                at_least(act, c_ready, n)
                nc.scalar.copy(wsum_hi[:], wsum[:].rearrange("p j s -> p (j s)")).then_inc(wsum_hi_ready, 1)

            def head(hp, r, first=False, second=False, final=False):
                h = 2 * hp + r
                nhp, nr = (hp, 1) if r == 0 else (hp + 1, 0)
                step(8 * h, 0, not first, True)
                if not final:
                    at_least(act, y_ready, 16 * h)
                    copy_head_values(nc, act, g, nhp, nr)
                    split_head_weights_hi(nc, act, g, nhp, nr)
                run_inner_pairs(act, lambda n, p: step(n, p, True, True), h)
                if not final:
                    split_head_values_hi(nc, act, g, nhp, nr)
                step(8 * h + 7, PAIRS - 1, True, not final)

            split_hi(0)
            run_heads(act, head)
            copy_column_sums(STEPS - 1)

        @block.vector
        def _(dve):
            def split_k_lo(n):
                dve.wait_ge(qk_hi_ready, 2 * n + 2)
                nc.vector.tensor_tensor(k_lo[:], ps_k[:], k_hi[:].bitcast(F32), ALU.subtract).then_inc(k_lo_ready, 1)

            def maxima(n):
                for j in range(2):
                    dve.wait_ge(scores_ready, 2 * n + j + 1)
                    nc.vector.tensor_reduce(negmax[:, 2 * j:2 * j + 2], ps_s[j][:].rearrange("p (q s) -> p q s", q=2),
                                            AX.X, ALU.max, negate=True).then_inc(negmax_ready, 1)

            def weigh_rows(n):
                dve.wait_ge(probs_ready, 4 * n + 4)
                nc.vector.reciprocal(rinv[:], rowsum[:]).then_inc(rinv_ready, 1)
                dve.wait_ge(rinv_ready, n + 1)
                for j in range(2):
                    nc.vector.tensor_scalar(half[:, j, :], probs[:, j, 0, :], rinv[:, 2 * j:2 * j + 1], None, ALU.mult).then_inc(half_ready, 1)
                at_least(dve, wsum_lo_ready, n)
                for j in range(2):
                    dve.wait_ge(half_ready, 2 * n + j + 1)
                    nc.vector.scalar_tensor_tensor(wsum[:, j, :], probs[:, j, 1, :], rinv[:, 2 * j + 1:2 * j + 2], half[:, j, :],
                                                   ALU.mult, ALU.add).then_inc(wsum_ready, 1)

            def products(n, to_acc=None):
                dve.wait_ge(c_copied, n + 1)
                if to_acc is None:
                    at_least(dve, acc_added, 2 * (n - PAIRS))
                for o in range(KT):
                    out = prod[:, o, :] if to_acc is None else g.accT[:, o, bass.ds(to_acc * PT, PT)]
                    nc.vector.tensor_tensor(out, ps_y[o][:], colsum[:], ALU.mult).then_inc(prod_ready, 1)

            def step(n, before, follow, to_acc=None):
                maxima(n)
                if before:
                    products(n - 1, to_acc)
                weigh_rows(n)
                if follow:
                    split_k_lo(n + 1)

            def head(hp, r, first=False, second=False, final=False):
                h = 2 * hp + r
                nhp, nr = (hp, 1) if r == 0 else (hp + 1, 0)
                step(8 * h, not first, True, PAIRS - 1 if second else None)
                run_inner_pairs(dve, lambda n, p: step(n, True, True, p - 1 if first else None), h)
                step(8 * h + 7, True, not final, PAIRS - 2 if first else None)
                if not final:
                    split_head_values_lo(nc, dve, g, nhp, nr)

            split_k_lo(0)
            run_heads(dve, head)
            products(STEPS - 1)

        @block.gpsimd
        def _(pool):
            def split_q_lo(n):
                pool.wait_ge(q32_ready, n + 1)
                pool.wait_ge(qk_hi_ready, 2 * n + 1)
                nc.gpsimd.tensor_tensor(q_lo[:], q32[:], q_hi[:].bitcast(F32), ALU.subtract).then_inc(q_lo_ready, 1)

            def add_products(n, pair, o):
                pool.wait_ge(prod_ready, 2 * n + o + 1)
                cols = g.accT[:, o, bass.ds(pair * PT, PT)]
                nc.gpsimd.tensor_tensor(cols, cols, prod[:, o, :], ALU.add).then_inc(acc_added, 1)

            def step(n, before, pair_before, follow):
                if before:
                    add_products(n - 1, pair_before, 0)
                if follow:
                    split_q_lo(n + 1)
                pool.wait_ge(wsum_hi_ready, n + 1)
                nc.gpsimd.tensor_tensor(wsum_lo[:], wsum[:].rearrange("p j s -> p (j s)"), wsum_hi[:].bitcast(F32), ALU.subtract).then_inc(wsum_lo_ready, 1)
                if before:
                    add_products(n - 1, pair_before, 1)

            def head(hp, r, first=False, second=False, final=False):
                h = 2 * hp + r
                nhp, nr = (hp, 1) if r == 0 else (hp + 1, 0)
                at_least(pool, acc_added, 2 * (8 * h - 1 - PAIRS))
                step(8 * h, not first and not second, PAIRS - 1, True)
                if not final:
                    split_head_weights_lo(nc, pool, g, nhp, nr)
                run_inner_pairs(pool, lambda n, p: step(n, not first, p - 1, True), h)
                step(8 * h + 7, not first, PAIRS - 2, not final)

            split_q_lo(0)
            run_heads(pool, head)
            for o in range(KT):
                add_products(STEPS - 1, PAIRS - 1, o)
            pool.wait_ge(acc_added, 2 * (STEPS - PAIRS))


class Shared:
    pass


def shared_memory(nc, m):
    g = Shared()
    g.ident = m.sb("ident", [P, P])
    g.ident_bf16 = m.sb("ident_bf16", [P, P], BF16)
    g.ones = m.sb("ones", [P, P])
    g.ones_r = m.sb("ones_r", [P, P], F32R)
    g.minus_half = m.sb("minus_half", [P, 4])
    g.first_rank = m.sb("first_rank", [P, 2, EXPERTS])
    g.modT = m.sb("modT", [P, 6, KT, B])
    g.ident_ready, g.ones_ready, g.ones_r_ready = m.sem("ident_ready"), m.sem("ones_ready"), m.sem("ones_r_ready")
    g.consts_ready, g.rank_ready = m.sem("consts_ready"), m.sem("rank_ready")
    g.ffn_raw_loaded = m.sem("ffn_raw_loaded")
    g.acc_stored = m.sem("acc_stored")
    g.raw_wg = m.sb("raw_wg", [EXPERTS, D])
    g.arena_offset = nc.sbuf_base
    g.arena = m.sb("arena", [P, ARENA])
    return g


def head_memory(nc, m, g):
    g.h_hi, g.h_lo = m.sb("h_hi", [P, KT, TOK], F32R), m.sb("h_lo", [P, KT, TOK], F32R)
    g.raw_qkv = m.sb("raw_qkv", [P, 2, KT, 3, DH])
    g.raw_o = m.sb("raw_o", [P, 2, D])
    g.wvT = m.sb("wvT", [P, D])
    g.wqk_hi = [m.sb(f"wqk_hi{r}", [P, KT, 2, DH], F32R) for r in range(2)]
    g.wqk_lo = [m.sb(f"wqk_lo{r}", [P, KT, 2, DH], F32R) for r in range(2)]
    g.m_hi = [m.sb(f"m_hi{r}", [P, KT, D], F32R) for r in range(2)]
    g.m_lo = [m.sb(f"m_lo{r}", [P, KT, D], F32R) for r in range(2)]
    g.accT = m.sb("accT", [P, KT, TOK])
    g.ps_head = m.ps("ps_head")
    g.raw_loaded = [m.sem("raw_loaded0"), m.sem("raw_loaded1")]
    g.wvT_ready, g.wvT_copied = m.sem("wvT_ready"), m.sem("wvT_copied")
    g.wqk_hi_ready, g.wqk_lo_ready = m.sem("wqk_hi_ready"), m.sem("wqk_lo_ready")
    g.m_ready, g.m_hi_ready, g.m_lo_ready = m.sem("m_ready"), m.sem("m_hi_ready"), m.sem("m_lo_ready")


def ffn_memory(nc, m, g):
    shapes = dict(A1=(KT, ER), A3=(KT, ER), W1=(KT, FF), W3=(KT, FF), B1=(ET, FF), B3=(ET, FF), W2=(FT, D), A2=(FT, ER), B2=(ET, D))
    g.wgT = m.sb("wgT", [P, KT, EXPERTS])
    g.w_hi = {name: m.sb(f"{name}T_hi", [P, *shape], F32R) for name, shape in shapes.items()}
    g.w_lo = {name: m.sb(f"{name}T_lo", [P, *shape], F32R) for name, shape in shapes.items()}




ARENA = 12288


class Arena:

    def __init__(self, nc, base, size):
        self.nc, self.at, self.end = nc, base, base + size

    def sb(self, name, shape, dt=F32):
        size = math.prod(shape[1:]) * (2 if dt == BF16 else 4)
        assert self.at + size <= self.end, name
        t = self.nc.alloc_sbuf_tensor_at(name, shape, dt, offset=self.at)
        self.at += size
        return t


RAW_SHAPES = dict(A1=(ET, D), A3=(ET, D), W1=(FT, D), W3=(FT, D), B1=(FT, ER), B3=(FT, ER),
                  W2=(KT, FF), A2=(ET, FF), B2=(KT, ER))


def raw_weights(g):
    at, views = 0, {}
    for name, (tiles, n) in RAW_SHAPES.items():
        views[name] = g.arena[:, at:at + tiles * n].rearrange("p (t n) -> p t n", t=tiles)
        at += tiles * n
    assert at <= ARENA
    return views


def load_ffn_weights(nc, sp, dram, g):
    raw = raw_weights(g)
    for name in ("W1", "W3", "W2"):
        sp.dma_start(raw[name], dram[name].rearrange("(t p) n -> p t n", p=P)).then_inc(g.ffn_raw_loaded, 16)
    for name in ("A1", "A3", "A2"):
        sp.dma_start(raw[name], dram[name].rearrange("e r n -> (e r) n").rearrange("(t p) n -> p t n", p=P)).then_inc(g.ffn_raw_loaded, 16)
    for name, tiles in (("B1", FT), ("B3", FT), ("B2", KT)):
        src = dram[name].rearrange("e (t p) r -> t p e r", p=P)
        for t in range(tiles):
            sp.dma_start(raw[name][:, t].rearrange("p (e r) -> p e r", e=EXPERTS), src[t]).then_inc(g.ffn_raw_loaded, 16)
    sp.dma_start(g.raw_wg[:], dram["Wg"]).then_inc(g.ffn_raw_loaded, 16)


FFN_LOADS = 16 * (6 + 2 * FT + KT + 1)


def weight_groups(g):
    raw, groups = raw_weights(g), []
    for name in RAW_SHAPES:
        tiles, n = RAW_SHAPES[name]
        blocks = [(outer, inner) for outer in range(n // P) for inner in range(tiles)]
        for at in range(0, len(blocks), 4):
            groups.append((name, at * P, blocks[at:at + 4]))
    return raw, groups


ROUTE = 17


def ffn_phase(nc, dram, g):
    with ExitStack() as ctx:
        m = Memory(nc, ctx)
        assert FT % 2 == 1, "tiles alternate over batches"
        arena = Arena(nc, g.arena_offset, 4 * ARENA)
        sb = arena.sb
        def slot(r):
            return sb(f"x_in2_{r}", [P, 2, D]), sb(f"acc_in{r}", [P, KT, S]), sb(f"x2_{r}", [P, 2, D])

        slots = [slot(0)]
        gated = sb("gated", [P, KT, S])
        xn = gated[:]
        h32 = sb("h32_2", [P, KT, S])
        chosen = sb("chosen_by_rank", [P, 2, 2, ER], BF16)
        maskT, weightT = [], []
        for r in range(2):
            maskT.append([sb(f"maskT{r}{k}", [P, ET, S], BF16) for k in range(2)])
            weightT.append(sb(f"weightT{r}", [P, 2, S]))
        slots.append(slot(1))
        x_in, acc_in, x2 = zip(*slots)
        mask_step = sb("mask_step", [P, ET, S], BF16)
        a_masked = [sb(f"a_masked{i}", [P, ET, S]) for i in range(2)]
        silu = [sb(f"silu{k}", [P, S]) for k in range(2)]
        glu = [sb(f"glu{k}", [P, S]) for k in range(2)]
        first_w = [sb(f"first_weighted{i}", [P, S]) for i in range(2)]
        second_w = sb("second_weighted", [P, S])
        both_w = sb("both_weighted", [P, S])
        a2_part = [sb(f"a2_part{k}", [P, ET, S]) for k in range(2)]
        out_gated = sb("out_gated", [P, KT, S])
        y_out = m.sb("y_out", [P, 2, D])
        stats, meanvar = m.sb("ln2_stats", [P, 2, 6]), m.sb("ln2_meanvar", [P, 2, 2])
        vareps, rstd = m.sb("ln2_vareps", [P, 2]), m.sb("ln2_rstd", [P, 2])
        logits, rest = m.sb("logits", [P, 2, EXPERTS]), m.sb("logits_rest", [P, 2, EXPERTS])
        equal = [m.sb(f"equal{k}", [P, 2, EXPERTS]) for k in range(2)]
        ranked = [m.sb(f"ranked{k}", [P, 2, EXPERTS]) for k in range(2)]
        onehot = [m.sb(f"onehot{k}", [P, 2, EXPERTS]) for k in range(2)]
        top = [m.sb(f"top{k}", [P, 2]) for k in range(2)]
        best = [m.sb(f"best_rank{k}", [P, 2]) for k in range(2)]
        gap, tanh_gap, weight = m.sb("gap", [P, 2]), m.sb("tanh_gap", [P, 2]), m.sb("weight", [P, 2, 2])
        h_hi = [m.sb(f"h2_hi{r}", [P, KT, S], F32R) for r in range(2)]
        h_lo = [m.sb(f"h2_lo{r}", [P, KT, S], F32R) for r in range(2)]
        a_hi = [[[m.sb(f"a_hi{r}{w}{k}", [P, ET, S], F32R) for k in range(2)] for w in range(2)] for r in range(2)]
        a_lo = [[[m.sb(f"a_lo{r}{w}{k}", [P, ET, S], F32R) for k in range(2)] for w in range(2)] for r in range(2)]
        v_hi = [[m.sb(f"v_hi{k}{i}", [P, S], F32R) for i in range(2)] for k in range(3)]
        v_lo = [[m.sb(f"v_lo{k}{i}", [P, S], F32R) for i in range(2)] for k in range(3)]
        a2_hi, a2_lo = m.sb("a2_hi", [P, ET, S], F32R), m.sb("a2_lo", [P, ET, S], F32R)

        ps_x1 = [m.ps(f"ps_x1_{i}") for i in range(2)]
        ps_x3 = [m.ps(f"ps_x3_{i}") for i in range(2)]
        ps_out = m.ps("ps_out")
        ps_a2 = [m.ps(f"ps_a2_{k}") for k in range(2)]
        ps_p = m.ps("ps_prep")
        ps_mask = ps_p[:].bitcast(BF16)[:, 0:ET * S]
        weight_banks, ps_wg = (*ps_x1, *ps_x3), ps_out
        raw, groups = weight_groups(g)

        w_transposed = m.sem("w_transposed")
        w_hi_ready, w_lo_ready = m.sem("w_hi_ready"), m.sem("w_lo_ready")
        wg_ready, wg_copied = m.sem("wg_ready"), m.sem("wg_copied")
        inputs_loaded = [m.sem("inputs_loaded0"), m.sem("inputs_loaded1")]
        gated_ready = m.sem("gated_ready")
        gatedT_ready = m.sem("gatedT_ready")
        x2_ready = m.sem("x2_ready")
        stats_ready, moments, ve_ready = m.sem("stats2_ready"), m.sem("moments2"), m.sem("ve2_ready")
        rstd_ready = m.sem("rstd2_ready")
        xn_ready = m.sem("xn2_ready")
        xnT_ready = m.sem("xn2T_ready")
        h32_ready = m.sem("h2_ready")
        h_hi_ready, h_lo_ready = m.sem("h2_hi_ready"), m.sem("h2_lo_ready")
        logits_ready = m.sem("logits_ready")
        route = m.sem("route")
        tanh_ready = m.sem("tanh_ready")
        mask_ready, maskT_ready = m.sem("mask_transposed"), m.sem("maskT_ready")
        mask_step_ready = m.sem("mask_step_ready")
        weight_ready, weightT_ready = m.sem("weight_transposed"), m.sem("weightT_ready")
        a_ready = m.sem("a_ready")
        masked_ready = m.sem("masked_ready")
        a_hi_ready, a_lo_ready = m.sem("a_hi_ready"), m.sem("a_lo_ready")
        up_ready = [m.sem("up_first_ready"), m.sem("up_second_ready")]
        silu_ready = [m.sem("silu_first_ready"), m.sem("silu_second_ready")]
        glu_ready = [m.sem("glu_first_ready"), m.sem("glu_second_ready")]
        weighted = [m.sem("weighted_first"), m.sem("weighted_second"), m.sem("weighted_both")]
        v_hi_ready = [m.sem(f"v_hi_ready{k}") for k in range(3)]
        v_lo_ready = [m.sem(f"v_lo_ready{k}") for k in range(3)]
        down_ready = m.sem("down_ready")
        a2_step = m.sem("a2_step")
        a2_hi_ready, a2_lo_ready = m.sem("a2_hi_ready"), m.sem("a2_lo_ready")
        out_ready = m.sem("out_ready")
        out_gated_ready = m.sem("out_gated_ready")
        outT_ready = m.sem("outT_ready")
        y_ready = m.sem("y_ready2")
        x2_kept = m.sem("x2_kept")
        stored = m.sem("stored")

        xg = dram["x"].rearrange("b (t p) c -> b p t c", p=P)
        og = dram["out"].rearrange("b (t p) c -> b p t c", p=P)
        accg = dram["acc"].rearrange("p k (b s) -> b p k s", s=S)

        def groups_of(*names):
            return sum(name in names for name, at, blocks in groups)

        def weight_columns(w, group):
            name, at, blocks = group
            return w[name][:].rearrange("p a b -> p (a b)")[:, at:at + len(blocks) * P]

        block = ctx.enter_context(nc.Block())

        @block.sync
        def _(sp):
            def load(b, r):
                sp.dma_start(x_in[r][:], xg[b]).then_inc(inputs_loaded[r], 16)
                sp.dma_start(acc_in[r][:], accg[b]).then_inc(inputs_loaded[r], 16)

            def iteration(b, r, more):
                if more:
                    sp.wait_ge(x2_ready, b + 1)
                    load(b + 2, r)
                sp.wait_ge(y_ready, b + 1)
                sp.dma_start(og[b], y_out[:]).then_inc(stored, 16)

            sp.wait_ge(g.acc_stored, 16 * PAIRS)
            sp.wait_ge(w_transposed, groups_of("A1", "A3"))
            load(0, 0)
            sp.wait_ge(w_transposed, len(groups))
            load(1, 1)
            with sp.Fori(0, B // 2 - 1) as i:
                for r in range(2):
                    iteration(2 * i + r, r, True)
            for r in range(2):
                iteration(B - 2 + r, r, False)
            sp.wait_ge(stored, 16 * B)

        def all_batches(eng, iteration):
            iteration(0, 0, False, True)
            iteration(1, 1, True, True)
            with eng.Fori(1, B // 2 - 1) as i:
                iteration(2 * i, 0, True, True)
                iteration(2 * i + 1, 1, True, True)
            iteration(B - 2, 0, True, True)
            iteration(B - 1, 1, True, False)

        @block.tensor
        def _(pe):
            def transpose_gated(q, r):
                pe.wait_ge(gated_ready, 2 * q + 2)
                at_least(pe, masked_ready, 4 * q)
                for t in range(2):
                    for k in range(KT):
                        last = nc.tensor.transpose(ps_p[:, t * D + k * P:t * D + (k + 1) * P], gated[:, k, t * P:(t + 1) * P], g.ident[:])
                last.then_inc(gatedT_ready, 1)

            def transpose_normalised(q, r):
                pe.wait_ge(xn_ready, 2 * q + 2)
                for k in range(KT):
                    for t in range(2):
                        last = nc.tensor.transpose(ps_p[:, k * S + t * P:k * S + (t + 1) * P], xn[:, t, k * P:(k + 1) * P], g.ident[:])
                last.then_inc(xnT_ready, 1)

            def router(q):
                pe.wait_ge(h32_ready, 2 * q + 2)
                for t in range(2):
                    for k in range(KT):
                        last = nc.tensor.matmul(ps_p[:, t * EXPERTS:(t + 1) * EXPERTS], h32[:, k, t * P:(t + 1) * P], g.wgT[:, k, :],
                                                start=(k == 0), stop=(k == KT - 1))
                last.then_inc(logits_ready, 1)

            def transpose_masks(q, choice):
                pe.wait_ge(route, ROUTE * q + ROUTE)
                at_least(pe, y_ready, q - 1)
                if choice == 1:
                    pe.wait_ge(maskT_ready, 2 * q + 1)
                for e in range(ET):
                    for t in range(2):
                        last = nc.tensor.transpose(ps_mask[:, e * S + t * P:e * S + (t + 1) * P], chosen[:, t, choice, e * P:(e + 1) * P], g.ident_bf16[:])
                last.then_inc(mask_ready, 1)

            def transpose_weights(q):
                pe.wait_ge(maskT_ready, 2 * q + 2)
                for k in range(2):
                    for t in range(2):
                        last = nc.tensor.transpose(ps_p[:, k * S + t * P:k * S + (t + 1) * P], weight[:, t, k:k + 1].broadcast_to([P, P]), g.ident[:])
                last.then_inc(weight_ready, 1)

            def lora_a(q, r, w):
                if w == 0:
                    pe.wait_ge(weightT_ready, q + 1)
                    pe.wait_ge(h_hi_ready, q + 1)
                    pe.wait_ge(h_lo_ready, q + 1)
                else:
                    pe.wait_ge(masked_ready, 4 * q + 2)
                hi, lo = g.w_hi[("A1", "A3")[w]], g.w_lo[("A1", "A3")[w]]
                for e in range(ET):
                    for k in range(KT):
                        cols = slice(e * P, (e + 1) * P)
                        last = three_pass(nc, ps_p[:, e * S:(e + 1) * S], hi[:, k, cols], lo[:, k, cols], h_hi[r][:, k, :], h_lo[r][:, k, :], k == 0, k == KT - 1)
                last.then_inc(a_ready, 1)

            def up_first(b, r, f):
                at_least(pe, glu_ready[1], FT * b + f - 1)
                if f == 0:
                    pe.wait_ge(h_hi_ready, b + 1)
                    pe.wait_ge(h_lo_ready, b + 1)
                cols = slice(f * P, (f + 1) * P)
                for w, ps in enumerate((ps_x1[(f + r) % 2], ps_x3[(f + r) % 2])):
                    base, lora = ("W1", "W3")[w], ("B1", "B3")[w]
                    for k in range(KT):
                        three_pass(nc, ps[:, 0:S], g.w_hi[base][:, k, cols], g.w_lo[base][:, k, cols], h_hi[r][:, k, :], h_lo[r][:, k, :],
                                   k == 0, False, skip_group_check=True)
                    if f == 0:
                        pe.wait_ge(a_hi_ready, 4 * b + 2 * w + 1)
                        pe.wait_ge(a_lo_ready, 4 * b + 2 * w + 1)
                    for e in range(ET):
                        last = three_pass(nc, ps[:, 0:S], g.w_hi[lora][:, e, cols], g.w_lo[lora][:, e, cols], a_hi[r][w][0][:, e, :], a_lo[r][w][0][:, e, :],
                                          False, e == ET - 1, skip_group_check=True)
                    last.then_inc(up_ready[0], 1)

            def up_second(b, r, f):
                pe.wait_ge(glu_ready[0], FT * b + f + 1)
                if f == 0:
                    pe.wait_ge(a_hi_ready, 4 * b + 4)
                    pe.wait_ge(a_lo_ready, 4 * b + 4)
                cols = slice(f * P, (f + 1) * P)
                for w, ps in enumerate((ps_x1[(f + r) % 2], ps_x3[(f + r) % 2])):
                    lora = ("B1", "B3")[w]
                    for e in range(ET):
                        last = three_pass(nc, ps[:, 0:S], g.w_hi[lora][:, e, cols], g.w_lo[lora][:, e, cols], a_hi[r][w][1][:, e, :], a_lo[r][w][1][:, e, :],
                                          False, e == ET - 1, skip_group_check=True)
                    last.then_inc(up_ready[1], 1)

            def down(b, r, f):
                if f == 0:
                    at_least(pe, out_gated_ready, 2 * b)
                    at_least(pe, a2_step, 3 * b)
                i = (f + r) % 2
                for k in range(2):
                    pe.wait_ge(v_hi_ready[k], FT * b + f + 1)
                    pe.wait_ge(v_lo_ready[k], FT * b + f + 1)
                    for e in range(ET):
                        cols = slice(e * P, (e + 1) * P)
                        three_pass(nc, ps_a2[k][:, e * S:(e + 1) * S], g.w_hi["A2"][:, f, cols], g.w_lo["A2"][:, f, cols], v_hi[k][i][:], v_lo[k][i][:],
                                   f == 0 and e == 0, f == FT - 1, skip_group_check=True)
                pe.wait_ge(v_hi_ready[2], FT * b + f + 1)
                pe.wait_ge(v_lo_ready[2], FT * b + f + 1)
                for o in range(KT):
                    cols = slice(o * P, (o + 1) * P)
                    last = three_pass(nc, ps_out[:, o * S:(o + 1) * S], g.w_hi["W2"][:, f, cols], g.w_lo["W2"][:, f, cols], v_hi[2][i][:], v_lo[2][i][:],
                                      f == 0 and o == 0, False, skip_group_check=True)
                last.then_inc(down_ready, 1)

            def lora_down(b):
                pe.wait_ge(a2_hi_ready, b + 1)
                pe.wait_ge(a2_lo_ready, b + 1)
                for o in range(KT):
                    cols = slice(o * P, (o + 1) * P)
                    for e in range(ET):
                        last = three_pass(nc, ps_out[:, o * S:(o + 1) * S], g.w_hi["B2"][:, e, cols], g.w_lo["B2"][:, e, cols], a2_hi[:, e, :], a2_lo[:, e, :],
                                          False, e == ET - 1, skip_group_check=True)
                last.then_inc(out_ready, 1)

            def transpose_out(b, after):
                if after:
                    pe.wait_ge(route, ROUTE * (b + 2) + 1)
                pe.wait_ge(out_gated_ready, 2 * b + 2)
                at_least(pe, y_ready, b)
                for t in range(2):
                    for k in range(KT):
                        last = nc.tensor.transpose(ps_p[:, t * D + k * P:t * D + (k + 1) * P], out_gated[:, k, t * P:(t + 1) * P], g.ident[:])
                last.then_inc(outT_ready, 1)

            def iteration(b, r, before, after):
                q, s = b + 1, 1 - r
                up_first(b, r, 0)
                if before:
                    down(b - 1, s, FT - 1)
                if after:
                    transpose_gated(q, s)
                up_first(b, r, 1)
                up_second(b, r, 0)
                if before:
                    lora_down(b - 1)
                up_first(b, r, 2)
                if after:
                    transpose_normalised(q, s)
                up_second(b, r, 1)
                down(b, r, 0)
                if after:
                    router(q)
                up_first(b, r, 3)
                if before:
                    transpose_out(b - 1, after)
                up_second(b, r, 2)
                down(b, r, 1)
                if after:
                    transpose_masks(q, 0)
                up_first(b, r, 4)
                if after:
                    transpose_masks(q, 1)
                up_second(b, r, 3)
                if after:
                    transpose_weights(q)
                down(b, r, 2)
                if after:
                    lora_a(q, s, 0)
                up_first(b, r, 5)
                up_second(b, r, 4)
                down(b, r, 3)
                if after:
                    lora_a(q, s, 1)
                up_first(b, r, 6)
                up_second(b, r, 5)
                down(b, r, 4)
                up_second(b, r, 6)
                down(b, r, 5)

            def transpose_groups(start, end):
                for n in range(start, end):
                    name, at, blocks = groups[n]
                    at_least(pe, w_lo_ready, n - 3)
                    for i, (outer, inner) in enumerate(blocks):
                        last = nc.tensor.transpose(weight_banks[n % 4][:, i * P:(i + 1) * P], raw[name][:, inner, outer * P:(outer + 1) * P], g.ident[:])
                    last.then_inc(w_transposed, 1)

            pe.wait_ge(g.ffn_raw_loaded, FFN_LOADS)
            for k in range(KT):
                last = nc.tensor.transpose(ps_wg[:, k * EXPERTS:(k + 1) * EXPERTS], g.raw_wg[:, k * P:(k + 1) * P], g.ident[0:EXPERTS, 0:EXPERTS])
            last.then_inc(wg_ready, 1)
            transpose_groups(0, 11)
            transpose_gated(0, 0)
            transpose_groups(11, 16)
            transpose_normalised(0, 0)
            transpose_groups(16, 19)
            pe.wait_ge(wg_copied, 1)
            router(0)
            transpose_groups(19, 23)
            transpose_masks(0, 0)
            transpose_groups(23, 24)
            transpose_masks(0, 1)
            transpose_groups(24, 25)
            transpose_weights(0)
            transpose_groups(25, 26)
            lora_a(0, 0, 0)
            transpose_groups(26, len(groups))
            pe.wait_ge(w_lo_ready, len(groups))
            lora_a(0, 0, 1)
            all_batches(pe, iteration)
            down(B - 1, 1, FT - 1)
            lora_down(B - 1)
            transpose_out(B - 1, False)

        @block.scalar
        def _(act):
            def modulate(q, r):
                act.wait_ge(xnT_ready, q + 1)
                for k in range(KT):
                    nc.scalar.activation(h32[:, k, :], ps_p[:, k * S:(k + 1) * S], ACT.Identity,
                                         scale=g.modT[:, CB, k, bass.ds(q, 1)], bias=g.modT[:, SB_, k, bass.ds(q, 1)]).then_inc(h32_ready, 1)
                act.wait_ge(h32_ready, 2 * q + 2)
                nc.scalar.copy(h_hi[r][:], h32[:]).then_inc(h_hi_ready, 1)

            def tanh_of_gap(q):
                act.wait_ge(route, ROUTE * q + 13)
                nc.scalar.activation(tanh_gap[:], gap[:], ACT.Tanh, scale=0.5).then_inc(tanh_ready, 1)

            def copy_mask(q, r, choice):
                act.wait_ge(mask_ready, 2 * q + choice + 1)
                nc.scalar.copy(maskT[r][choice][:].rearrange("p e s -> p (e s)"), ps_mask).then_inc(maskT_ready, 1)

            def copy_weights(q, r):
                act.wait_ge(weight_ready, q + 1)
                nc.scalar.copy(weightT[r][:].rearrange("p k s -> p (k s)"), ps_p[:]).then_inc(weightT_ready, 1)

            def split_a_hi(q, r, w):
                for k in range(2):
                    act.wait_ge(masked_ready, 4 * q + 2 * w + k + 1)
                    nc.scalar.copy(a_hi[r][w][k][:], a_masked[k][:]).then_inc(a_hi_ready, 1)

            def silu_of(b, r, f, k):
                act.wait_ge(up_ready[k], 2 * FT * b + 2 * f + 1)
                at_least(act, glu_ready[k], FT * b + f)
                nc.scalar.activation(silu[k][:], ps_x1[(f + r) % 2][:, 0:S], ACT.Silu).then_inc(silu_ready[k], 1)

            def split_v_hi(b, r, f, k):
                src = (first_w[(f + r) % 2], second_w, both_w)[k]
                act.wait_ge(weighted[k], FT * b + f + 1)
                at_least(act, down_ready, FT * b + f - 1)
                nc.scalar.copy(v_hi[k][(f + r) % 2][:], src[:]).then_inc(v_hi_ready[k], 1)

            def split_a2_hi(b):
                act.wait_ge(a2_step, 3 * b + 3)
                nc.scalar.copy(a2_hi[:], a2_part[0][:]).then_inc(a2_hi_ready, 1)

            def gate_out(b):
                act.wait_ge(out_ready, b + 1)
                for k in range(KT):
                    nc.scalar.activation(out_gated[:, k, :], ps_out[:, k * S:(k + 1) * S], ACT.Identity,
                                         scale=g.modT[:, GB, k, bass.ds(b, 1)]).then_inc(out_gated_ready, 1)

            def keep_x2(b, r):
                act.wait_ge(x2_ready, b + 1)
                at_least(act, stored, 16 * b)
                nc.scalar.copy(y_out[:], x2[r][:]).then_inc(x2_kept, 1)

            def finish_tiles(b, r):
                split_v_hi(b, r, FT - 1, 1)
                split_v_hi(b, r, FT - 1, 2)

            def iteration(b, r, before, after):
                q, s = b + 1, 1 - r
                if before:
                    finish_tiles(b - 1, s)
                    keep_x2(b - 1, s)
                silu_of(b, r, 0, 0)
                if before:
                    split_a2_hi(b - 1)
                silu_of(b, r, 1, 0)
                split_v_hi(b, r, 0, 0)
                silu_of(b, r, 0, 1)
                if before:
                    gate_out(b - 1)
                for f in range(2, FT):
                    split_v_hi(b, r, f - 2, 1)
                    split_v_hi(b, r, f - 2, 2)
                    if after and f == 4:
                        copy_mask(q, s, 0)
                    silu_of(b, r, f, 0)
                    if after and f == 2:
                        modulate(q, s)
                    if after and f == 3:
                        tanh_of_gap(q)
                    if after and f == 4:
                        copy_mask(q, s, 1)
                    split_v_hi(b, r, f - 1, 0)
                    silu_of(b, r, f - 1, 1)
                    if after and f == 4:
                        copy_weights(q, s)
                    if after and f >= 5:
                        split_a_hi(q, s, f - 5)
                split_v_hi(b, r, 5, 1)
                split_v_hi(b, r, 5, 2)
                split_v_hi(b, r, 6, 0)
                silu_of(b, r, 6, 1)

            def split_groups_hi(start, end):
                for n in range(start, end):
                    act.wait_ge(w_transposed, n + 1)
                    columns = weight_columns(g.w_hi, groups[n])
                    nc.scalar.copy(columns, weight_banks[n % 4][:, 0:columns.shape[-1]]).then_inc(w_hi_ready, 1)

            act.wait_ge(wg_ready, 1)
            nc.scalar.copy(g.wgT[:].rearrange("p k e -> p (k e)"), ps_wg[:, 0:KT * EXPERTS]).then_inc(wg_copied, 1)
            split_groups_hi(0, 16)
            modulate(0, 0)
            split_groups_hi(16, 18)
            act.wait_ge(g.acc_stored, 16 * PAIRS)
            split_groups_hi(18, 22)
            tanh_of_gap(0)
            split_groups_hi(22, 23)
            copy_mask(0, 0, 0)
            split_groups_hi(23, 24)
            copy_mask(0, 0, 1)
            split_groups_hi(24, 25)
            copy_weights(0, 0)
            split_groups_hi(25, len(groups))
            split_a_hi(0, 0, 0)
            split_a_hi(0, 0, 1)
            all_batches(act, iteration)
            finish_tiles(B - 1, 1)
            keep_x2(B - 1, 1)
            split_a2_hi(B - 1)
            gate_out(B - 1)

        @block.vector
        def _(dve):
            def gate_attention(q, r):
                dve.wait_ge(inputs_loaded[r], 16 * (q - r) + 32)
                at_least(dve, xnT_ready, q)
                for k in range(KT):
                    nc.vector.tensor_scalar(gated[:, k, :], acc_in[r][:, k, :], g.modT[:, GA, k, bass.ds(q, 1)], None, ALU.mult).then_inc(gated_ready, 1)

            def residual(q, r, before):
                if before:
                    dve.wait_ge(x2_kept, q - 1)
                dve.wait_ge(gatedT_ready, q + 1)
                nc.vector.tensor_tensor(x2[r][:].rearrange("p t c -> p (t c)"), ps_p[:], x_in[r][:].rearrange("p t c -> p (t c)"), ALU.add).then_inc(x2_ready, 1)

            def statistics(q, r):
                dve.wait_ge(x2_ready, q + 1)
                for t in range(2):
                    nc.vector.bn_stats(stats[:, t, :], x2[r][:, t, :]).then_inc(stats_ready, 1)
                dve.wait_ge(stats_ready, 2 * q + 2)
                combine_stats(nc, dve, stats, meanvar, vareps[:], moments, ve_ready, q)

            def normalise(q, r):
                dve.wait_ge(rstd_ready, q + 1)
                for t in range(2):
                    nc.vector.tensor_scalar(xn[:, t, :], x2[r][:, t, :], meanvar[:, t, 0:1], rstd[:, t:t + 1], ALU.subtract, ALU.mult).then_inc(xn_ready, 1)

            def split_h_lo(q, r):
                dve.wait_ge(h_hi_ready, q + 1)
                nc.vector.tensor_tensor(h_lo[r][:], h32[:], h_hi[r][:].bitcast(F32), ALU.subtract).then_inc(h_lo_ready, 1)

            def routing(q):
                done = ROUTE * q

                def over_experts(t):
                    return t[:].unsqueeze(2).broadcast_to([P, 2, EXPERTS])

                dve.wait_ge(logits_ready, q + 1)
                nc.vector.tensor_copy(logits[:].rearrange("p t e -> p (t e)"), ps_p[:, 0:2 * EXPERTS]).then_inc(route, 1)
                for k, src in enumerate((logits, rest)):
                    n = done + 1 + 6 * k
                    dve.wait_ge(route, n)
                    nc.vector.tensor_reduce(top[k][:], src[:], AX.X, ALU.max).then_inc(route, 1)
                    dve.wait_ge(route, n + 1)
                    nc.vector.tensor_tensor(equal[k][:], src[:], over_experts(top[k]), ALU.is_equal).then_inc(route, 1)
                    dve.wait_ge(route, n + 2)
                    nc.vector.tensor_tensor(ranked[k][:], equal[k][:], g.first_rank[:], ALU.mult).then_inc(route, 1)
                    dve.wait_ge(route, n + 3)
                    nc.vector.tensor_reduce(best[k][:], ranked[k][:], AX.X, ALU.max).then_inc(route, 1)
                    dve.wait_ge(route, n + 4)
                    nc.vector.tensor_tensor(onehot[k][:], ranked[k][:], over_experts(best[k]), ALU.is_equal).then_inc(route, 1)
                    if k == 0:
                        dve.wait_ge(route, n + 5)
                        nc.vector.scalar_tensor_tensor(rest[:], onehot[0][:], -3.0e38, logits[:], ALU.mult, ALU.add).then_inc(route, 1)
                nc.vector.tensor_tensor(gap[:], top[0][:], top[1][:], ALU.subtract).then_inc(route, 1)

            def choices(q):
                done = ROUTE * q
                dve.wait_ge(route, done + 13)
                at_least(dve, weight_ready, q)
                for k in range(2):
                    nc.vector.tensor_copy(chosen[:, :, k, :].rearrange("p t (e r) -> p t e r", e=EXPERTS),
                                          onehot[k][:].unsqueeze(3).broadcast_to([P, 2, EXPERTS, RANK])).then_inc(route, 1)
                dve.wait_ge(tanh_ready, q + 1)
                for k, sign in enumerate((0.5, -0.5)):
                    nc.vector.tensor_scalar(weight[:, :, k], tanh_gap[:], sign, 0.5, ALU.mult, ALU.add).then_inc(route, 1)

            def step_of_masks(q, r):
                dve.wait_ge(maskT_ready, 2 * q + 2)
                nc.vector.tensor_tensor(mask_step[:], maskT[r][1][:], maskT[r][0][:], ALU.subtract).then_inc(mask_step_ready, 1)

            def mask_a(q, r, w):
                dve.wait_ge(a_ready, 2 * q + w + 1)
                dve.wait_ge(mask_step_ready, q + 1)
                at_least(dve, a_lo_ready, 4 * q + 2 * w)
                for k, mask in enumerate((maskT[r][0], mask_step)):
                    nc.vector.tensor_tensor(a_masked[k][:], ps_p[:].rearrange("p (e s) -> p e s", e=ET), mask[:], ALU.mult).then_inc(masked_ready, 1)

            def glu_of(b, r, f, k):
                dve.wait_ge(silu_ready[k], FT * b + f + 1)
                dve.wait_ge(up_ready[k], 2 * FT * b + 2 * f + 2)
                at_least(dve, weighted[k], FT * b + f)
                nc.vector.tensor_tensor(glu[k][:], ps_x3[(f + r) % 2][:, 0:S], silu[k][:], ALU.mult).then_inc(glu_ready[k], 1)

            def split_v_lo(b, r, f, k):
                src = (first_w[(f + r) % 2], second_w, both_w)[k]
                dve.wait_ge(v_hi_ready[k], FT * b + f + 1)
                nc.vector.tensor_tensor(v_lo[k][(f + r) % 2][:], src[:], v_hi[k][(f + r) % 2][:].bitcast(F32), ALU.subtract).then_inc(v_lo_ready[k], 1)

            def mask_a2(b, r):
                dve.wait_ge(down_ready, FT * b + FT)
                for k in range(2):
                    nc.vector.tensor_tensor(a2_part[k][:], ps_a2[k][:].rearrange("p (e s) -> p e s", e=ET), maskT[r][k][:], ALU.mult).then_inc(a2_step, 1)
                dve.wait_ge(a2_step, 3 * b + 2)
                nc.vector.tensor_tensor(a2_part[0][:], a2_part[0][:], a2_part[1][:], ALU.add).then_inc(a2_step, 1)

            def split_a2_lo(b):
                dve.wait_ge(a2_hi_ready, b + 1)
                nc.vector.tensor_tensor(a2_lo[:], a2_part[0][:], a2_hi[:].bitcast(F32), ALU.subtract).then_inc(a2_lo_ready, 1)

            def output(b):
                dve.wait_ge(outT_ready, b + 1)
                dve.wait_ge(x2_kept, b + 1)
                nc.vector.tensor_tensor(y_out[:].rearrange("p t c -> p (t c)"), ps_p[:], y_out[:].rearrange("p t c -> p (t c)"), ALU.add).then_inc(y_ready, 1)

            def finish_tiles(b, r):
                split_v_lo(b, r, FT - 1, 1)
                split_v_lo(b, r, FT - 1, 2)

            def iteration(b, r, before, after):
                q, s = b + 1, 1 - r
                if before:
                    finish_tiles(b - 1, s)
                if after:
                    gate_attention(q, s)
                glu_of(b, r, 0, 0)
                if before:
                    mask_a2(b - 1, s)
                if after:
                    residual(q, s, before)
                if before:
                    split_a2_lo(b - 1)
                glu_of(b, r, 1, 0)
                split_v_lo(b, r, 0, 0)
                glu_of(b, r, 0, 1)
                if after:
                    statistics(q, s)
                    normalise(q, s)
                for f in range(2, FT):
                    split_v_lo(b, r, f - 2, 1)
                    split_v_lo(b, r, f - 2, 2)
                    if after and f == 3:
                        routing(q)
                    if after and f >= 5:
                        mask_a(q, s, f - 5)
                    glu_of(b, r, f, 0)
                    if before and f == 3:
                        output(b - 1)
                    if after and f == 3:
                        choices(q)
                    split_v_lo(b, r, f - 1, 0)
                    glu_of(b, r, f - 1, 1)
                    if after and f == 2:
                        split_h_lo(q, s)
                    if after and f == 4:
                        step_of_masks(q, s)
                split_v_lo(b, r, 5, 1)
                split_v_lo(b, r, 5, 2)
                split_v_lo(b, r, 6, 0)
                glu_of(b, r, 6, 1)

            def split_groups_lo(start, end):
                for n in range(start, end):
                    dve.wait_ge(w_hi_ready, n + 1)
                    columns = weight_columns(g.w_lo, groups[n])
                    nc.vector.tensor_tensor(columns, weight_banks[n % 4][:, 0:columns.shape[-1]],
                                            weight_columns(g.w_hi, groups[n]).bitcast(F32), ALU.subtract).then_inc(w_lo_ready, 1)

            split_groups_lo(0, 7)
            gate_attention(0, 0)
            split_groups_lo(7, 9)
            residual(0, 0, False)
            statistics(0, 0)
            split_groups_lo(9, 12)
            normalise(0, 0)
            split_groups_lo(12, 15)
            split_h_lo(0, 0)
            split_groups_lo(15, 18)
            routing(0)
            split_groups_lo(18, 19)
            choices(0)
            split_groups_lo(19, 26)
            step_of_masks(0, 0)
            split_groups_lo(26, len(groups))
            mask_a(0, 0, 0)
            mask_a(0, 0, 1)
            all_batches(dve, iteration)
            finish_tiles(B - 1, 1)
            mask_a2(B - 1, 1)
            split_a2_lo(B - 1)
            output(B - 1)

        @block.gpsimd
        def _(pool):
            def inverse_deviation(q):
                pool.wait_ge(ve_ready, 4 * q + 4)
                nc.gpsimd.tensor_tensor(rstd[:], vareps[:], g.minus_half[:, 0:2], ALU.pow).then_inc(rstd_ready, 1)

            def split_a_lo(q, r, w):
                for k in range(2):
                    pool.wait_ge(a_hi_ready, 4 * q + 2 * w + k + 1)
                    nc.gpsimd.tensor_tensor(a_lo[r][w][k][:], a_masked[k][:], a_hi[r][w][k][:].bitcast(F32), ALU.subtract).then_inc(a_lo_ready, 1)

            def weigh(b, r, f, k):
                out = (first_w[(f + r) % 2], second_w)[k]
                pool.wait_ge(glu_ready[k], FT * b + f + 1)
                at_least(pool, v_lo_ready[k], FT * b + f - (1 if k == 0 else 0))
                at_least(pool, weighted[2], FT * b + f - (1 if k == 0 else 0))
                nc.gpsimd.tensor_tensor(out[:], glu[k][:], weightT[r][:, k, :], ALU.mult).then_inc(weighted[k], 1)

            def add_choices(b, r, f):
                pool.wait_ge(weighted[1], FT * b + f + 1)
                at_least(pool, v_lo_ready[2], FT * b + f)
                nc.gpsimd.tensor_tensor(both_w[:], first_w[(f + r) % 2][:], second_w[:], ALU.add).then_inc(weighted[2], 1)

            def iteration(b, r, before, after):
                q, s = b + 1, 1 - r
                weigh(b, r, 0, 0)
                for f in range(1, FT):
                    weigh(b, r, f, 0)
                    weigh(b, r, f - 1, 1)
                    add_choices(b, r, f - 1)
                    if after and f == 1:
                        inverse_deviation(q)
                    if after and f >= 5:
                        split_a_lo(q, s, f - 5)
                weigh(b, r, FT - 1, 1)
                add_choices(b, r, FT - 1)

            inverse_deviation(0)
            split_a_lo(0, 0, 0)
            split_a_lo(0, 0, 1)
            all_batches(pool, iteration)


def adaln_attention_mixture_kernel(nc, x, w_qkv, w_o, Wg, W1, W2, W3, A1, B1, A2, B2, A3, B3, c, wmod, out):
    dram = dict(x=x, w_qkv=w_qkv, w_o=w_o, Wg=Wg, W1=W1, W2=W2, W3=W3, A1=A1, B1=B1, A2=A2, B2=B2, A3=A3, B3=B3,
                c=c, wmod=wmod, out=out, acc=nc.dram_tensor("acc_dram", [P, KT, TOK], F32, kind="Internal").ap())
    with ExitStack() as ctx:
        m = Memory(nc, ctx)
        g = shared_memory(nc, m)
        with ExitStack() as heads:
            head_memory(nc, Memory(nc, heads), g)
            setup_phase(nc, dram, g)
            attention_phase(nc, dram, g)
        with ExitStack() as ffn:
            ffn_memory(nc, Memory(nc, ffn), g)
            ffn_phase(nc, dram, g)


_INS = ['L0_attn_x', 'L0_attn_w_qkv', 'L0_attn_w_o', 'L0_ffn_Wg', 'L0_ffn_W1', 'L0_ffn_W2', 'L0_ffn_W3', 'L0_ffn_A1', 'L0_ffn_B1',
        'L0_ffn_A2', 'L0_ffn_B2', 'L0_ffn_A3', 'L0_ffn_B3', 'L0_c', 'L0_wmod']
_OUTS = [((B, S, D), 'float32')]


def kernel(**inputs):
    import numpy as _np
    import concourse.bacc as _bacc
    from concourse import mybir as _mybir
    from concourse.bass_utils import run_bass_kernel_spmd as _run

    nc = _bacc.Bacc("TRN2", target_bir_lowering=False, num_devices=1)
    arrays, args = {}, []
    for name in _INS:
        a = _np.ascontiguousarray(inputs[name])
        arrays[f"in_{name}_dram"] = a
        args.append(nc.dram_tensor(f"in_{name}_dram", a.shape, _mybir.dt.from_np(a.dtype), kind="ExternalInput").ap())
    for i, (shape, dtype) in enumerate(_OUTS):
        dt = _mybir.dt.from_np(_np.dtype(dtype))
        args.append(nc.dram_tensor(f"out_{i}_dram", shape, dt, kind="ExternalOutput").ap())
    adaln_attention_mixture_kernel(nc, *args)
    r = _run(nc, [arrays], core_ids=[0])
    return r.results[0]["out_0_dram"]
```
